# Optimizing a Trainium2 kernel written in Bass

```python
import numpy as np
import jax
import jax.numpy as jnp

def _softmax(x, axis=-1):
    return jax.nn.softmax(x, axis=axis)

def _gelu(x):
    return jax.nn.gelu(x, approximate=True)

def _silu(x):
    return jax.nn.silu(x)

def _sigmoid(x):
    return jax.nn.sigmoid(x)

def _layernorm(x, axis=-1, eps=1e-05):
    m = jnp.mean(x, axis=axis, keepdims=True)
    v = jnp.var(x, axis=axis, keepdims=True)
    return (x - m) / jnp.sqrt(v + eps)

def _scatter_add(tgt, idx, src, axis=0):
    return tgt.at[idx].add(src)

def _segment_sum(src, seg, n):
    return jax.ops.segment_sum(src, seg, n)
kernel_name = 'mk_vit_tower_d1_tok_img768_r4_1944f4'

def setup_inputs(seed: int=0):
    np.random.seed(seed)
    _w = jnp.asarray

    def _rec_inputs():
        import jax
        import jax.numpy as jnp
        _rk = jax.random.key(seed)
        x = -0.00016672 + 0.999947 * jax.random.normal(jax.random.fold_in(_rk, 1), (32, 3, 96, 96), jnp.float32)
        return x
    x = _rec_inputs()

    def _L0_tok_setup():
        import jax, jax.numpy as jnp
        import numpy as np
        EPS = 1e-05

        def _layernorm(x, gamma, beta):
            mu = jnp.mean(x, axis=-1, keepdims=True)
            var = jnp.mean(jnp.square(x - mu), axis=-1, keepdims=True)
            return (x - mu) * jax.lax.rsqrt(var + EPS) * gamma + beta
        key = jax.random.key(seed)
        ks = jax.random.split(key, 4)
        B, C, H, W = (64, 3, 96, 96)
        P, D = (16, 192)
        patch_dim = P * P * C
        x = jax.random.normal(ks[0], (B, C, H, W), dtype=jnp.float32)
        ln1_g = jnp.ones((patch_dim,), jnp.float32)
        ln1_b = jnp.zeros((patch_dim,), jnp.float32)
        Wl = jax.random.normal(ks[1], (patch_dim, D), jnp.float32) / np.sqrt(patch_dim)
        bl = jax.random.normal(ks[2], (D,), jnp.float32) * 0.01
        ln2_g = jnp.ones((D,), jnp.float32)
        ln2_b = jnp.zeros((D,), jnp.float32)
        return {'x': x, 'ln1_g': ln1_g, 'ln1_b': ln1_b, 'Wl': Wl, 'bl': bl, 'ln2_g': ln2_g, 'ln2_b': ln2_b, 'patch_size': 16}
    _L0_tok_all = _L0_tok_setup()
    _L0_tok_in = {k: v for k, v in _L0_tok_all.items() if k in ('ln1_g', 'ln1_b', 'Wl', 'bl', 'ln2_g', 'ln2_b')}
    del _L0_tok_all

    def _L0_attn_setup():
        import jax, jax.numpy as jnp
        import numpy as np
        D_MODEL = 192
        N_HEADS = 12
        D_HEAD = D_MODEL // N_HEADS
        key = jax.random.key(seed)
        k_x, k_qkv_w, k_qkv_b, k_out_w, k_out_b = jax.random.split(key, 5)
        B, T = (2, 1024)
        s_in = 1.0 / np.sqrt(D_MODEL)
        return {'x': jax.random.normal(k_x, (B, T, D_MODEL), dtype=jnp.float32), 'W_qkv': jax.random.uniform(k_qkv_w, (D_MODEL, 3 * D_MODEL), jnp.float32, -s_in, s_in), 'b_qkv': jax.random.uniform(k_qkv_b, (3 * D_MODEL,), jnp.float32, -s_in, s_in), 'W_out': jax.random.uniform(k_out_w, (D_MODEL, D_MODEL), jnp.float32, -s_in, s_in), 'b_out': jax.random.uniform(k_out_b, (D_MODEL,), jnp.float32, -s_in, s_in)}
    _L0_attn_all = _L0_attn_setup()
    _L0_attn_in = {k: v for k, v in _L0_attn_all.items() if k in ('W_qkv', 'b_qkv', 'W_out', 'b_out')}
    del _L0_attn_all

    def _L0_ffn_setup():
        import jax, jax.numpy as jnp
        import numpy as np
        NUM_EXPERTS = 8
        TOP_K = 2
        CAPACITY_FACTOR = 1.25
        MAX_GROUP_SIZE = 1024
        MIN_EXPERT_CAPACITY = 4

        def _moe_forward(x, w_router, wi, wo):
            B, T, D = x.shape
            E = NUM_EXPERTS
            num_tokens = B * T
            G = max(num_tokens // MAX_GROUP_SIZE, E)
            while num_tokens % G != 0 or G % E != 0:
                G += 1
            S = num_tokens // G
            C = max(int(TOP_K * CAPACITY_FACTOR * S / E), MIN_EXPERT_CAPACITY)
            xg = x.reshape(G, S, D)
            logits = jnp.einsum('gsd,de->gse', xg.astype(jnp.float32), w_router.astype(jnp.float32))
            probs = jax.nn.softmax(logits, axis=-1)
            gate, idx = jax.lax.top_k(probs, TOP_K)
            idx_kf = jnp.swapaxes(idx, 1, 2).reshape(G, TOP_K * S)
            mask = jax.nn.one_hot(idx_kf, E, dtype=jnp.int32)
            prio = jnp.cumsum(mask, axis=1) * mask - 1
            prio = jnp.swapaxes(prio.reshape(G, TOP_K, S, E), 1, 2)
            prio_se = prio.max(axis=2)
            gate_se = jnp.einsum('gsk,gske->gse', gate, jax.nn.one_hot(idx, E, dtype=gate.dtype))
            dispatch = jax.nn.one_hot(prio_se, C, dtype=x.dtype)
            combine = dispatch * gate_se[..., None].astype(x.dtype)
            expert_in = jnp.einsum('gsec,gsd->egcd', dispatch, xg)
            h = jax.nn.relu(jnp.einsum('egcd,edf->egcf', expert_in, wi))
            expert_out = jnp.einsum('egcf,efd->egcd', h, wo)
            out = jnp.einsum('gsec,egcd->gsd', combine, expert_out)
            return out.reshape(B, T, D)
        key = jax.random.key(seed)
        k1, k2, k3, k4 = jax.random.split(key, 4)
        B, T, D, F = (8, 256, 192, 768)
        x = jax.random.normal(k1, (B, T, D), jnp.float32)
        w_router = jax.random.normal(k2, (D, NUM_EXPERTS), jnp.float32) * D ** (-0.5)
        wi = jax.random.normal(k3, (NUM_EXPERTS, D, F), jnp.float32) * D ** (-0.5)
        wo = jax.random.normal(k4, (NUM_EXPERTS, F, D), jnp.float32) * F ** (-0.5)
        return {'x': x, 'w_router': w_router, 'wi': wi, 'wo': wo}
    _L0_ffn_all = _L0_ffn_setup()
    _L0_ffn_in = {k: v for k, v in _L0_ffn_all.items() if k in ('w_router', 'wi', 'wo')}
    del _L0_ffn_all
    return {'x': x, 'L0_tok_ln1_g': _L0_tok_in['ln1_g'], 'L0_tok_ln1_b': _L0_tok_in['ln1_b'], 'L0_tok_Wl': _L0_tok_in['Wl'], 'L0_tok_bl': _L0_tok_in['bl'], 'L0_tok_ln2_g': _L0_tok_in['ln2_g'], 'L0_tok_ln2_b': _L0_tok_in['ln2_b'], 'L0_attn_W_qkv': _L0_attn_in['W_qkv'], 'L0_attn_b_qkv': _L0_attn_in['b_qkv'], 'L0_attn_W_out': _L0_attn_in['W_out'], 'L0_attn_b_out': _L0_attn_in['b_out'], 'L0_ffn_w_router': _L0_ffn_in['w_router'], 'L0_ffn_wi': _L0_ffn_in['wi'], 'L0_ffn_wo': _L0_ffn_in['wo']}

def reference(x, L0_tok_ln1_g, L0_tok_ln1_b, L0_tok_Wl, L0_tok_bl, L0_tok_ln2_g, L0_tok_ln2_b, L0_attn_W_qkv, L0_attn_b_qkv, L0_attn_W_out, L0_attn_b_out, L0_ffn_w_router, L0_ffn_wi, L0_ffn_wo):
    import jax
    import jax.numpy as jnp

    def _L0_tok_ref(x, ln1_g, ln1_b, Wl, bl, ln2_g, ln2_b, patch_size):
        import jax, jax.numpy as jnp
        import numpy as np
        EPS = 1e-05

        def _layernorm(x, gamma, beta):
            mu = jnp.mean(x, axis=-1, keepdims=True)
            var = jnp.mean(jnp.square(x - mu), axis=-1, keepdims=True)
            return (x - mu) * jax.lax.rsqrt(var + EPS) * gamma + beta
        p = patch_size
        b, c, h, w = x.shape
        n = h * w // (p * p)
        xhwc = jnp.transpose(x, (0, 2, 3, 1))
        patches = xhwc.reshape(b, h // p, p, w // p, p, c)
        patches = jnp.transpose(patches, (0, 1, 3, 2, 4, 5)).reshape(b, n, p * p * c)
        y = _layernorm(patches, ln1_g, ln1_b)
        y = jnp.einsum('bnd,de->bne', y, Wl) + bl
        return _layernorm(y, ln2_g, ln2_b)

    def _L0_attn_ref(x, W_qkv, b_qkv, W_out, b_out):
        import jax, jax.numpy as jnp
        import numpy as np
        D_MODEL = 192
        N_HEADS = 12
        D_HEAD = D_MODEL // N_HEADS
        B, T, D = x.shape
        scale = D_HEAD ** (-0.5)
        qkv = (x @ W_qkv + b_qkv).reshape(B, T, 3, N_HEADS, D_HEAD)
        q, k, v = (qkv[:, :, 0], qkv[:, :, 1], qkv[:, :, 2])
        attn = jnp.einsum('bqhd,bkhd->bhqk', q, k) * scale
        causal = jnp.tril(jnp.ones((T, T), dtype=bool))
        attn = jnp.where(causal, attn, -jnp.inf)
        attn = jax.nn.softmax(attn, axis=-1)
        out = jnp.einsum('bhqk,bkhd->bqhd', attn, v).reshape(B, T, D)
        return out @ W_out + b_out

    def _L0_ffn_ref(x, w_router, wi, wo):
        import jax, jax.numpy as jnp
        import numpy as np
        NUM_EXPERTS = 8
        TOP_K = 2
        CAPACITY_FACTOR = 1.25
        MAX_GROUP_SIZE = 1024
        MIN_EXPERT_CAPACITY = 4

        def _moe_forward(x, w_router, wi, wo):
            B, T, D = x.shape
            E = NUM_EXPERTS
            num_tokens = B * T
            G = max(num_tokens // MAX_GROUP_SIZE, E)
            while num_tokens % G != 0 or G % E != 0:
                G += 1
            S = num_tokens // G
            C = max(int(TOP_K * CAPACITY_FACTOR * S / E), MIN_EXPERT_CAPACITY)
            xg = x.reshape(G, S, D)
            logits = jnp.einsum('gsd,de->gse', xg.astype(jnp.float32), w_router.astype(jnp.float32))
            probs = jax.nn.softmax(logits, axis=-1)
            gate, idx = jax.lax.top_k(probs, TOP_K)
            idx_kf = jnp.swapaxes(idx, 1, 2).reshape(G, TOP_K * S)
            mask = jax.nn.one_hot(idx_kf, E, dtype=jnp.int32)
            prio = jnp.cumsum(mask, axis=1) * mask - 1
            prio = jnp.swapaxes(prio.reshape(G, TOP_K, S, E), 1, 2)
            prio_se = prio.max(axis=2)
            gate_se = jnp.einsum('gsk,gske->gse', gate, jax.nn.one_hot(idx, E, dtype=gate.dtype))
            dispatch = jax.nn.one_hot(prio_se, C, dtype=x.dtype)
            combine = dispatch * gate_se[..., None].astype(x.dtype)
            expert_in = jnp.einsum('gsec,gsd->egcd', dispatch, xg)
            h = jax.nn.relu(jnp.einsum('egcd,edf->egcf', expert_in, wi))
            expert_out = jnp.einsum('egcf,efd->egcd', h, wo)
            out = jnp.einsum('gsec,egcd->gsd', combine, expert_out)
            return out.reshape(B, T, D)
        return _moe_forward(x, w_router, wi, wo)
    h = _L0_tok_ref(x, L0_tok_ln1_g, L0_tok_ln1_b, L0_tok_Wl, L0_tok_bl, L0_tok_ln2_g, L0_tok_ln2_b, 16)
    h = h + _L0_attn_ref(_layernorm(h, axis=-1), L0_attn_W_qkv, L0_attn_b_qkv, L0_attn_W_out, L0_attn_b_out)
    h = h + _L0_ffn_ref(_layernorm(h, axis=-1), L0_ffn_w_router, L0_ffn_wi, L0_ffn_wo)
    return h

_drawn_inputs = setup_inputs


def setup_inputs(seed=0):
    import zlib

    import numpy as np

    out = dict(_drawn_inputs(seed))
    spreads = {'L0_tok_ln1_g': (1.0, 0.2),
     'L0_tok_ln1_b': (0.0, 0.1),
     'L0_tok_ln2_g': (1.0, 0.2),
     'L0_tok_ln2_b': (0.0, 0.1)}
    factors = {'L0_tok_bl': 2.972}
    for name, (base, spread) in spreads.items():
        noise = np.random.default_rng([zlib.crc32(name.encode()), seed]).standard_normal(out[name].shape)
        drawn = base * np.exp(spread * noise) if base else spread * noise
        out[name] = jnp.asarray(drawn.astype(out[name].dtype))
    for name, factor in factors.items():
        out[name] = (out[name] * factor).astype(out[name].dtype)
    return out
```

```python
from contextlib import ExitStack

import concourse.bass as bass
from concourse import mybir

ALU = mybir.AluOpType
ACT = mybir.ActivationFunctionType
AX = mybir.AxisListType
F32 = mybir.dt.float32
F32R = mybir.dt.float32r
BF16 = mybir.dt.bfloat16

P = 128
B, C_IN, IMG = 32, 3, 96
PATCH = 16
SIDE = IMG // PATCH
T = SIDE * SIDE
N = B * T
NT = N // P
D_PATCH = PATCH * PATCH * C_IN
KJ = D_PATCH // P
D = 192
DH = D // 2
DT = D - P
HEADS, HD = 12, 16
HG = HEADS // 4
H3 = 3
G3 = HEADS // H3
PAIRS = B // 2
QROWS = 64 + T
NE = 8
GROUPS = 8
S = N // GROUPS
CAP = max(int(2 * 1.25 * S / NE), 4)
SLOTS = GROUPS * CAP
FF = 768
FM = FF // P
GP = GROUPS // 2
PS = 2 * CAP
PTOK = 2 * S
SHIFT = P - (2 * P - S)
ROWS = B // 2 * SIDE
QI = 8
NQ = B // QI
CHUNK = QI * T
QP = QI // 2
EPS = 1e-5
NEG = -1e30
assert SHIFT == S - P and NT == GROUPS + 1 and ROWS == DH
TABLES = 16 + NT
R_LSH, R_PICK2, R_SLOTBF = 3, 13, 23


def build(nc, x, ln1_g, ln1_b, Wl, bl, ln2_g, ln2_b, W_qkv, b_qkv, W_out, b_out, w_router, wi, wo, out, taps=None):
    v_dram = nc.dram_tensor("v_scratch", (N, D), F32, kind="Internal").ap()
    with ExitStack() as ctx:
        def sb(name, shape, dt=F32, where=ctx):
            return where.enter_context(nc.sbuf_tensor(name, shape, dt))

        def sem(name):
            return ctx.enter_context(nc.semaphore(name))

        bank = [ctx.enter_context(nc.psum_tensor(f"bank{i}", [P, 512], F32)) for i in range(8)]
        bank_bf = {i: bank[i][:, :].bitcast(BF16) for i in (6, 7)}

        identity = sb("identity", [P, P])
        identity_bf = sb("identity_bf", [P, P], BF16)
        fold = sb("fold", [P, DT])
        minus_half = sb("minus_half", [P, NT])
        h = sb("h", [P, NT, D])
        a = sb("a", [P, NT, D])
        aT = sb("aT", [DH, 2, N])
        stats = sb("stats", [P, NT, 6])
        moments = sb("moments", [P, NT, 2])
        rstd = sb("rstd", [P, NT])
        wr_sb = sb("wr_sb", [DH, 2, NE])
        wout_sb = sb("wout_sb", [DH, 2, D])
        bout_bc = sb("bout_bc", [P, D])
        oT = sb("oT", [DH, 2, N])
        y_acc = oT
        same = sb("same", [P, NT, P], BF16)
        before = sb("before", [P, NT, P], BF16)
        prev_tile = sb("prev_tile", [P, NT, P], BF16)
        next_tile = sb("next_tile", [P, NT, P], BF16)
        expert_no = sb("expert_no", [P, NE])
        slot_no = sb("slot_no", [P, 2, CAP])
        parity = sb("parity", [P, NT])
        slot_of_row = sb("slot_of_row", [PS, 1])
        second_row = sb("second_row", [PS, 1])
        pick = sb("pick", [NE, NE, PS], BF16)

        with ExitStack() as r1:
            xin = sb("xin", [ROWS, 2, C_IN * PATCH, SIDE, PATCH], where=r1)
            pT = sb("pT", [P, KJ, N], where=r1)
        with ExitStack() as r1:
            ones = sb("ones", [P, NT, P], BF16, where=r1)
            row_ge = sb("row_ge", [P, NT, P], BF16, where=r1)
            col_ge = sb("col_ge", [P, NT, P], BF16, where=r1)
        wi_raw = sb("wi_raw", [P, 2, 2, FF])
        wo_raw = sb("wo_raw", [P, 2, FM, D])
        wi_hi = sb("wi_hi", [P, 2, 2, FF], F32R)
        wi_lo = sb("wi_lo", [P, 2, 2, FF], F32R)
        wo_hi = sb("wo_hi", [P, 2, FM, 2 * P], F32R)
        wo_lo = sb("wo_lo", [P, 2, FM, P], F32R)

        with ExitStack() as r2:
            wqkv_sb = sb("wqkv_sb", [DH, 2, 3 * D], where=r2)
            wqk_pad = sb("wqk_pad", [DH, 2, 2, HEADS, 32], where=r2)
            bqk_pad = sb("bqk_pad", [P, 2, HG], where=r2)
            bv_bc = sb("bv_bc", [P, D], where=r2)
            v_sb = sb("v_sb", [P, 3, D], where=r2)
            qT = sb("qT", [P, 2, HG, CHUNK], where=r2)
            k_tmp = sb("k_tmp", [P, 3, CHUNK], where=r2)
            k_diag = sb("k_diag", [P, 2, HG, 4, CHUNK], where=r2)
            v_diag = sb("v_diag", [H3 * T, 2 * QI, G3, H3, HD + 1], where=r2)
            own_head = sb("own_head", [H3 * T, H3], where=r2)
            causal = sb("causal", [QROWS, T], where=r2)
            causal2 = sb("causal2", [QROWS, T], where=r2)
            head_rows = sb("head_rows", [P, 4], where=r2)
            with ExitStack() as r4:
                xn = sb("xn", [ROWS, SIDE, D_PATCH], where=r4)
                wl_sb = sb("wl_sb", [P, 2, C_IN, D], where=r4)
                g1_sb = sb("g1_sb", [P, 2, C_IN], where=r4)
                b1_sb = sb("b1_sb", [P, 2, C_IN], where=r4)
                bl_bc = sb("bl_bc", [P, D], where=r4)
                g2_bc = sb("g2_bc", [P, D], where=r4)
                b2_bc = sb("b2_bc", [P, D], where=r4)
                pstats = sb("pstats", [ROWS, 2, SIDE, 2, 6], where=r4)
                pmom = sb("pmom", [ROWS, 2, SIDE, 2], where=r4)
                prstd = sb("prstd", [ROWS, 2, SIDE], where=r4)
            v_rep = sb("v_rep", [H3 * T, QI, D], where=r2)
            sm = sb("sm", [QROWS, 2, HEADS, T], where=r2)
            smax = sb("smax", [QROWS, 2, HEADS], where=r2)
            probs = sb("probs", [QROWS, 2, HEADS, T], where=r2)
            probsT = sb("probsT", [H3 * T, 2, G3, QROWS], where=r2)
            rsum = sb("rsum", [QROWS, 2, HEADS], where=r2)
            o_sb = sb("o_sb", [QROWS, 2, HEADS, HD], where=r2)
        lg = sb("lg", [P, NT, NE])
        lg2 = sb("lg2", [P, NT, NE])
        top = sb("top", [P, 2, NT])
        eq = sb("eq", [P, NT, NE])
        first = sb("first", [P, 2, NT])
        pick1 = sb("pick1", [P, NT, NE], BF16)
        pick2 = sb("pick2", [P, NT, NE], BF16)
        lsh = sb("lsh", [P, NT, NE])
        ex = sb("ex", [P, NT, NE])
        esum = sb("esum", [P, NT])
        erec = sb("erec", [P, NT])
        gate = sb("gate", [P, NT, NE])
        gate_hi = sb("gate_hi", [P, NT, NE], F32R)
        gate_lo = sb("gate_lo", [P, NT, NE])
        s1 = sb("s1", [P, NT, NE])
        s2 = sb("s2", [P, NT, NE])
        slot = sb("slot", [P, NT, NE])
        slot_bf = sb("slot_bf", [P, NT, NE], BF16)
        slotT = sb("slotT", [NE, N], BF16)
        ein_hi = sb("ein_hi", [P, NE, SLOTS], F32R)
        ein_lo = sb("ein_lo", [P, NE, SLOTS], F32R)
        ein_tail = sb("ein_tail", [P, NE, SLOTS], F32R)
        with ExitStack() as r3:
            a_hi = sb("a_hi", [P, NT, 2 * P], F32R, where=r3)
            a_lo = sb("a_lo", [P, NT, 2 * P], F32R, where=r3)
            d01 = sb("d01", [P, 4, NE, CAP], where=r3)
            d_hi = sb("d_hi", [P, 4, NE, CAP], F32R, where=r3)
            d_lo = sb("d_lo", [P, 4, NE, CAP], F32R, where=r3)
        hid_hi = sb("hid_hi", [P, FM, SLOTS], F32R)
        hid_lo = sb("hid_lo", [P, FM, SLOTS], F32R)
        comb = sb("comb", [PS, 2, GP, PTOK], F32R)
        eoT = sb("eoT", [P, 2, SLOTS])
        eo_hi = sb("eo_hi", [PS, GP, D], F32R)
        eo_lo = sb("eo_lo", [PS, GP, D], F32R)

        x_in = [sem(f"x_in{t}") for t in range(2)]
        wl_in, aff_in, wq_in, wo_in, bqk_in = sem("wl_in"), sem("aff_in"), sem("wq_in"), sem("wo_in"), sem("bqk_in")
        wi_in = [sem(f"wi_in{i}") for i in range(2)]
        consts, vones, tables, scratch = sem("consts"), sem("vones"), sem("tables"), sem("scratch")
        bank_set = sem("bank_set")
        pstat_done, pmom_done, prstd_done, pnorm_done = sem("pstat_done"), sem("pmom_done"), sem("prstd_done"), sem("pnorm_done")
        pt_made, pt_act, pt_dve = sem("pt_made"), sem("pt_act"), sem("pt_dve")
        emb_made, emb_out = sem("emb_made"), sem("emb_out")
        st_done, mo_done, var_done, rstd_done = sem("st_done"), sem("mo_done"), sem("var_done"), sem("rstd_done")
        norm_done, gain_done, h_done = sem("norm_done"), sem("gain_done"), sem("h_done")
        aT_made, aT_done = sem("aT_made"), sem("aT_done")
        v_made, v_out, v_stored, v_loaded, v_ready = sem("v_made"), sem("v_out"), [sem(f"v_stored{i}") for i in range(3)], [sem(f"v_loaded{i}") for i in range(2)], sem("v_ready")
        wqk_ready, masks = sem("wqk_ready"), sem("masks")
        qk_made, q_out, k_out, k_ready = sem("qk_made"), sem("q_out"), sem("k_out"), sem("k_ready")
        sc_made, sm_masked, sm_max, sm_shift, p_done = sem("sc_made"), sem("sm_masked"), sem("sm_max"), sem("sm_shift"), sem("p_done")
        pT_made, pT_done, o_made, rs_done, o_done, oT_made, oT_done = (sem(s) for s in ("pT_made", "pT_done", "o_made", "rs_done", "o_done", "oT_made", "oT_done"))
        wout_made, res1 = sem("wout_made"), sem("res1")
        lg_made, route, ex_done, prio_made, slotT_made, slotT_done, ahi_done, alo_done = (sem(s) for s in ("lg_made", "route", "ex_done", "prio_made", "slotT_made", "slotT_done", "ahi_done", "alo_done"))
        d01_done, dhi_done, dlo_done, disp_made, einhi_done, einlo_done = (sem(s) for s in ("d01_done", "dhi_done", "dlo_done", "disp_made", "einhi_done", "einlo_done"))
        whi_done, wlo_done, twice_done = sem("whi_done"), sem("wlo_done"), sem("twice_done")
        up_made, hidhi_done, hidlo_done, down_made, eoT_done = (sem(s) for s in ("up_made", "hidhi_done", "hidlo_done", "down_made", "eoT_done"))
        eo_made, eohi_done, eolo_done, bc_made, comb_done, y_made, y_done = (sem(s) for s in ("eo_made", "eohi_done", "eolo_done", "bc_made", "comb_done", "y_made", "y_done"))
        yt_made, fin_done, out_sent = sem("yt_made"), sem("fin_done"), sem("out_sent")

        BATCHES = [range(0, 4), range(4, NT)]
        LN_SETS = [("emb", t, BATCHES[t]) for t in range(2)]

        ctx.enter_context(nc.allow_non_contiguous_dma("row-sized runs"))
        block = ctx.enter_context(nc.Block())

        def patch_unit(u):
            t, j, w = u // (2 * KJ), u // 2 % KJ, u % 2
            src = bank[u % 4][:, 0:3 * ROWS].rearrange("p (w r) -> p w r", w=3)
            dst = pT[:, j, t * ROWS * SIDE:(t + 1) * ROWS * SIDE].rearrange("p (r w) -> p w r", w=SIDE)[:, 3 * w:3 * w + 3, :]
            gain, bias = (v[:, j % 2, j // 2:j // 2 + 1] for v in (g1_sb, b1_sb))
            return src, dst, gain, bias

        @block.sync
        def _(sp):
            xv = x.rearrange("(t b) c (h q) w -> t c b h (q w)", t=2, q=PATCH)
            for t in range(2):
                for c in range(C_IN):
                    sp.dma_start(xin[:, t, c * PATCH:(c + 1) * PATCH, :, :], xv[t, c]).then_inc(x_in[t], 16)
                if t == 0:
                    sp.dma_start(wl_sb[:], Wl.rearrange("(f n c) e -> n f c e", f=2, c=C_IN)).then_inc(wl_in, 16)
            sp.dma_start(wqkv_sb[:], W_qkv.rearrange("(k p) n -> p k n", k=2)).then_inc(wq_in, 16)
            sp.dma_start(wout_sb[:], W_out.rearrange("(k p) n -> p k n", k=2)).then_inc(wo_in, 16)
            sp.dma_start(wr_sb[:], w_router.rearrange("(k p) n -> p k n", k=2)).then_inc(wo_in, 16)
            sp.dma_start(bout_bc[:], b_out.rearrange("(o n) -> o n", o=1).to_broadcast([P, D])).then_inc(wo_in, 16)
            for i in range(NT):
                sp.wait_ge(v_out, i + 1)
                sp.dma_start(v_dram[i * P:(i + 1) * P, :], v_sb[:, i % 3, :]).then_inc(v_stored[i % 3], 16)
            for r in range(3):
                sp.wait_ge(v_stored[r], 16 * (NT // 3))
            for q in range(NQ):
                if q >= 1:
                    sp.wait_ge(v_ready, q)
                vq = v_dram[q * CHUNK:(q + 1) * CHUNK, :].rearrange("(b k) d -> k b d", k=T)
                for r in range(H3):
                    sp.dma_start(v_rep[r * T:(r + 1) * T, :, :], vq).then_inc(v_loaded[q % 2], 16)
            sp.wait_ge(tables, TABLES)
            for e in range(NE):
                if e >= 2:
                    sp.wait_ge(wlo_done, 2 * (e - 1))
                sp.dma_start(wi_raw[:, e % 2, 0, :], wi[e, 0:P, :]).then_inc(wi_in[e % 2], 16)
                for r in range(2):
                    sp.dma_start(wi_raw[r * DT:(r + 1) * DT, e % 2, 1, :], wi[e, P:D, :]).then_inc(wi_in[e % 2], 16)
                sp.dma_start(wo_raw[:, e % 2, :, :], wo[e].rearrange("(m p) d -> p m d", m=FM)).then_inc(wi_in[e % 2], 16)
            for i in range(NT):
                sp.wait_ge(fin_done, i + 1)
                sp.dma_start(out[i * P:(i + 1) * P, :], a[:, i, :]).then_inc(out_sent, 16)
            sp.wait_ge(out_sent, 16 * NT)
            if taps:
                for nm, ap in taps.items():
                    src = locals_[nm]
                    sp.dma_start(ap, src[:]).then_inc(out_sent, 16)
                sp.wait_ge(out_sent, 16 * (NT + len(taps)))

        locals_ = dict(h=h, a=a, aT=aT, qT=qT, oT=oT, lg=lg, gate=gate, slot=slot, slotT=slotT, y_acc=y_acc, pT=pT, k_diag=k_diag, v_diag=v_diag, ein_hi=ein_hi, probs=probs, sm=sm)

        @block.gpsimd
        def _(gp):
            gp.memset(identity[:], 0.0).then_inc(consts, 1)
            gp.memset(identity_bf[:], 0.0).then_inc(consts, 1)
            gp.memset(minus_half[:], -0.5).then_inc(consts, 1)
            gp.memset(causal[:], 0.0).then_inc(consts, 1)
            gp.memset(causal2[:], 0.0).then_inc(consts, 1)
            gp.memset(head_rows[:], 1.0).then_inc(consts, 1)
            gp.memset(bqk_pad[:], 0.0).then_inc(consts, 1)
            gp.memset(own_head[:], 1.0).then_inc(consts, 1)
            gp.memset(pick[:], 1.0).then_inc(consts, 1)
            gp.wait_ge(consts, 9)
            for m in (identity, identity_bf):
                gp.affine_select(out=m[:], in_=m[:], compare_op=ALU.not_equal, fill=1.0, base=0,
                                 pattern=[[-1, P]], channel_multiplier=1).then_inc(consts, 1)
            gp.wait_ge(consts, 11)
            gp.tensor_tensor(fold[:], identity[:, 0:DT], identity[:, DT:P], ALU.add).then_inc(consts, 1)
            for t in range(2):
                gp.wait_ge(pmom_done, SIDE * (t + 1))
                gp.tensor_scalar(prstd[:, t, :], pmom[:, t, :, 1], EPS, None, ALU.add).then_inc(prstd_done, 1)
                gp.wait_ge(prstd_done, 2 * t + 1)
                gp.tensor_tensor(prstd[:, t, :], prstd[:, t, :], minus_half[0:ROWS, 0:SIDE], ALU.pow).then_inc(prstd_done, 1)
                if t == 0:
                    gp.memset(wqk_pad[:], 0.0).then_inc(wqk_ready, 1)
                    gp.wait_ge(wq_in, 16)
                    gp.wait_ge(wqk_ready, 1)
                    for i in range(2):
                        gp.tensor_copy(wqk_pad[:, :, i, :, 0:HD],
                                       wqkv_sb[:, :, i * D:(i + 1) * D].rearrange("p k (h d) -> p k h d", h=HEADS)).then_inc(wqk_ready, 1)
            for n in range(4):
                tiles = BATCHES[n // 2]
                lo, hi = tiles[0], tiles[-1] + 1
                gp.wait_ge(mo_done, [4, 8, 13, 18][n])
                gp.tensor_scalar(rstd[:, lo:hi], moments[:, lo:hi, 1], EPS, None, ALU.add).then_inc(var_done, 1)
                gp.wait_ge(var_done, n + 1)
                gp.tensor_tensor(rstd[:, lo:hi], rstd[:, lo:hi], minus_half[:, lo:hi], ALU.pow).then_inc(rstd_done, 1)
                if n == 1:
                    gp.affine_select(out=causal[:], in_=causal[:], compare_op=ALU.is_ge, fill=NEG, base=0,
                                     pattern=[[-1, T]], channel_multiplier=1).then_inc(masks, 1)
                    gp.affine_select(out=causal2[:], in_=causal2[:], compare_op=ALU.is_ge, fill=NEG, base=-64,
                                     pattern=[[-1, T]], channel_multiplier=1).then_inc(masks, 1)
                    gp.affine_select(out=own_head[:], in_=own_head[:], compare_op=ALU.is_ge, fill=0.0, base=0,
                                     pattern=[[-T, H3]], channel_multiplier=1).then_inc(masks, 1)
                    gp.affine_select(out=head_rows[:], in_=head_rows[:], compare_op=ALU.is_ge, fill=0.0, base=0,
                                     pattern=[[-32, 4]], channel_multiplier=1).then_inc(masks, 1)
                    gp.wait_ge(masks, 4)
                    gp.affine_select(out=causal2[:], in_=causal2[:], compare_op=ALU.is_ge, fill=0.0, base=-64,
                                     pattern=[[0, T]], channel_multiplier=1).then_inc(masks, 1)
                    gp.affine_select(out=own_head[:], in_=own_head[:], compare_op=ALU.is_ge, fill=0.0, base=T - 1,
                                     pattern=[[T, H3]], channel_multiplier=-1).then_inc(masks, 1)
                    gp.affine_select(out=head_rows[:], in_=head_rows[:], compare_op=ALU.is_ge, fill=0.0, base=31,
                                     pattern=[[32, 4]], channel_multiplier=-1).then_inc(masks, 1)
                    gp.wait_ge(masks, 7)
                    gp.tensor_tensor(causal[:], causal[:], causal2[:], ALU.add).then_inc(masks, 1)
                    for b in range(2 * QI):
                        gp.tensor_copy(v_diag[:, b, :, :, HD], own_head[:, None, :].to_broadcast([H3 * T, G3, H3])).then_inc(vones, 1)
            for q in range(NQ):
                if q >= 2:
                    gp.wait_ge(sc_made, QP * (q - 1))
                for g in range(HG):
                    n = q * HG + g
                    gp.wait_ge(k_out, n + 1)
                    gp.tensor_tensor(k_diag[:, q % 2, g, :, :], k_tmp[:, n % 3, None, :].to_broadcast([P, 4, CHUNK]),
                                     head_rows[:, :, None].to_broadcast([P, 4, CHUNK]), ALU.mult).then_inc(k_ready, 1)
                if q >= 2:
                    gp.wait_ge(o_made, QP * (q - 1))
                gp.wait_ge(v_loaded[q % 2], 16 * H3 * (q // 2 + 1))
                for b in range(QI):
                    ins = gp.tensor_tensor(v_diag[:, q % 2 * QI + b, :, :, 0:HD],
                                           v_rep[:, b, :].rearrange("p (g h d) -> p g h d", g=G3, h=H3),
                                           own_head[:, None, :, None].to_broadcast([H3 * T, G3, H3, HD]), ALU.mult)
                ins.then_inc(v_ready, 1)
            gp.wait_ge(emb_made, NT)
            gp.memset(ones[:], 1.0).then_inc(scratch, 1)
            gp.wait_ge(scratch, 1)
            gp.affine_select(out=row_ge[:], in_=ones[:], compare_op=ALU.is_ge, fill=0.0, base=0,
                             pattern=[[-SHIFT, NT], [0, P]], channel_multiplier=1).then_inc(tables, 1)
            gp.affine_select(out=col_ge[:], in_=ones[:], compare_op=ALU.is_ge, fill=0.0, base=0,
                             pattern=[[-SHIFT, NT], [1, P]], channel_multiplier=0).then_inc(tables, 1)
            gp.affine_select(out=prev_tile[:], in_=ones[:], compare_op=ALU.is_ge, fill=0.0, base=SHIFT,
                             pattern=[[-SHIFT, NT], [0, P]], channel_multiplier=1).then_inc(tables, 1)
            gp.affine_select(out=next_tile[:], in_=ones[:], compare_op=ALU.is_gt, fill=0.0, base=SHIFT,
                             pattern=[[SHIFT, NT], [0, P]], channel_multiplier=-1).then_inc(tables, 1)
            gp.affine_select(out=pick[:], in_=pick[:], compare_op=ALU.is_equal, fill=0.0, base=0,
                             pattern=[[-1, NE], [0, PS]], channel_multiplier=1).then_inc(tables, 1)
            gp.iota(expert_no[:], pattern=[[1, NE]], base=-NE, channel_multiplier=0, allow_small_or_imprecise_dtypes=True).then_inc(tables, 1)
            gp.iota(slot_no[:], pattern=[[64, 2], [1, CAP]], base=1, channel_multiplier=0, allow_small_or_imprecise_dtypes=True).then_inc(tables, 1)
            gp.iota(slot_of_row[:], pattern=[[0, 1]], base=1, channel_multiplier=1, allow_small_or_imprecise_dtypes=True).then_inc(tables, 1)
            gp.memset(second_row[:], 64.0 - CAP).then_inc(tables, 1)
            gp.wait_ge(tables, 9)
            gp.tensor_tensor(ones[:], row_ge[:], col_ge[:], ALU.subtract).then_inc(tables, 1)
            gp.affine_select(out=prev_tile[:], in_=prev_tile[:], compare_op=ALU.is_gt, fill=0.0, base=0,
                             pattern=[[SHIFT, NT], [-1, P]], channel_multiplier=0).then_inc(tables, 1)
            gp.affine_select(out=next_tile[:], in_=next_tile[:], compare_op=ALU.is_ge, fill=0.0, base=0,
                             pattern=[[-SHIFT, NT], [1, P]], channel_multiplier=0).then_inc(tables, 1)
            gp.tensor_copy(parity[:], row_ge[:, :, 0]).then_inc(tables, 1)
            gp.affine_select(out=second_row[:], in_=second_row[:], compare_op=ALU.is_ge, fill=0.0, base=-CAP,
                             pattern=[[0, 1]], channel_multiplier=1).then_inc(tables, 1)
            gp.wait_ge(tables, 14)
            gp.tensor_tensor(col_ge[:], ones[:], ones[:], ALU.mult).then_inc(scratch, 1)
            gp.wait_ge(scratch, 2)
            gp.tensor_scalar(same[:], col_ge[:], -1.0, 1.0, ALU.mult, ALU.add).then_inc(scratch, 1)
            gp.wait_ge(scratch, 3)
            gp.affine_select(out=before[:], in_=same[:], compare_op=ALU.is_gt, fill=0.0, base=0,
                             pattern=[[0, NT], [1, P]], channel_multiplier=-1).then_inc(tables, 1)
            gp.tensor_tensor(slot_of_row[:], slot_of_row[:], second_row[:], ALU.add).then_inc(tables, 1)
            for t in range(NT):
                scale, off = (64.0, 0.0) if t % 2 else (-64.0, 64.0)
                gp.tensor_scalar(parity[:, t:t + 1], parity[:, t:t + 1], scale, off, ALU.mult, ALU.add).then_inc(tables, 1)

            def split_weights(e):
                s = e % 2
                gp.wait_ge(whi_done, 2 * e + 1)
                gp.tensor_tensor(wi_lo[:, s, :, :], wi_raw[:, s, :, :], wi_hi[:, s, :, :].bitcast(F32), ALU.subtract).then_inc(wlo_done, 1)
                gp.wait_ge(whi_done, 2 * e + 2)
                gp.tensor_tensor(wo_lo[:, s, :, :], wo_raw[:, s, :, 0:P], wo_hi[:, s, :, 0:P].bitcast(F32), ALU.subtract)
                gp.tensor_tensor(wo_hi[:, s, :, D:2 * P], wo_raw[:, s, :, P:D], wo_hi[:, s, :, P:D].bitcast(F32), ALU.subtract).then_inc(wlo_done, 1)

            gp.wait_ge(mo_done, 3 * NT)
            gp.tensor_scalar(rstd[:], moments[:, :, 1], EPS, None, ALU.add).then_inc(var_done, 1)
            gp.wait_ge(var_done, 5)
            gp.tensor_tensor(rstd[:], rstd[:], minus_half[:], ALU.pow).then_inc(rstd_done, 1)
            for n, (done, part) in enumerate(((ahi_done, a_hi), (alo_done, a_lo))):
                gp.wait_ge(done, NT)
                gp.tensor_copy(part[:, :, D:2 * P], part[:, :, P:D].bitcast(F32)).then_inc(twice_done, 1)
            split_weights(0)
            for n in range(2 * GROUPS):
                gp.wait_ge(d01_done, n + 1)
                if n >= 4:
                    gp.wait_ge(disp_made, 2 * ((n - 4) // 2 + 1))
                t = n // 2 + n % 2
                gp.tensor_tensor(d_lo[:, n % 4, :, :], d01[:, n % 4, :, :],
                                 gate_lo[:, t, :, None].to_broadcast([P, NE, CAP]), ALU.mult).then_inc(dlo_done, 1)
            for e in range(1, NE):
                split_weights(e)

        def ein_low(g):
            c = slice(g * CAP, (g + 1) * CAP)
            src = [bank[(2 * g + k) % 4][:, 0:NE * CAP].rearrange("p (e c) -> p e c", e=NE) for k in range(2)]
            nc.vector.wait_ge(einhi_done, 2 * g + 1)
            nc.vector.tensor_tensor(ein_lo[:, :, c], src[0], ein_hi[:, :, c].bitcast(F32), ALU.subtract).then_inc(einlo_done, 1)
            nc.vector.wait_ge(einhi_done, 2 * g + 2)
            nc.vector.tensor_tensor(ein_tail[DT:P, :, c], src[1][DT:P], ein_tail[DT:P, :, c].bitcast(F32), ALU.subtract).then_inc(einlo_done, 1)

        @block.scalar
        def _(act):
            act.dma_start(g1_sb[:], ln1_g.rearrange("(f n c) -> n f c", f=2, c=C_IN)).then_inc(aff_in, 16)
            act.dma_start(b1_sb[:], ln1_b.rearrange("(f n c) -> n f c", f=2, c=C_IN)).then_inc(aff_in, 16)
            for dst, src in ((bl_bc, bl), (g2_bc, ln2_g), (b2_bc, ln2_b), (bv_bc, b_qkv[2 * D:3 * D])):
                act.dma_start(dst[:], src.rearrange("(o n) -> o n", o=1).to_broadcast([P, D])).then_inc(aff_in, 16)
            act.wait_ge(consts, 9)
            for i in range(2):
                for hh in range(4):
                    act.dma_start(bqk_pad[32 * hh:32 * hh + HD, i, :],
                                  b_qkv[i * D:(i + 1) * D].rearrange("(g h d) -> h d g", h=4, d=HD)[hh]).then_inc(bqk_in, 16)
            act.wait_ge(aff_in, 16 * 6)
            for u in range(0, 4 * KJ, 2):
                src, dst, gain, bias = patch_unit(u)
                act.wait_ge(pt_made, u + 1)
                act.activation(dst, src, ACT.Identity, bias=bias, scale=gain).then_inc(pt_act, 1)
            for i in range(NT):
                act.wait_ge(aT_made, i + 1)
                act.activation(aT[:, :, i * P:(i + 1) * P], bank[6 + i % 2][0:DH, 0:2 * P].rearrange("p (k n) -> p k n", k=2),
                               ACT.Copy).then_inc(aT_done, 1)
            act.wait_ge(bqk_in, 16 * 8)

            def key_out(n):
                act.wait_ge(qk_made, 2 * n + 2)
                if n >= 3:
                    act.wait_ge(k_ready, n - 2)
                act.activation(k_tmp[:, n % 3, :], bank[7][:, 0:CHUNK], ACT.Identity,
                               bias=bqk_pad[:, 1, n % HG:n % HG + 1]).then_inc(k_out, 1)

            for n in range(HG):
                key_out(n)
            for step in range(PAIRS + 4):
                p = step - 1
                if 0 <= p < PAIRS:
                    act.wait_ge(sm_shift, p + 1)
                    if p >= 2:
                        act.wait_ge(pT_made, p - 1)
                    act.activation(probs[:, p % 2, :, :], sm[:, p % 2, :, :], ACT.Exp, scale=HD ** -0.5).then_inc(p_done, 1)
                p = step - 2
                if 0 <= p < PAIRS:
                    act.wait_ge(pT_made, p + 1)
                    if p >= 2:
                        act.wait_ge(o_made, p - 1)
                    act.activation(probsT[:, p % 2, :, :], bank[2 + p % 2][0:H3 * T, 0:G3 * QROWS].rearrange("p (g q) -> p g q", g=G3),
                                   ACT.Copy).then_inc(pT_done, 1)
                p = step - 4
                if 0 <= p < PAIRS:
                    act.wait_ge(oT_made, p + 1)
                    src = bank[5][0:DH, 0:256].rearrange("p (k b q) -> p k b q", k=2, b=2)[:, :, :, 0:T]
                    act.activation(oT[:, :, p * 2 * T:(p + 1) * 2 * T].rearrange("p k (b q) -> p k b q", b=2), src,
                                   ACT.Copy).then_inc(oT_done, 1)
                if step % QP < HG and step // QP + 1 < NQ:
                    key_out((step // QP + 1) * HG + step % QP)
            def round_up_weights(e):
                s = e % 2
                act.wait_ge(wi_in[s], 16 * 4 * (e // 2 + 1))
                if e >= 2:
                    act.wait_ge(up_made, FM * (e - 1))
                act.activation(wi_hi[:, s, :, :], wi_raw[:, s, :, :], ACT.Copy).then_inc(whi_done, 1)

            def round_down_weights(e):
                s = e % 2
                if e >= 2:
                    act.wait_ge(down_made, e - 1)
                act.activation(wo_hi[:, s, :, 0:D], wo_raw[:, s, :, :], ACT.Copy).then_inc(whi_done, 1)

            for i in range(NT):
                act.wait_ge(norm_done, 3 * NT - NT + i + 1)
                act.activation(a_hi[:, i, 0:D], a[:, i, :], ACT.Copy).then_inc(ahi_done, 1)
                act.wait_ge(aT_made, NT + i + 1)
                act.activation(aT[:, :, i * P:(i + 1) * P], bank[2 + i % 2][0:DH, 0:2 * P].rearrange("p (k n) -> p k n", k=2),
                               ACT.Copy).then_inc(aT_done, 1)
            act.wait_ge(route, R_LSH)
            act.activation(ex[:], lsh[:], ACT.Exp).then_inc(ex_done, 1)
            round_up_weights(0)
            round_down_weights(0)
            round_up_weights(1)
            for g in range(GROUPS):
                for k in range(2):
                    n = 2 * g + k
                    act.wait_ge(disp_made, n + 1)
                    act.activation((ein_hi, ein_tail)[k][:, :, g * CAP:(g + 1) * CAP],
                                   bank[n % 4][:, 0:NE * CAP].rearrange("p (e c) -> p e c", e=NE), ACT.Copy).then_inc(einhi_done, 1)

            def eo_high(e):
                for r in range(2):
                    act.wait_ge(eo_made, 2 * e + r + 1)
                    if e >= 1:
                        act.wait_ge(y_made, 2 * GP * e)
                    act.activation(eo_hi[:, 2 * r:2 * r + 2, :], bank[4 + r][0:PS, 0:2 * D].rearrange("p (g d) -> p g d", g=2),
                                   ACT.Copy).then_inc(eohi_done, 1)

            for e in range(NE):
                for m in range(FM):
                    act.wait_ge(up_made, FM * e + m + 1)
                    if e >= 1:
                        act.wait_ge(down_made, e)
                    act.activation(hid_hi[:, m, :], bank[m % 2][:, 0:SLOTS], ACT.Relu).then_inc(hidhi_done, 1)
                    if m == 1 and e >= 1:
                        eo_high(e - 1)
                if e + 1 < NE:
                    round_down_weights(e + 1)
                if e + 2 < NE:
                    round_up_weights(e + 2)
                act.wait_ge(down_made, e + 1)
                if e >= 1:
                    act.wait_ge(eo_made, 2 * e)
                for k in range(2):
                    act.activation(eoT[:, k, :], bank[2 + k][:, 0:SLOTS], ACT.Copy).then_inc(eoT_done, 1)
            eo_high(NE - 1)

        @block.tensor
        def _(pe):
            pe.wait_ge(consts, 12)
            pe.wait_ge(bank_set, 3)

            def embed(i):
                for j in range(KJ):
                    mm = pe.matmul(bank[4 + i % 4][:, 0:D], pT[:, j, i * P:(i + 1) * P], wl_sb[:, j % 2, j // 2, :],
                                   start=(j == 0), stop=(j == KJ - 1))
                mm.then_inc(emb_made, 1)

            for t in range(2):
                pe.wait_ge(pnorm_done, SIDE * (t + 1))
                for v in range(2 * KJ):
                    u = 2 * KJ * t + v
                    j, w = v // 2, v % 2
                    if u >= 4:
                        pe.wait_ge(pt_act if u % 2 == 0 else pt_dve, (u - 4) // 2 + 1)
                    for k in range(3):
                        src = xn[:, 3 * w + k, j * P:(j + 1) * P]
                        mm = pe.transpose(bank[u % 4][:, k * ROWS:(k + 1) * ROWS], src, identity[0:ROWS, 0:ROWS])
                    mm.then_inc(pt_made, 1)
                pe.wait_ge(pt_act, KJ * (t + 1))
                pe.wait_ge(pt_dve, KJ * (t + 1))
                pe.wait_ge(wl_in, 16)
                for i in BATCHES[t]:
                    if i >= 4:
                        pe.wait_ge(emb_out, i - 3)
                    embed(i)
            pe.wait_ge(emb_out, NT)
            for i in range(NT):
                pe.wait_ge(norm_done, [*range(4 + 1, 8 + 1), *range(13 + 1, 18 + 1)][i])
                if i >= 2:
                    pe.wait_ge(aT_done, i - 1)
                for k in range(2):
                    mm = pe.transpose(bank[6 + i % 2][0:DH, k * P:(k + 1) * P], a[:, i, k * DH:(k + 1) * DH], identity[:])
                mm.then_inc(aT_made, 1)
            for i in range(NT):
                pe.wait_ge(aT_done, i + 1)
                if i == 0:
                    pe.wait_ge(emb_out, NT)
                    pe.wait_ge(wq_in, 16)
                if i >= 2:
                    pe.wait_ge(v_out, i - 1)
                for k in range(2):
                    mm = pe.matmul(bank[4 + i % 2][:, 0:D], aT[:, k, i * P:(i + 1) * P], wqkv_sb[:, k, 2 * D:3 * D], start=(k == 0), stop=(k == 1))
                mm.then_inc(v_made, 1)
            pe.wait_ge(wqk_ready, 3)
            pe.wait_ge(pt_act, 2 * KJ)
            pe.wait_ge(pt_dve, 2 * KJ)

            def project(n):
                q, g = n // HG, n % HG
                for i in range(2):
                    if n == 0:
                        pe.wait_ge(aT_done, NT)
                    else:
                        pe.wait_ge(k_out if i else q_out, n)
                    for k in range(2):
                        mm = pe.matmul(bank[6 + i][:, 0:CHUNK], wqk_pad[:, k, i, 4 * g:4 * g + 4, :],
                                       aT[:, k, q * CHUNK:(q + 1) * CHUNK], start=(k == 0), stop=(k == 1))
                    mm.then_inc(qk_made, 1)

            for n in range(HG):
                project(n)
            for step in range(PAIRS + 4):
                p = step
                if p < PAIRS:
                    if p % QP == 0:
                        pe.wait_ge(q_out, HG * (p // QP + 1))
                        pe.wait_ge(k_ready, HG * (p // QP + 1))
                    if p >= 2:
                        pe.wait_ge(sm_masked, p - 1)
                    for b in range(2):
                        tok = (2 * p + b) % QI * T
                        s = p // QP % 2
                        for g in range(HG):
                            mm = pe.matmul(bank[p % 2][64 * b:64 * b + T, g * 4 * T:(g + 1) * 4 * T], qT[:, s, g, tok:tok + T],
                                           k_diag[:, s, g, :, tok:tok + T], start=True, stop=True)
                    mm.then_inc(sc_made, 1)
                if step % QP < HG and step // QP + 1 < NQ:
                    project((step // QP + 1) * HG + step % QP)
                p = step - 2
                if 0 <= p < PAIRS:
                    pe.wait_ge(p_done, p + 1)
                    if p >= 2:
                        pe.wait_ge(pT_done, p - 1)
                    for g in range(G3):
                        mm = pe.transpose(bank[2 + p % 2][0:H3 * T, g * QROWS:(g + 1) * QROWS], probs[:, p % 2, H3 * g:H3 * g + H3, :],
                                          identity[0:QROWS, 0:QROWS])
                    mm.then_inc(pT_made, 1)
                p = step - 3
                if 0 <= p < PAIRS:
                    pe.wait_ge(pT_done, p + 1)
                    if p % QP == 0:
                        pe.wait_ge(v_ready, p // QP + 1)
                    if p == 0:
                        pe.wait_ge(v_out, NT)
                        pe.wait_ge(vones, 2 * QI)
                    if p >= 1:
                        pe.wait_ge(o_done, p)
                    for b in range(2):
                        for g in range(G3):
                            w = H3 * (HD + 1)
                            mm = pe.matmul(bank[4][64 * b:64 * b + T, g * w:(g + 1) * w], probsT[:, p % 2, g, 64 * b:64 * b + T],
                                           v_diag[:, (2 * p + b) % (2 * QI), g, :, :], start=True, stop=True)
                    mm.then_inc(o_made, 1)
                p = step - 4
                if 0 <= p < PAIRS:
                    pe.wait_ge(o_done, p + 1)
                    if p >= 1:
                        pe.wait_ge(oT_done, p)
                    for k in range(2):
                        mm = pe.transpose(bank[5][0:DH, k * P:k * P + QROWS], o_sb[:, p % 2, 6 * k:6 * k + 6, :], identity[0:QROWS, 0:QROWS])
                    mm.then_inc(oT_made, 1)
            pe.wait_ge(wo_in, 48)
            pe.wait_ge(sm_masked, PAIRS)
            for i in range(NT):
                pe.wait_ge(oT_done, min(PAIRS, -(-(i + 1) * P // (2 * T))))
                if i >= 2:
                    pe.wait_ge(res1, i - 1)
                for k in range(2):
                    mm = pe.matmul(bank[i % 2][:, 0:D], oT[:, k, i * P:(i + 1) * P], wout_sb[:, k, :], start=(k == 0), stop=(k == 1))
                mm.then_inc(wout_made, 1)
            pe.wait_ge(pT_done, PAIRS)
            for i in range(NT):
                pe.wait_ge(norm_done, 2 * NT + i + 1)
                if i >= 2:
                    pe.wait_ge(aT_done, NT + i - 1)
                for k in range(2):
                    mm = pe.transpose(bank[2 + i % 2][0:DH, k * P:(k + 1) * P], a[:, i, k * DH:(k + 1) * DH], identity[:])
                mm.then_inc(aT_made, 1)
            pe.wait_ge(o_done, PAIRS)
            for i in range(NT):
                pe.wait_ge(aT_done, NT + i + 1)
                for k in range(2):
                    mm = pe.matmul(bank[4][:, i * NE:(i + 1) * NE], aT[:, k, i * P:(i + 1) * P], wr_sb[:, k, :], start=(k == 0), stop=(k == 1))
            mm.then_inc(lg_made, 1)
            pe.wait_ge(tables, TABLES)
            pe.wait_ge(route, R_PICK2)
            for t in range(NT):
                terms = [(before, t, pick1, t)] + ([(prev_tile, t, pick1, t - 1)] if t else [])
                for n, (m, tt, pk, ts) in enumerate(terms):
                    pe.matmul(bank[5][:, t * NE:(t + 1) * NE], m[:, tt, :], pk[:, ts, :], start=(n == 0), stop=(n == len(terms) - 1))
            for t in range(NT):
                terms = [(before, t, pick2, t), (same, t, pick1, t)]
                if t:
                    terms += [(prev_tile, t, pick2, t - 1), (prev_tile, t, pick1, t - 1)]
                if t < NT - 1:
                    terms += [(next_tile, t, pick1, t + 1)]
                for n, (m, tt, pk, ts) in enumerate(terms):
                    mm = pe.matmul(bank[5][:, 128 + t * NE:128 + (t + 1) * NE], m[:, tt, :], pk[:, ts, :], start=(n == 0), stop=(n == len(terms) - 1))
            mm.then_inc(prio_made, 1)
            pe.wait_ge(route, R_SLOTBF)
            pe.wait_ge(oT_done, PAIRS)
            for t in range(NT):
                dst = bank_bf[6 + t // 8]
                mm = pe.transpose(dst[0:NE, (t % 8) * P:(t % 8 + 1) * P], slot_bf[:, t, :], identity_bf[:])
            mm.then_inc(slotT_made, 1)
            pe.wait_ge(res1, NT)
            for g in range(GROUPS):
                pe.wait_ge(dhi_done, 2 * g + 2)
                pe.wait_ge(dlo_done, 2 * g + 2)
                for k in range(2):
                    n = 2 * g + k
                    if g == 0:
                        pe.wait_ge(alo_done, NT)
                        pe.wait_ge(ahi_done, NT)
                        pe.wait_ge(twice_done, 2)
                    if n >= 4:
                        pe.wait_ge(einlo_done, n - 3)
                    m = 0
                    for t in (g, g + 1):
                        s = (2 * g + t - g) % 4
                        for w, r in ((a_hi, d_hi), (a_hi, d_lo), (a_lo, d_hi)):
                            mm = pe.matmul(bank[n % 4][:, 0:NE * CAP], w[:, t, k * P:(k + 1) * P], r[:, s, :, :],
                                           start=(m == 0), stop=(m == 5))
                            m += 1
                    mm.then_inc(disp_made, 1)

            def transpose_out(e):
                pe.wait_ge(eoT_done, 2 * e + 2)
                for r in range(2):
                    pe.wait_ge(comb_done, GP * (e + 1))
                    for gg in range(2):
                        rows = slice((2 * r + gg) * PS, (2 * r + gg + 1) * PS)
                        pe.transpose(bank[4 + r][0:PS, gg * D:gg * D + P], eoT[:, 0, rows], identity[:])
                        mm = pe.matmul(bank[4 + r][0:PS, gg * D + P:(gg + 1) * D], eoT[:, 1, rows], fold[:], start=True, stop=True)
                    mm.then_inc(eo_made, 1)

            def slots_bc(e, q):
                n = GP * e + q
                if e == 0 and q == 0:
                    pe.wait_ge(slotT_done, 2)
                if q >= 2:
                    pe.wait_ge(comb_done, n - 1)
                elif e >= 1:
                    pe.wait_ge(eolo_done, 2 * e)
                    pe.wait_ge(eohi_done, 2 * e)
                pe.matmul(bank[4 + q % 2][0:PS, 0:PTOK], pick[:, e, :], slotT[:, q * PTOK:(q + 1) * PTOK], start=True, stop=True).then_inc(bc_made, 1)

            def combine(e, q):
                pe.wait_ge(eohi_done, 2 * e + q // 2 + 1)
                pe.wait_ge(eolo_done, 2 * e + q // 2 + 1)
                pe.wait_ge(comb_done, GP * e + q + 1)
                for k in range(2):
                    n = 2 * (GP * e + q) + k
                    if n >= 2:
                        pe.wait_ge(y_done, n - 1)
                    pe.matmul(bank[6 + k][0:DH, 0:PTOK], eo_hi[:, q, k * DH:(k + 1) * DH], comb[:, e % 2, q, :], start=True, stop=False)
                    pe.matmul(bank[6 + k][0:DH, 0:PTOK], eo_lo[:, q, k * DH:(k + 1) * DH], comb[:, e % 2, q, :], start=False, stop=True).then_inc(y_made, 1)

            pe.wait_ge(einlo_done, 2 * GROUPS)
            pe.wait_ge(einhi_done, 2 * GROUPS)
            for e in range(NE):
                s = e % 2
                pe.wait_ge(wlo_done, 2 * e + 2)
                for m in range(FM):
                    n = FM * e + m
                    if n >= 2:
                        pe.wait_ge(hidlo_done, n - 1)
                    for i, (w, k, r) in enumerate(((wi_hi, 0, ein_hi), (wi_lo, 0, ein_hi), (wi_hi, 0, ein_lo), (wi_hi, 1, ein_tail), (wi_lo, 1, ein_tail))):
                        mm = pe.matmul(bank[m % 2][:, 0:SLOTS], w[:, s, k, m * P:(m + 1) * P], r[:, e, :], start=(i == 0), stop=(i == 4))
                    mm.then_inc(up_made, 1)
                    if e and m == 1:
                        transpose_out(e - 1)
                    if e and m in (3, 5):
                        combine(e - 1, (m - 3) // 2)
                if e:
                    pe.wait_ge(eoT_done, 2 * e)
                for m in range(FM):
                    pe.wait_ge(hidhi_done, FM * e + m + 1)
                    pe.wait_ge(hidlo_done, FM * e + m + 1)
                    def tail_columns():
                        return pe.matmul(bank[3][:, 0:SLOTS], wo_hi[:, s, m, P:2 * P], hid_hi[:, m, :], start=(m == 0), stop=(m == FM - 1))

                    if m == 0:
                        tail_columns()
                    for i, (w, r) in enumerate(((wo_hi, hid_hi), (wo_lo, hid_hi), (wo_hi, hid_lo))):
                        pe.matmul(bank[2][:, 0:SLOTS], w[:, s, m, 0:P], r[:, m, :], start=(m == 0 and i == 0), stop=(m == FM - 1 and i == 2))
                    mm = pe.matmul(bank[3][0:DT, 0:SLOTS], wo_hi[:, s, m, P:D], hid_lo[:, m, :], start=False, stop=False)
                    if m:
                        mm = tail_columns()
                    if e and m in (1, 3):
                        combine(e - 1, 2 + m // 2)
                    if m < GP:
                        slots_bc(e, m)
                mm.then_inc(down_made, 1)
            transpose_out(NE - 1)
            for q in range(GP):
                combine(NE - 1, q)
            for i in range(NT):
                need = 2 * GP * (NE - 1) + 2 * min(GP, -(-(i + 1) * P // PTOK))
                pe.wait_ge(y_done, need)
                if i >= 2:
                    pe.wait_ge(fin_done, i - 1)
                if i == 0:
                    pe.wait_ge(hidlo_done, FM * NE)
                for k in range(2):
                    mm = pe.transpose(bank[i % 2][:, k * DH:(k + 1) * DH], y_acc[:, k, i * P:(i + 1) * P], identity[0:DH, 0:DH])
                mm.then_inc(yt_made, 1)

        @block.vector
        def _(dve):
            def normalize(i, src, dst, n):
                dve.tensor_scalar(dst, src, moments[:, i, 0:1], rstd[:, i:i + 1], ALU.subtract, ALU.mult).then_inc(norm_done, 1)

            def statistics(tiles, n0):
                for n, i in enumerate(tiles):
                    dve.bn_stats(stats[:, i, :], h[:, i, :]).then_inc(st_done, 1)
                for n, i in enumerate(tiles):
                    dve.wait_ge(st_done, n0 + n + 1)
                    dve.bn_aggr(moments[:, i, :], stats[:, i, :]).then_inc(mo_done, 1)

            def patch_stats(t):
                dve.wait_ge(x_in[t], 16 * C_IN)
                for w in range(SIDE):
                    for f in range(2):
                        dve.bn_stats(pstats[:, t, w, f, :], xin[:, t, 24 * f:24 * f + 24, w, :]).then_inc(pstat_done, 1)
                    dve.wait_ge(pstat_done, 2 * (SIDE * t + w) + 2)
                    dve.bn_aggr(pmom[:, t, w, :], pstats[:, t, w, :, :]).then_inc(pmom_done, 1)

            def patch_norm(t):
                dve.wait_ge(prstd_done, 2 * t + 2)
                dve.wait_ge(pmom_done, SIDE * (t + 1))
                dve.wait_ge(pt_made, 2 * KJ * t)
                for w in range(SIDE):
                    dve.tensor_scalar(xn[:, w, :].rearrange("p (r e) -> p r e", e=PATCH), xin[:, t, :, w, :], pmom[:, t, w, 0:1], prstd[:, t, w:w + 1], ALU.subtract, ALU.mult).then_inc(pnorm_done, 1)

            def embedded(t):
                tiles = BATCHES[t]
                lo, hi, w = tiles[0], tiles[-1] + 1, len(tiles)
                for i in tiles:
                    dve.wait_ge(emb_made, i + 1)
                    dve.tensor_tensor(h[:, i, :], bank[4 + i % 4][:, 0:D], bl_bc[:], ALU.add).then_inc(emb_out, 1)
                dve.wait_ge(emb_out, hi)
                done = 2 * lo
                statistics(tiles, done)
                dve.wait_ge(rstd_done, 2 * t + 1)
                for i in tiles:
                    normalize(i, h[:, i, :], h[:, i, :], 0)
                dve.wait_ge(norm_done, done + w)
                dve.tensor_tensor(h[:, lo:hi, :], h[:, lo:hi, :], g2_bc[:, None, :].to_broadcast([P, w, D]), ALU.mult).then_inc(gain_done, 1)
                dve.wait_ge(gain_done, t + 1)
                dve.tensor_tensor(h[:, lo:hi, :], h[:, lo:hi, :], b2_bc[:, None, :].to_broadcast([P, w, D]), ALU.add).then_inc(h_done, 1)
                dve.wait_ge(h_done, t + 1)
                statistics(tiles, done + w)
                dve.wait_ge(rstd_done, 2 * t + 2)
                for i in tiles:
                    normalize(i, h[:, i, :], a[:, i, :], 0)

            def patch_out(u):
                src, dst, gain, bias = patch_unit(u)
                dve.wait_ge(pt_made, u + 1)
                dve.tensor_scalar(dst, src, gain, bias, ALU.mult, ALU.add).then_inc(pt_dve, 1)

            for i in (0, 1, 4):
                dve.memset(bank[i][:], 1.0).then_inc(bank_set, 1)
            patch_stats(0)
            patch_norm(0)
            dve.wait_ge(aff_in, 16 * 6)
            for u in range(1, 2 * KJ, 2):
                patch_out(u)
            patch_stats(1)
            patch_norm(1)
            for u in range(2 * KJ + 1, 4 * KJ, 2):
                patch_out(u)
            embedded(0)
            embedded(1)
            for i in range(NT):
                dve.wait_ge(v_made, i + 1)
                if i >= 3:
                    dve.wait_ge(v_stored[i % 3], 16 * (i // 3))
                dve.tensor_tensor(v_sb[:, i % 3, :], bank[4 + i % 2][:, 0:D], bv_bc[:], ALU.add).then_inc(v_out, 1)
            dve.wait_ge(bqk_in, 16 * 8)

            def query_out(n):
                q, g = n // HG, n % HG
                dve.wait_ge(qk_made, 2 * n + 1)
                if q >= 2:
                    dve.wait_ge(sc_made, QP * (q - 1))
                dve.tensor_scalar(qT[:, q % 2, g, :], bank[6][:, 0:CHUNK], bqk_pad[:, 0, g:g + 1], None, ALU.add).then_inc(q_out, 1)

            for n in range(HG):
                query_out(n)
            dve.wait_ge(masks, 8)
            for step in range(PAIRS + 3):
                p = step
                if p < PAIRS:
                    s = p % 2
                    dve.wait_ge(sc_made, p + 1)
                    if p >= 2:
                        dve.wait_ge(p_done, p - 1)
                    dve.tensor_tensor(sm[:, s, :, :], bank[s][0:QROWS, 0:HEADS * T].rearrange("p (h k) -> p h k", h=HEADS),
                                      causal[:, None, :].to_broadcast([QROWS, HEADS, T]), ALU.add).then_inc(sm_masked, 1)
                    dve.wait_ge(sm_masked, p + 1)
                    dve.tensor_reduce(smax[:, s, :], sm[:, s, :, :], AX.X, ALU.max).then_inc(sm_max, 1)
                    dve.wait_ge(sm_max, p + 1)
                    dve.tensor_tensor(sm[:, s, :, :], sm[:, s, :, :], smax[:, s, :, None].to_broadcast([QROWS, HEADS, T]), ALU.subtract).then_inc(sm_shift, 1)
                if step % QP < HG and step // QP + 1 < NQ:
                    query_out((step // QP + 1) * HG + step % QP)
                p = step - 3
                if 0 <= p < PAIRS:
                    s = p % 2
                    o = bank[4][0:QROWS, 0:HEADS * (HD + 1)].rearrange("p (h d) -> p h d", h=HEADS)
                    dve.wait_ge(o_made, p + 1)
                    dve.reciprocal(rsum[:, s, :], o[:, :, HD]).then_inc(rs_done, 1)
                    dve.wait_ge(rs_done, p + 1)
                    if p >= 2:
                        dve.wait_ge(oT_made, p - 1)
                    dve.tensor_tensor(o_sb[:, s, :, :], o[:, :, 0:HD], rsum[:, s, :, None].to_broadcast([QROWS, HEADS, HD]), ALU.mult).then_inc(o_done, 1)
            dve.wait_ge(wo_in, 48)
            for i in range(NT):
                dve.tensor_tensor(h[:, i, :], h[:, i, :], bout_bc[:], ALU.add).then_inc(gain_done, 1)
            for i in range(NT):
                dve.wait_ge(gain_done, 2 + i + 1)
                dve.wait_ge(wout_made, i + 1)
                dve.tensor_tensor(h[:, i, :], bank[i % 2][:, 0:D], h[:, i, :], ALU.add).then_inc(res1, 1)
            dve.wait_ge(res1, NT)
            statistics(range(NT), 2 * NT)
            dve.wait_ge(rstd_done, 5)
            dve.wait_ge(aT_made, NT)
            for i in range(NT):
                normalize(i, h[:, i, :], a[:, i, :], 0)
            for i in range(NT):
                dve.wait_ge(ahi_done, i + 1)
                dve.tensor_tensor(a_lo[:, i, 0:D], a[:, i, :], a_hi[:, i, 0:D].bitcast(F32), ALU.subtract).then_inc(alo_done, 1)
            count = [0]

            def link(ins):
                count[0] += 1
                ins.then_inc(route, 1)
                dve.wait_ge(route, count[0])

            def bc(ap):
                return ap[:, :, None].to_broadcast([P, NT, NE])

            exp_bc = expert_no[:, None, :].to_broadcast([P, NT, NE])
            dve.wait_ge(lg_made, 1)
            dve.wait_ge(tables, TABLES)
            link(dve.tensor_copy(lg[:], bank[4][:, 0:NT * NE].rearrange("p (t e) -> p t e", t=NT)))
            link(dve.tensor_reduce(top[:, 0, :], lg[:], AX.X, ALU.max))
            link(dve.tensor_tensor(lsh[:], lg[:], bc(top[:, 0, :]), ALU.subtract))
            assert count[0] == R_LSH
            link(dve.tensor_tensor(eq[:], lg[:], bc(top[:, 0, :]), ALU.is_equal))
            link(dve.tensor_tensor(eq[:], eq[:], exp_bc, ALU.mult))
            link(dve.tensor_reduce(first[:, 0, :], eq[:], AX.X, ALU.min))
            link(dve.tensor_tensor(pick1[:], exp_bc, bc(first[:, 0, :]), ALU.is_equal))
            link(dve.scalar_tensor_tensor(lg2[:], pick1[:], -3e38, lg[:], ALU.mult, ALU.add))
            link(dve.tensor_reduce(top[:, 1, :], lg2[:], AX.X, ALU.max))
            link(dve.tensor_tensor(eq[:], lg2[:], bc(top[:, 1, :]), ALU.is_equal))
            link(dve.tensor_tensor(eq[:], eq[:], exp_bc, ALU.mult))
            link(dve.tensor_reduce(first[:, 1, :], eq[:], AX.X, ALU.min))
            link(dve.tensor_tensor(pick2[:], exp_bc, bc(first[:, 1, :]), ALU.is_equal))
            assert count[0] == R_PICK2
            dve.wait_ge(ex_done, 1)
            link(dve.tensor_reduce(esum[:], ex[:], AX.X, ALU.add))
            link(dve.reciprocal(erec[:], esum[:]))
            link(dve.tensor_tensor(gate[:], ex[:], bc(erec[:]), ALU.mult))
            link(dve.tensor_copy(gate_hi[:], gate[:]))
            link(dve.tensor_tensor(gate_lo[:], gate[:], gate_hi[:].bitcast(F32), ALU.subtract))
            dve.wait_ge(prio_made, 1)
            link(dve.scalar_tensor_tensor(s1[:], bank[5][:, 0:NT * NE].rearrange("p (t e) -> p t e", t=NT), 1.0, pick1[:], ALU.add, ALU.mult))
            link(dve.scalar_tensor_tensor(s2[:], bank[5][:, 128:128 + NT * NE].rearrange("p (t e) -> p t e", t=NT), 1.0, pick2[:], ALU.add, ALU.mult))
            link(dve.tensor_tensor(s1[:], s1[:], s2[:], ALU.add))
            link(dve.scalar_tensor_tensor(slot[:], s1[:], 50.0, bc(parity[:]), ALU.min, ALU.add))
            link(dve.tensor_copy(slot_bf[:], slot[:]))
            assert count[0] == R_SLOTBF
            for n in range(2 * GROUPS):
                g = n // 2
                t = g + n % 2
                if n >= 4:
                    dve.wait_ge(disp_made, 2 * ((n - 4) // 2 + 1))
                    dve.wait_ge(dlo_done, n - 3)
                dve.tensor_tensor(d01[:, n % 4, :, :], slot[:, t, :, None].to_broadcast([P, NE, CAP]),
                                  slot_no[:, g % 2, None, :].to_broadcast([P, NE, CAP]), ALU.is_equal).then_inc(d01_done, 1)
                dve.wait_ge(d01_done, n + 1)
                dve.tensor_tensor(d_hi[:, n % 4, :, :], d01[:, n % 4, :, :],
                                  gate_hi[:, t, :, None].bitcast(F32).to_broadcast([P, NE, CAP]), ALU.mult).then_inc(dhi_done, 1)
                if n == 1:
                    dve.wait_ge(slotT_made, 1)
                    dve.tensor_copy(slotT[:, 0:8 * P], bank_bf[6][0:NE, :]).then_inc(slotT_done, 1)
                    dve.tensor_copy(slotT[:, 8 * P:], bank_bf[7][0:NE, 0:P]).then_inc(slotT_done, 1)
                if n >= 5 and n % 2:
                    ein_low(g - 2)
            ein_low(GROUPS - 2)
            ein_low(GROUPS - 1)

            def eo_low(e):
                for r in range(2):
                    dve.wait_ge(eohi_done, 2 * e + r + 1)
                    dve.tensor_tensor(eo_lo[:, 2 * r:2 * r + 2, :], bank[4 + r][0:PS, 0:2 * D].rearrange("p (g d) -> p g d", g=2),
                                      eo_hi[:, 2 * r:2 * r + 2, :].bitcast(F32), ALU.subtract).then_inc(eolo_done, 1)

            def add_y(e, q):
                for k in range(2):
                    n = 2 * (GP * e + q) + k
                    dve.wait_ge(y_made, n + 1)
                    dst = y_acc[:, k, q * PTOK:(q + 1) * PTOK]
                    if e == 0:
                        dve.tensor_copy(dst, bank[6 + k][0:DH, 0:PTOK]).then_inc(y_done, 1)
                    else:
                        dve.wait_ge(y_done, n + 1 - 2 * GP)
                        dve.tensor_tensor(dst, bank[6 + k][0:DH, 0:PTOK], dst, ALU.add).then_inc(y_done, 1)

            def slot_rows(e, q):
                n = GP * e + q
                dve.wait_ge(bc_made, n + 1)
                if e >= 2:
                    dve.wait_ge(y_made, 2 * GP * (e - 2) + 2 * q + 2)
                dve.tensor_scalar(comb[:, e % 2, q, :], bank[4 + q % 2][0:PS, 0:PTOK], slot_of_row[:], None, ALU.is_equal).then_inc(comb_done, 1)

            for e in range(NE):
                for m in range(FM):
                    dve.wait_ge(hidhi_done, FM * e + m + 1)
                    dve.scalar_tensor_tensor(hid_lo[:, m, :], bank[m % 2][:, 0:SLOTS], 0.0, hid_hi[:, m, :].bitcast(F32), ALU.max, ALU.subtract).then_inc(hidlo_done, 1)
                    if e and m == 1:
                        eo_low(e - 1)
                    if e and m in (3, 5):
                        add_y(e - 1, (m - 3) // 2)
                for q in range(GP):
                    if e and q in (1, 3):
                        add_y(e - 1, 2 + q // 2)
                    slot_rows(e, q)
            eo_low(NE - 1)
            for q in range(GP):
                add_y(NE - 1, q)
            for i in range(NT):
                dve.wait_ge(yt_made, i + 1)
                dve.tensor_tensor(a[:, i, :], bank[i % 2][:, 0:D], h[:, i, :], ALU.add).then_inc(fin_done, 1)


_NAMES = ["x", "L0_tok_ln1_g", "L0_tok_ln1_b", "L0_tok_Wl", "L0_tok_bl", "L0_tok_ln2_g", "L0_tok_ln2_b",
          "L0_attn_W_qkv", "L0_attn_b_qkv", "L0_attn_W_out", "L0_attn_b_out", "L0_ffn_w_router", "L0_ffn_wi", "L0_ffn_wo"]


def kernel(**inputs):
    import numpy as np
    import concourse.bacc as bacc
    from concourse.bass_utils import run_bass_kernel_spmd

    nc = bacc.Bacc("TRN2", target_bir_lowering=False, num_devices=1)
    arrays, args = {}, []
    for name in _NAMES:
        arrays[name] = np.ascontiguousarray(inputs[name])
        args.append(nc.dram_tensor(name, arrays[name].shape, F32, kind="ExternalInput").ap())
    out = nc.dram_tensor("out", (N, D), F32, kind="ExternalOutput").ap()
    build(nc, *args, out)
    r = run_bass_kernel_spmd(nc, [arrays], core_ids=[0])
    return r.results[0]["out"].reshape(B, T, D)
```

```python
from contextlib import ExitStack

import concourse.bass as bass
from concourse import mybir

ALU = mybir.AluOpType
ACT = mybir.ActivationFunctionType
AX = mybir.AxisListType
F32 = mybir.dt.float32
F32R = mybir.dt.float32r
BF16 = mybir.dt.bfloat16

P = 128
B, C_IN, IMG = 32, 3, 96
PATCH = 16
SIDE = IMG // PATCH
T = SIDE * SIDE
N = B * T
NT = N // P
D_PATCH = PATCH * PATCH * C_IN
KJ = D_PATCH // P
D = 192
DH = D // 2
DT = D - P
HEADS, HD = 12, 16
H6 = DH // HD
HG = HEADS // H6
H3 = 3
G3 = HEADS // H3
PAIRS = B // 2
QROWS = 64 + T
NE = 8
GROUPS = 8
S = N // GROUPS
CAP = max(int(2 * 1.25 * S / NE), 4)
SLOTS = GROUPS * CAP
FF = 768
FM = FF // P
GP = GROUPS // 2
PS = 2 * CAP
PTOK = 2 * S
SHIFT = P - (2 * P - S)
ROWS = B // 2 * SIDE
QI = 8
NQ = B // QI
CHUNK = QI * T
QP = QI // 2
EPS = 1e-5
NEG = -1e30
LG = 256
LATE = NQ // 4 * 3 * QP - 1
assert all((LATE + i - 4 + 1) * 2 * T >= (i + 1) * P for i in range(NT))
assert SHIFT == S - P and NT == GROUPS + 1 and ROWS == DH
TABLES = 16 + NT
R_LSH, R_PICK2, R_SLOTBF = 3, 13, 23


def build(nc, x, ln1_g, ln1_b, Wl, bl, ln2_g, ln2_b, W_qkv, b_qkv, W_out, b_out, w_router, wi, wo, out, taps=None):
    v_dram = nc.dram_tensor("v_scratch", (N, D), F32, kind="Internal").ap()
    with ExitStack() as ctx:
        def sb(name, shape, dt=F32, where=ctx):
            return where.enter_context(nc.sbuf_tensor(name, shape, dt))

        def sem(name):
            return ctx.enter_context(nc.semaphore(name))

        bank = [ctx.enter_context(nc.psum_tensor(f"bank{i}", [P, 512], F32)) for i in range(8)]
        bank_bf = {i: bank[i][:, :].bitcast(BF16) for i in (6, 7)}

        identity = sb("identity", [P, P])
        identity_bf = sb("identity_bf", [P, P], BF16)
        fold = sb("fold", [P, DT])
        sum_halves = sb("sum_halves", [2 * NE, NE, 2], F32R)
        minus_half = sb("minus_half", [P, NT])
        h = sb("h", [P, NT, D])
        a = sb("a", [P, NT, D])
        aT = sb("aT", [DH, 2, N])
        act_warm = sb("act_warm", [P, 1])
        stats = sb("stats", [P, NT, 6])
        moments = sb("moments", [P, NT, 2])
        rstd = sb("rstd", [P, NT])
        wr_sb = sb("wr_sb", [DH, 2, NE])
        wout_sb = sb("wout_sb", [DH, 2, D])
        bout_bc = sb("bout_bc", [P, D])
        oT = sb("oT", [DH, 2, N])
        y_acc = oT
        same = sb("same", [P, NT, P], BF16)
        before = sb("before", [P, NT, P], BF16)
        prev_tile = sb("prev_tile", [P, NT, P], BF16)
        next_tile = sb("next_tile", [P, NT, P], BF16)
        expert_no = sb("expert_no", [P, NE])
        slot_no = sb("slot_no", [P, 2, CAP])
        parity = sb("parity", [P, NT])
        slot_of_row = sb("slot_of_row", [PS, 1])
        second_row = sb("second_row", [PS, 1])
        pick = sb("pick", [NE, NE, PS], BF16)

        with ExitStack() as r1:
            xin = sb("xin", [ROWS, 2, C_IN * PATCH, SIDE, PATCH], where=r1)
            pT = sb("pT", [P, KJ, N], where=r1)
        wi_raw = sb("wi_raw", [P, 2, 2, FF])
        wo_raw = sb("wo_raw", [P, 2, FM, D])
        wi_hi = sb("wi_hi", [P, 2, 2, FF], F32R)
        wi_lo = sb("wi_lo", [P, 2, 2, FF], F32R)
        wo_hi = sb("wo_hi", [P, 2, FM, 2 * P], F32R)
        wo_lo = sb("wo_lo", [P, 2, FM, P], F32R)

        with ExitStack() as r2:
            wqkv_sb = sb("wqkv_sb", [DH, 2, 3 * D], where=r2)
            bqk_sb = sb("bqk_sb", [DH, 2, HG], where=r2)
            bv_bc = sb("bv_bc", [P, D], where=r2)
            v_sb = sb("v_sb", [P, 3, D], where=r2)
            qT = sb("qT", [DH, 2, HG, CHUNK], where=r2)
            k_tmp = sb("k_tmp", [DH, 3, CHUNK], where=r2)
            with ExitStack() as r5:
                ones = sb("ones", [P, NT, P], BF16, where=r5)
                row_ge = sb("row_ge", [P, NT, P], BF16, where=r5)
                col_ge = sb("col_ge", [P, NT, P], BF16, where=r5)
            k_diag = sb("k_diag", [DH, 2, HG, H6, CHUNK], where=r2)
            v_diag = sb("v_diag", [H3 * T, 2 * QI, G3, H3, HD + 1], where=r2)
            own_head = sb("own_head", [H3 * T, H3], where=r2)
            causal = sb("causal", [QROWS, T], where=r2)
            causal2 = sb("causal2", [QROWS, T], where=r2)
            head_rows = sb("head_rows", [DH, H6], where=r2)
            with ExitStack() as r4:
                xn = sb("xn", [ROWS, SIDE, D_PATCH], where=r4)
                wl_sb = sb("wl_sb", [P, 2, C_IN, D], where=r4)
                g1_sb = sb("g1_sb", [P, 2, C_IN], where=r4)
                b1_sb = sb("b1_sb", [P, 2, C_IN], where=r4)
                bl_bc = sb("bl_bc", [P, D], where=r4)
                g2_bc = sb("g2_bc", [P, D], where=r4)
                b2_bc = sb("b2_bc", [P, D], where=r4)
                pstats = sb("pstats", [ROWS, 2, SIDE, C_IN, 6], where=r4)
                pmom = sb("pmom", [ROWS, 2, SIDE, 2], where=r4)
                prstd = sb("prstd", [ROWS, 2, SIDE], where=r4)
                pshift = sb("pshift", [ROWS, 2, SIDE], where=r4)
            v_rep = sb("v_rep", [H3 * T, QI, D], where=r2)
            sm = sb("sm", [QROWS, 2, HEADS, T], where=r2)
            smax = sb("smax", [QROWS, 2, HEADS], where=r2)
            probs = sb("probs", [QROWS, 2, HEADS, T], where=r2)
            probsT = sb("probsT", [H3 * T, 2, G3, QROWS], where=r2)
            rsum = sb("rsum", [QROWS, 2, HEADS], where=r2)
            o_sb = sb("o_sb", [QROWS, 2, HEADS, HD], where=r2)
        lg = sb("lg", [P, NT, NE])
        lg2 = sb("lg2", [P, NT, NE])
        top = sb("top", [P, 2, NT])
        eq = sb("eq", [P, NT, NE])
        first = sb("first", [P, 2, NT])
        pick1 = sb("pick1", [P, NT, NE], BF16)
        pick2 = sb("pick2", [P, NT, NE], BF16)
        lsh = sb("lsh", [P, NT, NE])
        ex = sb("ex", [P, NT, NE])
        esum = sb("esum", [P, NT])
        erec = sb("erec", [P, NT])
        gate = sb("gate", [P, NT, NE])
        gate_split = sb("gate_split", [P, NT, 2 * NE], F32R)
        gate_rows = sb("gate_rows", [2 * NE, NE, SLOTS], F32R)
        gate_slot = sb("gate_slot", [PS, NE * GP])
        s1 = sb("s1", [P, NT, NE])
        s2 = sb("s2", [P, NT, NE])
        slot = sb("slot", [P, NT, NE])
        slot_bf = sb("slot_bf", [P, NT, NE], BF16)
        slotT = sb("slotT", [NE, N], BF16)
        ein_hi = sb("ein_hi", [P, NE, SLOTS], F32R)
        ein_lo = sb("ein_lo", [P, NE, SLOTS], F32R)
        ein_tail = sb("ein_tail", [P, NE, SLOTS], F32R)
        with ExitStack() as r3:
            a_split = sb("a_split", [P, NT, 3 * P], F32R, where=r3)
            d01 = sb("d01", [P, 4, NE, CAP], F32R, where=r3)
        hid_hi = sb("hid_hi", [P, FM, SLOTS], F32R)
        hid_lo = sb("hid_lo", [P, FM, SLOTS], F32R)
        comb = sb("comb", [PS, 2, GP, PTOK], F32R)
        eoT = sb("eoT", [P, 2, SLOTS])
        eo_hi = sb("eo_hi", [PS, GP, D], F32R)
        eo_lo = sb("eo_lo", [PS, GP, D], F32R)

        x_in = [[sem(f"x_in{t}_{c}") for c in range(C_IN)] for t in range(2)]
        wl_in, aff_in, wq_in, wo_in, bqk_in = sem("wl_in"), sem("aff_in"), sem("wq_in"), sem("wo_in"), sem("bqk_in")
        wi_in = [sem(f"wi_in{i}") for i in range(2)]
        consts, vones, tables, scratch = sem("consts"), sem("vones"), sem("tables"), sem("scratch")
        bank_set = sem("bank_set")
        pstat_done, pmom_done, prstd_done, pshift_done, pnorm_act, pnorm_dve = (sem(s) for s in ("pstat_done", "pmom_done", "prstd_done", "pshift_done", "pnorm_act", "pnorm_dve"))
        pt_made, pt_act, pt_dve = sem("pt_made"), sem("pt_act"), sem("pt_dve")
        emb_made, emb_out = sem("emb_made"), sem("emb_out")
        st_done, mo_done, var_done, rstd_done = sem("st_done"), sem("mo_done"), sem("var_done"), sem("rstd_done")
        centred, norm_done, gain_done = sem("centred"), sem("norm_done"), sem("gain_done")
        aT_made, aT_done = sem("aT_made"), sem("aT_done")
        v_made, v_out, v_stored, v_loaded, v_ready = sem("v_made"), sem("v_out"), [sem(f"v_stored{i}") for i in range(3)], [sem(f"v_loaded{i}") for i in range(2)], sem("v_ready")
        masks = sem("masks")
        qk_made, q_out, k_out, k_ready = sem("qk_made"), sem("q_out"), sem("k_out"), sem("k_ready")
        sc_made, sm_masked, sm_max, sm_shift, p_done = sem("sc_made"), sem("sm_masked"), sem("sm_max"), sem("sm_shift"), sem("p_done")
        pT_made, pT_done, o_made, rs_done, o_done, oT_made, oT_done = (sem(s) for s in ("pT_made", "pT_done", "o_made", "rs_done", "o_done", "oT_made", "oT_done"))
        wout_made, res1 = sem("wout_made"), sem("res1")
        lg_made, route, ex_done, prio_made, slotT_made, slotT_done, ahi_done, alo_done = (sem(s) for s in ("lg_made", "route", "ex_done", "prio_made", "slotT_made", "slotT_done", "ahi_done", "alo_done"))
        d01_done, disp_made, ein_act, ein_dve, gate_made, gate_done = (sem(s) for s in ("d01_done", "disp_made", "ein_act", "ein_dve", "gate_made", "gate_done"))
        whi_done, wlo_done = sem("whi_done"), sem("wlo_done")
        up_made, hidhi_done, hidlo_done, down_made, eoT_done = (sem(s) for s in ("up_made", "hidhi_done", "hidlo_done", "down_made", "eoT_done"))
        eo_made, eohi_done, eolo_done, bc_made, comb_done, y_made, y_done = (sem(s) for s in ("eo_made", "eohi_done", "eolo_done", "bc_made", "comb_done", "y_made", "y_done"))
        yt_made, fin_done, out_sent = sem("yt_made"), sem("fin_done"), sem("out_sent")

        BATCHES = [range(0, 4), range(4, NT)]
        LN_SETS = [("emb", t, BATCHES[t]) for t in range(2)]

        ctx.enter_context(nc.allow_non_contiguous_dma("row-sized runs"))
        block = ctx.enter_context(nc.Block())

        def patch_unit(u):
            t, w, j = u // (2 * KJ), u // KJ % 2, u % KJ
            src = bank[u % 4][:, 0:3 * ROWS].rearrange("p (w r) -> p w r", w=3)
            dst = pT[:, j, t * ROWS * SIDE:(t + 1) * ROWS * SIDE].rearrange("p (r w) -> p w r", w=SIDE)[:, 3 * w:3 * w + 3, :]
            gain, bias = (v[:, j % 2, j // 2:j // 2 + 1] for v in (g1_sb, b1_sb))
            return src, dst, gain, bias

        @block.sync
        def _(sp):
            xv = x.rearrange("(t b) c (h q) w -> t c b h (q w)", t=2, q=PATCH)
            for t in range(2):
                for c in range(C_IN):
                    sp.dma_start(xin[:, t, c * PATCH:(c + 1) * PATCH, :, :], xv[t, c]).then_inc(x_in[t][c], 16)
                if t == 0:
                    sp.dma_start(wl_sb[:], Wl.rearrange("(f n c) e -> n f c e", f=2, c=C_IN)).then_inc(wl_in, 16)
            sp.dma_start(wqkv_sb[:], W_qkv.rearrange("(k p) n -> p k n", k=2)).then_inc(wq_in, 16)
            sp.dma_start(wout_sb[:], W_out.rearrange("(k p) n -> p k n", k=2)).then_inc(wo_in, 16)
            sp.dma_start(wr_sb[:], w_router.rearrange("(k p) n -> p k n", k=2)).then_inc(wo_in, 16)
            sp.dma_start(bout_bc[:], b_out.rearrange("(o n) -> o n", o=1).to_broadcast([P, D])).then_inc(wo_in, 16)
            def store_values(tiles):
                for i in tiles:
                    sp.wait_ge(v_out, i + 1)
                    sp.dma_start(v_dram[i * P:(i + 1) * P, :], v_sb[:, i % 3, :]).then_inc(v_stored[i % 3], 16)

            def load_values(q):
                for i in range(-(-q * CHUNK // P), -(-(q + 1) * CHUNK // P)):
                    sp.wait_ge(v_stored[i % 3], 16 * (i // 3 + 1))
                if q >= 1:
                    sp.wait_ge(v_ready, q)
                vq = v_dram[q * CHUNK:(q + 1) * CHUNK, :].rearrange("(b k) d -> k b d", k=T)
                for r in range(H3):
                    sp.dma_start(v_rep[r * T:(r + 1) * T, :, :], vq).then_inc(v_loaded[q % 2], 16)

            store_values(range(3))
            load_values(0)
            store_values(range(3, NT))
            for q in range(1, NQ):
                load_values(q)
            sp.wait_ge(tables, TABLES)
            for e in range(NE):
                if e >= 2:
                    sp.wait_ge(wlo_done, 2 * (e - 1))
                sp.dma_start(wi_raw[:, e % 2, 0, :], wi[e, 0:P, :]).then_inc(wi_in[e % 2], 16)
                for r in range(2):
                    sp.dma_start(wi_raw[r * DT:(r + 1) * DT, e % 2, 1, :], wi[e, P:D, :]).then_inc(wi_in[e % 2], 16)
                sp.dma_start(wo_raw[:, e % 2, :, :], wo[e].rearrange("(m p) d -> p m d", m=FM)).then_inc(wi_in[e % 2], 16)
            for i in range(NT):
                sp.wait_ge(fin_done, i + 1)
                sp.dma_start(out[i * P:(i + 1) * P, :], a[:, i, :]).then_inc(out_sent, 16)
            sp.wait_ge(out_sent, 16 * NT)
            if taps:
                for nm, ap in taps.items():
                    src = locals_[nm]
                    sp.dma_start(ap, src[:]).then_inc(out_sent, 16)
                sp.wait_ge(out_sent, 16 * (NT + len(taps)))

        locals_ = dict(h=h, a=a, aT=aT, qT=qT, oT=oT, lg=lg, gate=gate, slot=slot, slotT=slotT, y_acc=y_acc, pT=pT, k_diag=k_diag, v_diag=v_diag, ein_hi=ein_hi, probs=probs, sm=sm)

        @block.gpsimd
        def _(gp):
            gp.memset(identity[:], 0.0).then_inc(consts, 1)
            gp.memset(identity_bf[:], 0.0).then_inc(consts, 1)
            gp.memset(minus_half[:], -0.5).then_inc(consts, 1)
            gp.memset(causal[:], 0.0).then_inc(consts, 1)
            gp.memset(causal2[:], 0.0).then_inc(consts, 1)
            gp.memset(head_rows[:], 1.0).then_inc(consts, 1)
            gp.memset(own_head[:], 1.0).then_inc(consts, 1)
            gp.memset(pick[:], 1.0).then_inc(consts, 1)
            gp.wait_ge(consts, 8)
            for m in (identity, identity_bf):
                gp.affine_select(out=m[:], in_=m[:], compare_op=ALU.not_equal, fill=1.0, base=0,
                                 pattern=[[-1, P]], channel_multiplier=1).then_inc(consts, 1)
            gp.wait_ge(consts, 10)
            gp.tensor_tensor(fold[:], identity[:, 0:DT], identity[:, DT:P], ALU.add).then_inc(consts, 1)
            gp.tensor_tensor(sum_halves[:], identity[0:2 * NE, 0:NE, None].to_broadcast([2 * NE, NE, 2]),
                             identity[0:2 * NE, NE:2 * NE, None].to_broadcast([2 * NE, NE, 2]), ALU.add).then_inc(consts, 1)
            def patch_rstd(t):
                for w in range(2):
                    part = slice(w * SIDE // 2, (w + 1) * SIDE // 2)
                    gp.wait_ge(pmom_done, SIDE * t + (w + 1) * SIDE // 2)
                    gp.tensor_scalar(prstd[:, t, part], pmom[:, t, part, 1], EPS, None, ALU.add).then_inc(prstd_done, 1)
                    if w == 1:
                        gp.tensor_scalar(pshift[:, t, part], pmom[:, t, part, 0], -1.0, None, ALU.mult).then_inc(pshift_done, 1)
                    gp.wait_ge(prstd_done, 2 * (2 * t + w) + 1)
                    gp.tensor_tensor(prstd[:, t, part], prstd[:, t, part], minus_half[0:ROWS, 0:SIDE // 2], ALU.pow).then_inc(prstd_done, 1)
                    if w == 1:
                        gp.wait_ge(prstd_done, 2 * (2 * t + w) + 2)
                        gp.wait_ge(pshift_done, 2 * t + 1)
                        gp.tensor_tensor(pshift[:, t, part], pshift[:, t, part], prstd[:, t, part], ALU.mult).then_inc(pshift_done, 1)
            patch_rstd(0)
            gp.affine_select(out=causal[:], in_=causal[:], compare_op=ALU.is_ge, fill=NEG, base=0,
                             pattern=[[-1, T]], channel_multiplier=1).then_inc(masks, 1)
            gp.affine_select(out=causal2[:], in_=causal2[:], compare_op=ALU.is_ge, fill=NEG, base=-64,
                             pattern=[[-1, T]], channel_multiplier=1).then_inc(masks, 1)
            gp.affine_select(out=own_head[:], in_=own_head[:], compare_op=ALU.is_ge, fill=0.0, base=0,
                             pattern=[[-T, H3]], channel_multiplier=1).then_inc(masks, 1)
            gp.affine_select(out=head_rows[:], in_=head_rows[:], compare_op=ALU.is_ge, fill=0.0, base=0,
                             pattern=[[-HD, H6]], channel_multiplier=1).then_inc(masks, 1)
            gp.wait_ge(masks, 4)
            gp.affine_select(out=causal2[:], in_=causal2[:], compare_op=ALU.is_ge, fill=0.0, base=-64,
                             pattern=[[0, T]], channel_multiplier=1).then_inc(masks, 1)
            gp.affine_select(out=own_head[:], in_=own_head[:], compare_op=ALU.is_ge, fill=0.0, base=T - 1,
                             pattern=[[T, H3]], channel_multiplier=-1).then_inc(masks, 1)
            gp.affine_select(out=head_rows[:], in_=head_rows[:], compare_op=ALU.is_ge, fill=0.0, base=HD - 1,
                             pattern=[[HD, H6]], channel_multiplier=-1).then_inc(masks, 1)
            gp.wait_ge(masks, 7)
            gp.tensor_tensor(causal[:], causal[:], causal2[:], ALU.add).then_inc(masks, 1)
            gp.memset(ones[:], 1.0).then_inc(scratch, 1)
            gp.wait_ge(scratch, 1)
            gp.affine_select(out=row_ge[:], in_=ones[:], compare_op=ALU.is_ge, fill=0.0, base=0,
                             pattern=[[-SHIFT, NT], [0, P]], channel_multiplier=1).then_inc(tables, 1)
            gp.affine_select(out=col_ge[:], in_=ones[:], compare_op=ALU.is_ge, fill=0.0, base=0,
                             pattern=[[-SHIFT, NT], [1, P]], channel_multiplier=0).then_inc(tables, 1)
            gp.affine_select(out=prev_tile[:], in_=ones[:], compare_op=ALU.is_ge, fill=0.0, base=SHIFT,
                             pattern=[[-SHIFT, NT], [0, P]], channel_multiplier=1).then_inc(tables, 1)
            gp.affine_select(out=next_tile[:], in_=ones[:], compare_op=ALU.is_gt, fill=0.0, base=SHIFT,
                             pattern=[[SHIFT, NT], [0, P]], channel_multiplier=-1).then_inc(tables, 1)
            gp.affine_select(out=pick[:], in_=pick[:], compare_op=ALU.is_equal, fill=0.0, base=0,
                             pattern=[[-1, NE], [0, PS]], channel_multiplier=1).then_inc(tables, 1)
            gp.iota(expert_no[:], pattern=[[1, NE]], base=-NE, channel_multiplier=0, allow_small_or_imprecise_dtypes=True).then_inc(tables, 1)
            gp.iota(slot_no[:], pattern=[[64, 2], [1, CAP]], base=1, channel_multiplier=0, allow_small_or_imprecise_dtypes=True).then_inc(tables, 1)
            gp.iota(slot_of_row[:], pattern=[[0, 1]], base=1, channel_multiplier=1, allow_small_or_imprecise_dtypes=True).then_inc(tables, 1)
            gp.memset(second_row[:], 64.0 - CAP).then_inc(tables, 1)
            gp.wait_ge(tables, 9)
            gp.tensor_tensor(ones[:], row_ge[:], col_ge[:], ALU.subtract).then_inc(tables, 1)
            gp.affine_select(out=prev_tile[:], in_=prev_tile[:], compare_op=ALU.is_gt, fill=0.0, base=0,
                             pattern=[[SHIFT, NT], [-1, P]], channel_multiplier=0).then_inc(tables, 1)
            gp.affine_select(out=next_tile[:], in_=next_tile[:], compare_op=ALU.is_ge, fill=0.0, base=0,
                             pattern=[[-SHIFT, NT], [1, P]], channel_multiplier=0).then_inc(tables, 1)
            gp.tensor_copy(parity[:], row_ge[:, :, 0]).then_inc(tables, 1)
            gp.affine_select(out=second_row[:], in_=second_row[:], compare_op=ALU.is_ge, fill=0.0, base=-CAP,
                             pattern=[[0, 1]], channel_multiplier=1).then_inc(tables, 1)
            patch_rstd(1)
            gp.wait_ge(tables, 14)
            gp.tensor_tensor(col_ge[:], ones[:], ones[:], ALU.mult).then_inc(scratch, 1)
            gp.wait_ge(scratch, 2)
            gp.tensor_scalar(same[:], col_ge[:], -1.0, 1.0, ALU.mult, ALU.add).then_inc(scratch, 1)
            gp.wait_ge(scratch, 3)
            gp.affine_select(out=before[:], in_=same[:], compare_op=ALU.is_gt, fill=0.0, base=0,
                             pattern=[[0, NT], [1, P]], channel_multiplier=-1).then_inc(tables, 1)
            gp.tensor_tensor(slot_of_row[:], slot_of_row[:], second_row[:], ALU.add).then_inc(tables, 1)
            for t in range(NT):
                scale, off = (64.0, 0.0) if t % 2 else (-64.0, 64.0)
                gp.tensor_scalar(parity[:, t:t + 1], parity[:, t:t + 1], scale, off, ALU.mult, ALU.add).then_inc(tables, 1)

            for n in range(4):
                tiles = BATCHES[n // 2]
                lo, hi = tiles[0], tiles[-1] + 1
                gp.wait_ge(mo_done, [4, 8, 13, 18][n])
                gp.tensor_scalar(rstd[:, lo:hi], moments[:, lo:hi, 1], EPS, None, ALU.add).then_inc(var_done, 1)
                gp.wait_ge(var_done, n + 1)
                gp.tensor_tensor(rstd[:, lo:hi], rstd[:, lo:hi], minus_half[:, lo:hi], ALU.pow).then_inc(rstd_done, 1)
                if n == 1:
                    for b in range(2 * QI):
                        gp.tensor_copy(v_diag[:, b, :, :, HD], own_head[:, None, :].to_broadcast([H3 * T, G3, H3])).then_inc(vones, 1)
            for q in range(NQ):
                if q >= 2:
                    gp.wait_ge(sc_made, QP * (q - 1))
                for g in range(HG):
                    n = q * HG + g
                    gp.wait_ge(k_out, n + 1)
                    gp.tensor_tensor(k_diag[:, q % 2, g, :, :], k_tmp[:, n % 3, None, :].to_broadcast([DH, H6, CHUNK]),
                                     head_rows[:, :, None].to_broadcast([DH, H6, CHUNK]), ALU.mult).then_inc(k_ready, 1)
                if q >= 2:
                    gp.wait_ge(o_made, QP * (q - 1))
                gp.wait_ge(v_loaded[q % 2], 16 * H3 * (q // 2 + 1))
                for b in range(QI):
                    ins = gp.tensor_tensor(v_diag[:, q % 2 * QI + b, :, :, 0:HD],
                                           v_rep[:, b, :].rearrange("p (g h d) -> p g h d", g=G3, h=H3),
                                           own_head[:, None, :, None].to_broadcast([H3 * T, G3, H3, HD]), ALU.mult)
                ins.then_inc(v_ready, 1)
            def split_up(e):
                s = e % 2
                gp.wait_ge(whi_done, 2 * e + 1)
                gp.tensor_tensor(wi_lo[:, s, :, :], wi_raw[:, s, :, :], wi_hi[:, s, :, :].bitcast(F32), ALU.subtract).then_inc(wlo_done, 1)

            def split_down(e):
                s = e % 2
                gp.wait_ge(whi_done, 2 * e + 2)
                gp.tensor_tensor(wo_lo[:, s, :, :], wo_raw[:, s, :, 0:P], wo_hi[:, s, :, 0:P].bitcast(F32), ALU.subtract)
                gp.tensor_tensor(wo_hi[:, s, :, D:2 * P], wo_raw[:, s, :, P:D], wo_hi[:, s, :, P:D].bitcast(F32), ALU.subtract).then_inc(wlo_done, 1)

            for i in range(NT):
                gp.wait_ge(mo_done, 2 * NT + i + 1)
                gp.tensor_scalar(rstd[:, i:i + 1], moments[:, i, 1:2], EPS, None, ALU.add).then_inc(var_done, 1)
                gp.wait_ge(var_done, 4 + i + 1)
                gp.tensor_tensor(rstd[:, i:i + 1], rstd[:, i:i + 1], minus_half[:, i:i + 1], ALU.pow).then_inc(rstd_done, 1)
                if i == 1:
                    split_up(0)
                if i == 2:
                    split_down(0)
                if i == 4:
                    split_up(1)
            for r in range(3):
                gp.wait_ge(ahi_done, r + 1)
                part = slice(3 * r, 3 * r + 3)
                gp.tensor_tensor(a_split[:, part, D:2 * P], a[:, part, P:D], a_split[:, part, P:D].bitcast(F32), ALU.subtract)
                gp.tensor_tensor(a_split[:, part, 2 * P:3 * P], a[:, part, 0:P], a_split[:, part, 0:P].bitcast(F32), ALU.subtract).then_inc(alo_done, 1)
            for e in range(1, NE):
                split_down(e)
                if e + 1 < NE:
                    split_up(e + 1)

        @block.scalar
        def _(act):
            act.dma_start(g1_sb[:], ln1_g.rearrange("(f n c) -> n f c", f=2, c=C_IN)).then_inc(aff_in, 16)
            act.dma_start(b1_sb[:], ln1_b.rearrange("(f n c) -> n f c", f=2, c=C_IN)).then_inc(aff_in, 16)
            for dst, src in ((bl_bc, bl), (g2_bc, ln2_g), (b2_bc, ln2_b), (bv_bc, b_qkv[2 * D:3 * D])):
                act.dma_start(dst[:], src.rearrange("(o n) -> o n", o=1).to_broadcast([P, D])).then_inc(aff_in, 16)
            def patch_norm_act(t):
                act.wait_ge(pshift_done, 2 * t + 2)
                if t:
                    act.wait_ge(pt_made, 2 * KJ * t)
                for w in range(SIDE // 2, SIDE):
                    act.activation(xn[:, w, :].rearrange("p (r e) -> p r e", e=PATCH), xin[:, t, :, w, :], ACT.Identity,
                                   bias=pshift[:, t, w:w + 1], scale=prstd[:, t, w:w + 1]).then_inc(pnorm_act, 1)

            def patches_out(t, w):
                for u in range(KJ * (2 * t + w), KJ * (2 * t + w + 1), 2):
                    src, dst, gain, bias = patch_unit(u)
                    act.wait_ge(pt_made, u + 1)
                    act.activation(dst, src, ACT.Identity, bias=bias, scale=gain).then_inc(pt_act, 1)

            act.wait_ge(consts, 8)
            act.activation(act_warm[:], minus_half[:, 0:1], ACT.Identity)
            for i in range(2):
                act.dma_start(bqk_sb[:, i, :], b_qkv[i * D:(i + 1) * D].rearrange("(g p) -> p g", g=HG)).then_inc(bqk_in, 16)
            act.wait_ge(aff_in, 16 * 6)
            patch_norm_act(0)
            patches_out(0, 0)
            patches_out(0, 1)
            patch_norm_act(1)
            patches_out(1, 0)
            patches_out(1, 1)
            def transposed_out(i):
                act.wait_ge(aT_made, i + 1)
                act.activation(aT[:, :, i * P:(i + 1) * P], bank[6 + i % 2][0:DH, 0:2 * P].rearrange("p (k n) -> p k n", k=2),
                               ACT.Copy).then_inc(aT_done, 1)
            for i in BATCHES[0]:
                transposed_out(i)
            act.wait_ge(bqk_in, 32)

            def key_out(n):
                act.wait_ge(qk_made, 2 * n + 2)
                if n >= 3:
                    act.wait_ge(k_ready, n - 2)
                act.activation(k_tmp[:, n % 3, :], bank[7][0:DH, 0:CHUNK], ACT.Identity,
                               bias=bqk_sb[:, 1, n % HG:n % HG + 1]).then_inc(k_out, 1)

            def round_up_weights(e):
                s = e % 2
                act.wait_ge(wi_in[s], 16 * 4 * (e // 2 + 1))
                if e >= 2:
                    act.wait_ge(up_made, FM * (e - 1))
                act.activation(wi_hi[:, s, :, :], wi_raw[:, s, :, :], ACT.Copy).then_inc(whi_done, 1)

            def round_down_weights(e):
                s = e % 2
                if e >= 2:
                    act.wait_ge(down_made, e - 1)
                act.activation(wo_hi[:, s, :, 0:D], wo_raw[:, s, :, :], ACT.Copy).then_inc(whi_done, 1)

            def late_transposed(i):
                act.wait_ge(aT_made, NT + i + 1)
                act.activation(aT[:, :, i * P:(i + 1) * P], bank[7][0:DH, 0:2 * P].rearrange("p (k n) -> p k n", k=2), ACT.Copy).then_inc(aT_done, 1)

            for n in range(HG):
                key_out(n)
            for i in BATCHES[1]:
                transposed_out(i)
            for step in range(PAIRS + 4):
                p = step - 1
                if 0 <= p < PAIRS:
                    act.wait_ge(sm_shift, p + 1)
                    if p >= 2:
                        act.wait_ge(pT_made, p - 1)
                    act.activation(probs[:, p % 2, :, :], sm[:, p % 2, :, :], ACT.Exp, scale=HD ** -0.5).then_inc(p_done, 1)
                p = step - 2
                if 0 <= p < PAIRS:
                    act.wait_ge(pT_made, p + 1)
                    if p >= 2:
                        act.wait_ge(o_made, p - 1)
                    act.activation(probsT[:, p % 2, :, :], bank[2 + p % 2][0:H3 * T, 0:G3 * QROWS].rearrange("p (g q) -> p g q", g=G3),
                                   ACT.Copy).then_inc(pT_done, 1)
                p = step - 4
                if 0 <= p < PAIRS:
                    act.wait_ge(oT_made, p + 1)
                    src = bank[5][0:DH, 0:256].rearrange("p (k b q) -> p k b q", k=2, b=2)[:, :, :, 0:T]
                    act.activation(oT[:, :, p * 2 * T:(p + 1) * 2 * T].rearrange("p k (b q) -> p k b q", b=2), src,
                                   ACT.Copy).then_inc(oT_done, 1)
                if step % QP < HG and step // QP + 1 < NQ:
                    key_out((step // QP + 1) * HG + step % QP)
                if 0 <= step - LATE - 1 < NT:
                    late_transposed(step - LATE - 1)
                if step == LATE + 1:
                    round_up_weights(0)
                if step == LATE + 2:
                    round_down_weights(0)
                if step == LATE + 4:
                    round_up_weights(1)
            late_transposed(NT - 1)
            act.wait_ge(oT_made, PAIRS)
            for r in range(3):
                act.wait_ge(norm_done, 2 * NT + 3 * r + 3)
                act.activation(a_split[:, 3 * r:3 * r + 3, 0:D], a[:, 3 * r:3 * r + 3, :], ACT.Copy).then_inc(ahi_done, 1)
            act.wait_ge(route, R_LSH)
            act.activation(ex[:], lsh[:], ACT.Exp).then_inc(ex_done, 1)
            for g in range(GROUPS):
                for k, dst in ((0, ein_hi), (1, ein_lo), (3, gate_rows)):
                    act.wait_ge(disp_made, 4 * g + k + 1)
                    rows = 2 * NE if k == 3 else P
                    act.activation(dst[:, :, g * CAP:(g + 1) * CAP], bank[4 * (g % 2) + k][0:rows, 0:NE * CAP].rearrange("p (e c) -> p e c", e=NE),
                                   ACT.Copy).then_inc(ein_act, 1)

            def eo_high(e):
                for r in range(2):
                    act.wait_ge(eo_made, 2 * e + r + 1)
                    if e >= 1:
                        act.wait_ge(y_made, 2 * GP * e)
                    if e == 0 and r == 0:
                        act.wait_ge(gate_done, 1)
                    for q in (2 * r, 2 * r + 1):
                        act.activation(eo_hi[:, q, :], bank[4 + r][0:PS, q % 2 * D:(q % 2 + 1) * D], ACT.Copy,
                                       scale=gate_slot[:, GP * e + q:GP * e + q + 1]).then_inc(eohi_done, 1)

            for e in range(NE):
                for m in range(FM):
                    act.wait_ge(up_made, FM * e + m + 1)
                    if e >= 1:
                        act.wait_ge(down_made, e)
                    act.activation(hid_hi[:, m, :], bank[m % 2][:, 0:SLOTS], ACT.Relu).then_inc(hidhi_done, 1)
                    if m == 1 and e >= 1:
                        eo_high(e - 1)
                if e + 1 < NE:
                    round_down_weights(e + 1)
                if e + 2 < NE:
                    round_up_weights(e + 2)
                act.wait_ge(down_made, e + 1)
                if e >= 1:
                    act.wait_ge(eo_made, 2 * e)
                for k in range(2):
                    act.activation(eoT[:, k, :], bank[2 + k][:, 0:SLOTS], ACT.Copy).then_inc(eoT_done, 1)
            eo_high(NE - 1)

        @block.tensor
        def _(pe):
            pe.wait_ge(consts, 12)
            pe.wait_ge(bank_set, 3)

            def embed(i):
                for j in range(KJ):
                    mm = pe.matmul(bank[(4 + i) % 8][:, 0:D], pT[:, j, i * P:(i + 1) * P], wl_sb[:, j % 2, j // 2, :],
                                   start=(j == 0), stop=(j == KJ - 1))
                mm.then_inc(emb_made, 1)

            for t in range(2):
                for v in range(2 * KJ):
                    u = 2 * KJ * t + v
                    j, w = v % KJ, v // KJ
                    if j == 0:
                        pe.wait_ge((pnorm_dve, pnorm_act)[w], SIDE // 2 * (t + 1))
                    if u >= 4:
                        pe.wait_ge(pt_act if u % 2 == 0 else pt_dve, (u - 4) // 2 + 1)
                    for k in range(3):
                        src = xn[:, 3 * w + k, j * P:(j + 1) * P]
                        mm = pe.transpose(bank[u % 4][:, k * ROWS:(k + 1) * ROWS], src, identity[0:ROWS, 0:ROWS])
                    mm.then_inc(pt_made, 1)
                pe.wait_ge(pt_act, KJ * (t + 1))
                pe.wait_ge(pt_dve, KJ * (t + 1))
                pe.wait_ge(wl_in, 16)
                for i in BATCHES[t]:
                    if i >= 8:
                        pe.wait_ge(emb_out, i - 7)
                    embed(i)

            def transpose_norm(i):
                pe.wait_ge(norm_done, [*range(4 + 1, 8 + 1), *range(13 + 1, 18 + 1)][i])
                if i >= 2:
                    pe.wait_ge(aT_done, i - 1)
                if i == 4:
                    pe.wait_ge(q_out, HG)
                    pe.wait_ge(k_out, HG)
                for k in range(2):
                    mm = pe.transpose(bank[6 + i % 2][0:DH, k * P:(k + 1) * P], a[:, i, k * DH:(k + 1) * DH], identity[:])
                mm.then_inc(aT_made, 1)

            def values(i):
                pe.wait_ge(aT_done, i + 1)
                if i == 0:
                    pe.wait_ge(wq_in, 16)
                if i >= 2:
                    pe.wait_ge(v_out, i - 1)
                for k in range(2):
                    mm = pe.matmul(bank[4 + i % 2][:, 0:D], aT[:, k, i * P:(i + 1) * P], wqkv_sb[:, k, 2 * D:3 * D], start=(k == 0), stop=(k == 1))
                mm.then_inc(v_made, 1)

            def project(n):
                q, g = n // HG, n % HG
                for i in range(2):
                    if n == 0:
                        pe.wait_ge(aT_done, len(BATCHES[0]))
                    else:
                        pe.wait_ge(k_out if i else q_out, n)
                    if n == HG:
                        pe.wait_ge(aT_done, NT)
                    for k in range(2):
                        mm = pe.matmul(bank[6 + i][0:DH, 0:CHUNK], wqkv_sb[:, k, i * D + g * DH:i * D + (g + 1) * DH],
                                       aT[:, k, q * CHUNK:(q + 1) * CHUNK], start=(k == 0), stop=(k == 1))
                    mm.then_inc(qk_made, 1)

            for i in BATCHES[0]:
                transpose_norm(i)
            pe.wait_ge(emb_out, NT)
            for i in BATCHES[0]:
                values(i)
            def late_project(i):
                if i == 0:
                    pe.wait_ge(wo_in, 48)
                    pe.wait_ge(q_out, HG * NQ)
                    pe.wait_ge(k_out, HG * NQ)
                pe.wait_ge(oT_done, min(PAIRS, -(-(i + 1) * P // (2 * T))))
                if i:
                    pe.wait_ge(res1, i)
                for k in range(2):
                    mm = pe.matmul(bank[6][:, 0:D], oT[:, k, i * P:(i + 1) * P], wout_sb[:, k, :], start=(k == 0), stop=(k == 1))
                mm.then_inc(wout_made, 1)

            def late_transpose(i):
                pe.wait_ge(norm_done, 2 * NT + i + 1)
                if i:
                    pe.wait_ge(aT_done, NT + i)
                for k in range(2):
                    mm = pe.transpose(bank[7][0:DH, k * P:(k + 1) * P], a[:, i, k * DH:(k + 1) * DH], identity[:])
                mm.then_inc(aT_made, 1)

            def logits(i):
                pe.wait_ge(aT_done, NT + i + 1)
                for k in range(2):
                    mm = pe.matmul(bank[7][:, LG + i * NE:LG + (i + 1) * NE], aT[:, k, i * P:(i + 1) * P], wr_sb[:, k, :], start=(k == 0), stop=(k == 1))
                mm.then_inc(lg_made, 1)

            for n in range(HG):
                project(n)
            for i in BATCHES[1]:
                transpose_norm(i)
            for i in BATCHES[1]:
                values(i)
            for step in range(PAIRS + 4):
                p = step
                if p < PAIRS:
                    if p % QP == 0:
                        pe.wait_ge(q_out, HG * (p // QP + 1))
                        pe.wait_ge(k_ready, HG * (p // QP + 1))
                    if p >= 2:
                        pe.wait_ge(sm_masked, p - 1)
                    for b in range(2):
                        tok = (2 * p + b) % QI * T
                        s = p // QP % 2
                        for g in range(HG):
                            mm = pe.matmul(bank[p % 2][64 * b:64 * b + T, g * H6 * T:(g + 1) * H6 * T], qT[:, s, g, tok:tok + T],
                                           k_diag[:, s, g, :, tok:tok + T], start=True, stop=True)
                    mm.then_inc(sc_made, 1)
                if step % QP < HG and step // QP + 1 < NQ:
                    project((step // QP + 1) * HG + step % QP)
                p = step - 2
                if 0 <= p < PAIRS:
                    pe.wait_ge(p_done, p + 1)
                    if p >= 2:
                        pe.wait_ge(pT_done, p - 1)
                    for g in range(G3):
                        mm = pe.transpose(bank[2 + p % 2][0:H3 * T, g * QROWS:(g + 1) * QROWS], probs[:, p % 2, H3 * g:H3 * g + H3, :],
                                          identity[0:QROWS, 0:QROWS])
                    mm.then_inc(pT_made, 1)
                p = step - 3
                if 0 <= p < PAIRS:
                    pe.wait_ge(pT_done, p + 1)
                    if p % QP == 0:
                        pe.wait_ge(v_ready, p // QP + 1)
                    if p == 0:
                        pe.wait_ge(v_out, NT)
                        pe.wait_ge(vones, 2 * QI)
                    if p >= 1:
                        pe.wait_ge(o_done, p)
                    for b in range(2):
                        for g in range(G3):
                            w = H3 * (HD + 1)
                            mm = pe.matmul(bank[4][64 * b:64 * b + T, g * w:(g + 1) * w], probsT[:, p % 2, g, 64 * b:64 * b + T],
                                           v_diag[:, (2 * p + b) % (2 * QI), g, :, :], start=True, stop=True)
                    mm.then_inc(o_made, 1)
                p = step - 4
                if 0 <= p < PAIRS:
                    pe.wait_ge(o_done, p + 1)
                    if p >= 1:
                        pe.wait_ge(oT_done, p)
                    for k in range(2):
                        mm = pe.transpose(bank[5][0:DH, k * P:k * P + QROWS], o_sb[:, p % 2, 6 * k:6 * k + 6, :], identity[0:QROWS, 0:QROWS])
                    mm.then_inc(oT_made, 1)
                if step >= LATE:
                    late_project(step - LATE)
                if step >= LATE + 2:
                    logits(step - LATE - 2)
                if step >= LATE + 1:
                    late_transpose(step - LATE - 1)
            logits(NT - 2)
            late_transpose(NT - 1)
            logits(NT - 1)
            pe.wait_ge(tables, TABLES)
            pe.wait_ge(res1, NT)
            pe.wait_ge(route, R_PICK2)
            for t in range(NT):
                terms = [(before, t, pick1, t)] + ([(prev_tile, t, pick1, t - 1)] if t else [])
                for n, (m, tt, pk, ts) in enumerate(terms):
                    pe.matmul(bank[6][:, t * NE:(t + 1) * NE], m[:, tt, :], pk[:, ts, :], start=(n == 0), stop=(n == len(terms) - 1))
            for t in range(NT):
                terms = [(before, t, pick2, t), (same, t, pick1, t)]
                if t:
                    terms += [(prev_tile, t, pick2, t - 1), (prev_tile, t, pick1, t - 1)]
                if t < NT - 1:
                    terms += [(next_tile, t, pick1, t + 1)]
                for n, (m, tt, pk, ts) in enumerate(terms):
                    mm = pe.matmul(bank[6][:, 128 + t * NE:128 + (t + 1) * NE], m[:, tt, :], pk[:, ts, :], start=(n == 0), stop=(n == len(terms) - 1))
            mm.then_inc(prio_made, 1)
            pe.wait_ge(route, R_SLOTBF)
            pe.wait_ge(oT_done, PAIRS)
            for t in range(NT):
                dst = bank_bf[7 - t // 8]
                mm = pe.transpose(dst[0:NE, (t % 8) * P:(t % 8 + 1) * P], slot_bf[:, t, :], identity_bf[:])
            mm.then_inc(slotT_made, 1)
            for g in range(GROUPS):
                pe.wait_ge(d01_done, 2 * g + 2)
                if g == 0:
                    pe.wait_ge(alo_done, 3)
                    pe.wait_ge(ahi_done, 3)
                if g == 1:
                    pe.wait_ge(slotT_done, 2)
                if g >= 2:
                    pe.wait_ge(ein_act, 3 * (g - 1))
                    pe.wait_ge(ein_dve, g - 1)
                for k, (w, c0, m) in enumerate(((a_split, 0, P), (a_split, 2 * P, P), (a_split, P, P), (gate_split, 0, 2 * NE))):
                    for t in (g, g + 1):
                        mm = pe.matmul(bank[4 * (g % 2) + k][0:m, 0:NE * CAP], w[:, t, c0:c0 + m], d01[:, (2 * g + t - g) % 4, :, :],
                                       start=(t == g), stop=(t == g + 1))
                    mm.then_inc(disp_made, 1)

            def gates_to_slots(q):
                for e in range(NE):
                    n = 2 * (GP * e + q)
                    mm = pe.matmul(bank[6][0:PS, n:n + 2], gate_rows[:, e, q * PS:(q + 1) * PS], sum_halves[:, e, :], start=True, stop=True)
                mm.then_inc(gate_made, 1)

            def transpose_out(e):
                pe.wait_ge(eoT_done, 2 * e + 2)
                for r in range(2):
                    pe.wait_ge(comb_done, GP * (e + 1))
                    for gg in range(2):
                        rows = slice((2 * r + gg) * PS, (2 * r + gg + 1) * PS)
                        pe.transpose(bank[4 + r][0:PS, gg * D:gg * D + P], eoT[:, 0, rows], identity[:])
                        mm = pe.matmul(bank[4 + r][0:PS, gg * D + P:(gg + 1) * D], eoT[:, 1, rows], fold[:], start=True, stop=True)
                    mm.then_inc(eo_made, 1)

            def slots_bc(e, q):
                n = GP * e + q
                if e == 0 and q == 0:
                    pe.wait_ge(slotT_done, 2)
                if q >= 2:
                    pe.wait_ge(comb_done, n - 1)
                elif e >= 1:
                    pe.wait_ge(eolo_done, GP * e)
                    pe.wait_ge(eohi_done, GP * e)
                pe.matmul(bank[4 + q % 2][0:PS, 0:PTOK], pick[:, e, :], slotT[:, q * PTOK:(q + 1) * PTOK], start=True, stop=True).then_inc(bc_made, 1)

            def combine(e, q):
                pe.wait_ge(eohi_done, GP * e + q + 1)
                pe.wait_ge(eolo_done, GP * e + q + 1)
                pe.wait_ge(comb_done, GP * e + q + 1)
                for k in range(2):
                    n = 2 * (GP * e + q) + k
                    if n >= 2:
                        pe.wait_ge(y_done, n - 1)
                    elif k == 0:
                        pe.wait_ge(gate_done, 1)
                    pe.matmul(bank[6 + k][0:DH, 0:PTOK], eo_hi[:, q, k * DH:(k + 1) * DH], comb[:, e % 2, q, :], start=True, stop=False)
                    pe.matmul(bank[6 + k][0:DH, 0:PTOK], eo_lo[:, q, k * DH:(k + 1) * DH], comb[:, e % 2, q, :], start=False, stop=True).then_inc(y_made, 1)

            pe.wait_ge(ein_act, 3 * GROUPS)
            pe.wait_ge(ein_dve, GROUPS)
            for e in range(NE):
                s = e % 2
                pe.wait_ge(wlo_done, 2 * e + 2)
                for m in range(FM):
                    n = FM * e + m
                    if n >= 2:
                        pe.wait_ge(hidlo_done, n - 1)
                    for i, (w, k, r) in enumerate(((wi_hi, 0, ein_hi), (wi_lo, 0, ein_hi), (wi_hi, 0, ein_lo), (wi_hi, 1, ein_tail), (wi_lo, 1, ein_tail))):
                        mm = pe.matmul(bank[m % 2][:, 0:SLOTS], w[:, s, k, m * P:(m + 1) * P], r[:, e, :], start=(i == 0), stop=(i == 4))
                    mm.then_inc(up_made, 1)
                    if e == 0 and m < GP:
                        gates_to_slots(m)
                    if e and m == 1:
                        transpose_out(e - 1)
                    if e and m in (3, 5):
                        combine(e - 1, (m - 3) // 2)
                if e:
                    pe.wait_ge(eoT_done, 2 * e)
                for m in range(FM):
                    pe.wait_ge(hidhi_done, FM * e + m + 1)
                    pe.wait_ge(hidlo_done, FM * e + m + 1)
                    def tail_columns():
                        return pe.matmul(bank[3][:, 0:SLOTS], wo_hi[:, s, m, P:2 * P], hid_hi[:, m, :], start=(m == 0), stop=(m == FM - 1))

                    if m == 0:
                        tail_columns()
                    for i, (w, r) in enumerate(((wo_hi, hid_hi), (wo_lo, hid_hi), (wo_hi, hid_lo))):
                        pe.matmul(bank[2][:, 0:SLOTS], w[:, s, m, 0:P], r[:, m, :], start=(m == 0 and i == 0), stop=(m == FM - 1 and i == 2))
                    mm = pe.matmul(bank[3][0:DT, 0:SLOTS], wo_hi[:, s, m, P:D], hid_lo[:, m, :], start=False, stop=False)
                    if m:
                        mm = tail_columns()
                    if e and m in (1, 3):
                        combine(e - 1, 2 + m // 2)
                    if m < GP:
                        slots_bc(e, m)
                mm.then_inc(down_made, 1)
            transpose_out(NE - 1)
            for q in range(GP):
                combine(NE - 1, q)
            for i in range(NT):
                need = 2 * GP * (NE - 1) + 2 * min(GP, -(-(i + 1) * P // PTOK))
                pe.wait_ge(y_done, need)
                if i >= 2:
                    pe.wait_ge(fin_done, i - 1)
                if i == 0:
                    pe.wait_ge(hidlo_done, FM * NE)
                for k in range(2):
                    mm = pe.transpose(bank[i % 2][:, k * DH:(k + 1) * DH], y_acc[:, k, i * P:(i + 1) * P], identity[0:DH, 0:DH])
                mm.then_inc(yt_made, 1)

        @block.vector
        def _(dve):
            def normalize(i, src, dst, n):
                dve.tensor_scalar(dst, src, moments[:, i, 0:1], rstd[:, i:i + 1], ALU.subtract, ALU.mult).then_inc(norm_done, 1)

            def statistics(tiles, n0):
                for n, i in enumerate(tiles):
                    dve.bn_stats(stats[:, i, :], h[:, i, :]).then_inc(st_done, 1)
                for n, i in enumerate(tiles):
                    dve.wait_ge(st_done, n0 + n + 1)
                    dve.bn_aggr(moments[:, i, :], stats[:, i, :]).then_inc(mo_done, 1)

            def channel_stats(t, c, ws):
                for w in ws:
                    if w == ws[0]:
                        dve.wait_ge(x_in[t][c], 16)
                    dve.bn_stats(pstats[:, t, w, c, :], xin[:, t, c * PATCH:(c + 1) * PATCH, w, :]).then_inc(pstat_done, 1)

            def patch_moments(t, ws):
                for w in ws:
                    dve.wait_ge(pstat_done, SIDE * (C_IN * t + 2) + w + 1)
                    dve.bn_aggr(pmom[:, t, w, :], pstats[:, t, w, :, :]).then_inc(pmom_done, 1)

            def patch_norm(t):
                dve.wait_ge(prstd_done, 4 * t + 2)
                if t:
                    dve.wait_ge(pt_made, KJ * (2 * t - 1))
                dve.wait_ge(pmom_done, SIDE * t + SIDE // 2)
                for w in range(SIDE // 2):
                    dve.tensor_scalar(xn[:, w, :].rearrange("p (r e) -> p r e", e=PATCH), xin[:, t, :, w, :], pmom[:, t, w, 0:1], prstd[:, t, w:w + 1], ALU.subtract, ALU.mult).then_inc(pnorm_dve, 1)

            def add_bias(i):
                dve.wait_ge(emb_made, i + 1)
                dve.tensor_tensor(h[:, i, :], bank[(4 + i) % 8][:, 0:D], bl_bc[:], ALU.add).then_inc(emb_out, 1)

            def embedded(t, between):
                tiles = BATCHES[t]
                done, w = 2 * tiles[0], len(tiles)
                dve.wait_ge(emb_out, tiles[-1] + 1)
                statistics(tiles, done)
                dve.wait_ge(mo_done, done + w)
                for n, i in enumerate(tiles):
                    dve.scalar_tensor_tensor(h[:, i, :], h[:, i, :], moments[:, i, 0:1], g2_bc[:], ALU.subtract, ALU.mult).then_inc(centred, 1)
                    between(0, n)
                dve.wait_ge(rstd_done, 2 * t + 1)
                for n, i in enumerate(tiles):
                    dve.wait_ge(centred, i + 1)
                    dve.scalar_tensor_tensor(h[:, i, :], h[:, i, :], rstd[:, i:i + 1], b2_bc[:], ALU.mult, ALU.add).then_inc(norm_done, 1)
                    between(1, n)
                dve.wait_ge(norm_done, done + w)
                statistics(tiles, done + w)
                for n in range(w):
                    between(2, n)
                dve.wait_ge(rstd_done, 2 * t + 2)
                for n, i in enumerate(tiles):
                    normalize(i, h[:, i, :], a[:, i, :], 0)
                    between(3, n)

            def value_out(i):
                dve.wait_ge(v_made, i + 1)
                if i >= 3:
                    dve.wait_ge(v_stored[i % 3], 16 * (i // 3))
                dve.tensor_tensor(v_sb[:, i % 3, :], bank[4 + i % 2][:, 0:D], bv_bc[:], ALU.add).then_inc(v_out, 1)

            def query_out(n):
                q, g = n // HG, n % HG
                if n == 0:
                    dve.wait_ge(bqk_in, 32)
                dve.wait_ge(qk_made, 2 * n + 1)
                if q >= 2:
                    dve.wait_ge(sc_made, QP * (q - 1))
                dve.tensor_scalar(qT[:, q % 2, g, :], bank[6][0:DH, 0:CHUNK], bqk_sb[:, 0, g:g + 1], None, ALU.add).then_inc(q_out, 1)

            def patch_out(u):
                src, dst, gain, bias = patch_unit(u)
                dve.wait_ge(pt_made, u + 1)
                dve.tensor_scalar(dst, src, gain, bias, ALU.mult, ALU.add).then_inc(pt_dve, 1)

            for i in (0, 1, 4):
                dve.memset(bank[i][:], 1.0).then_inc(bank_set, 1)
            left, right = range(0, SIDE // 2), range(SIDE // 2, SIDE)
            for c in range(C_IN):
                for ws in (left, right):
                    channel_stats(0, c, ws)
                    if c == C_IN - 1:
                        patch_moments(0, ws)
            patch_norm(0)
            dve.wait_ge(aff_in, 16 * 6)
            for n, u in enumerate(range(1, 2 * KJ, 2)):
                patch_out(u)
                channel_stats(1, n // 2, (left, right)[n % 2])
                if n // 2 == C_IN - 1:
                    patch_moments(1, (left, right)[n % 2])
            patch_norm(1)
            for u in range(2 * KJ + 1, 4 * KJ, 2):
                patch_out(u)
            for i in BATCHES[0]:
                add_bias(i)
            embedded(0, lambda stage, n: add_bias(4 + n) if stage == 2 else None)
            add_bias(NT - 1)

            def first_values_and_queries(stage, n):
                todo = {(0, 2): (value_out, 0), (0, 4): (value_out, 1), (1, 2): (value_out, 2), (1, 4): (value_out, 3),
                        (2, 0): (query_out, 0), (3, 1): (query_out, 1)}
                if (stage, n) in todo:
                    f, k = todo[stage, n]
                    f(k)

            embedded(1, first_values_and_queries)
            for i in BATCHES[1]:
                value_out(i)
            def late_residual(i):
                dve.wait_ge(wout_made, i + 1)
                dve.wait_ge(gain_done, i + 1)
                dve.tensor_tensor(h[:, i, :], bank[6][:, 0:D], h[:, i, :], ALU.add).then_inc(res1, 1)
                dve.wait_ge(res1, i + 1)
                statistics([i], 2 * NT + i)

            def late_normalize(i):
                dve.wait_ge(rstd_done, 4 + i + 1)
                normalize(i, h[:, i, :], a[:, i, :], 0)

            dve.wait_ge(masks, 8)
            for step in range(PAIRS + 4):
                p = step
                if p < PAIRS:
                    s = p % 2
                    dve.wait_ge(sc_made, p + 1)
                    if p >= 2:
                        dve.wait_ge(p_done, p - 1)
                    dve.tensor_tensor(sm[:, s, :, :], bank[s][0:QROWS, 0:HEADS * T].rearrange("p (h k) -> p h k", h=HEADS),
                                      causal[:, None, :].to_broadcast([QROWS, HEADS, T]), ALU.add).then_inc(sm_masked, 1)
                    dve.wait_ge(sm_masked, p + 1)
                    dve.tensor_reduce(smax[:, s, :], sm[:, s, :, :], AX.X, ALU.max).then_inc(sm_max, 1)
                    dve.wait_ge(sm_max, p + 1)
                    dve.tensor_tensor(sm[:, s, :, :], sm[:, s, :, :], smax[:, s, :, None].to_broadcast([QROWS, HEADS, T]), ALU.subtract).then_inc(sm_shift, 1)
                if step % QP < HG and step // QP + 1 < NQ:
                    query_out((step // QP + 1) * HG + step % QP)
                p = step - 3
                if 0 <= p < PAIRS:
                    s = p % 2
                    o = bank[4][0:QROWS, 0:HEADS * (HD + 1)].rearrange("p (h d) -> p h d", h=HEADS)
                    dve.wait_ge(o_made, p + 1)
                    dve.reciprocal(rsum[:, s, :], o[:, :, HD]).then_inc(rs_done, 1)
                    dve.wait_ge(rs_done, p + 1)
                    if p >= 2:
                        dve.wait_ge(oT_made, p - 1)
                    dve.tensor_tensor(o_sb[:, s, :, :], o[:, :, 0:HD], rsum[:, s, :, None].to_broadcast([QROWS, HEADS, HD]), ALU.mult).then_inc(o_done, 1)
                if step >= LATE + 1:
                    late_normalize(step - LATE - 1)
                if step == LATE - 1:
                    dve.wait_ge(wo_in, 48)
                if 0 <= step - LATE + 1 < NT:
                    i = step - LATE + 1
                    dve.tensor_tensor(h[:, i, :], h[:, i, :], bout_bc[:], ALU.add).then_inc(gain_done, 1)
                if step >= LATE:
                    late_residual(step - LATE)
            late_normalize(NT - 1)
            count = [0]

            def link(ins):
                count[0] += 1
                ins.then_inc(route, 1)
                dve.wait_ge(route, count[0])

            def bc(ap):
                return ap[:, :, None].to_broadcast([P, NT, NE])

            exp_bc = expert_no[:, None, :].to_broadcast([P, NT, NE])
            dve.wait_ge(lg_made, NT)
            dve.wait_ge(tables, TABLES)
            link(dve.tensor_copy(lg[:], bank[7][:, LG:LG + NT * NE].rearrange("p (t e) -> p t e", t=NT)))
            link(dve.tensor_reduce(top[:, 0, :], lg[:], AX.X, ALU.max))
            link(dve.tensor_tensor(lsh[:], lg[:], bc(top[:, 0, :]), ALU.subtract))
            assert count[0] == R_LSH
            link(dve.tensor_tensor(eq[:], lg[:], bc(top[:, 0, :]), ALU.is_equal))
            link(dve.tensor_tensor(eq[:], eq[:], exp_bc, ALU.mult))
            link(dve.tensor_reduce(first[:, 0, :], eq[:], AX.X, ALU.min))
            link(dve.tensor_tensor(pick1[:], exp_bc, bc(first[:, 0, :]), ALU.is_equal))
            link(dve.scalar_tensor_tensor(lg2[:], pick1[:], -3e38, lg[:], ALU.mult, ALU.add))
            link(dve.tensor_reduce(top[:, 1, :], lg2[:], AX.X, ALU.max))
            link(dve.tensor_tensor(eq[:], lg2[:], bc(top[:, 1, :]), ALU.is_equal))
            link(dve.tensor_tensor(eq[:], eq[:], exp_bc, ALU.mult))
            link(dve.tensor_reduce(first[:, 1, :], eq[:], AX.X, ALU.min))
            link(dve.tensor_tensor(pick2[:], exp_bc, bc(first[:, 1, :]), ALU.is_equal))
            assert count[0] == R_PICK2
            dve.wait_ge(ex_done, 1)
            link(dve.tensor_reduce(esum[:], ex[:], AX.X, ALU.add))
            link(dve.reciprocal(erec[:], esum[:]))
            link(dve.tensor_tensor(gate[:], ex[:], bc(erec[:]), ALU.mult))
            link(dve.tensor_copy(gate_split[:, :, 0:NE], gate[:]))
            link(dve.tensor_tensor(gate_split[:, :, NE:2 * NE], gate[:], gate_split[:, :, 0:NE].bitcast(F32), ALU.subtract))
            dve.wait_ge(prio_made, 1)
            link(dve.scalar_tensor_tensor(s1[:], bank[6][:, 0:NT * NE].rearrange("p (t e) -> p t e", t=NT), 1.0, pick1[:], ALU.add, ALU.mult))
            link(dve.scalar_tensor_tensor(s2[:], bank[6][:, 128:128 + NT * NE].rearrange("p (t e) -> p t e", t=NT), 1.0, pick2[:], ALU.add, ALU.mult))
            link(dve.tensor_tensor(s1[:], s1[:], s2[:], ALU.add))
            link(dve.scalar_tensor_tensor(slot[:], s1[:], 50.0, bc(parity[:]), ALU.min, ALU.add))
            link(dve.tensor_copy(slot_bf[:], slot[:]))
            assert count[0] == R_SLOTBF

            def ein_last(g):
                dve.wait_ge(disp_made, 4 * g + 3)
                dve.tensor_copy(ein_tail[:, :, g * CAP:(g + 1) * CAP],
                                bank[4 * (g % 2) + 2][:, 0:NE * CAP].rearrange("p (e c) -> p e c", e=NE)).then_inc(ein_dve, 1)

            for n in range(2 * GROUPS):
                g = n // 2
                t = g + n % 2
                if n >= 4:
                    dve.wait_ge(disp_made, 4 * (g - 1))
                dve.tensor_tensor(d01[:, n % 4, :, :], slot[:, t, :, None].to_broadcast([P, NE, CAP]),
                                  slot_no[:, g % 2, None, :].to_broadcast([P, NE, CAP]), ALU.is_equal).then_inc(d01_done, 1)
                if n == 1:
                    dve.wait_ge(slotT_made, 1)
                    dve.tensor_copy(slotT[:, 0:8 * P], bank_bf[7][0:NE, :]).then_inc(slotT_done, 1)
                    dve.tensor_copy(slotT[:, 8 * P:], bank_bf[6][0:NE, 0:P]).then_inc(slotT_done, 1)
                if n >= 3 and n % 2:
                    ein_last(g - 1)
            ein_last(GROUPS - 1)

            def eo_low(e):
                for r in range(2):
                    dve.wait_ge(eohi_done, GP * e + 2 * r + 2)
                    for q in (2 * r, 2 * r + 1):
                        dve.scalar_tensor_tensor(eo_lo[:, q, :], bank[4 + r][0:PS, q % 2 * D:(q % 2 + 1) * D], gate_slot[:, GP * e + q:GP * e + q + 1],
                                                 eo_hi[:, q, :].bitcast(F32), ALU.mult, ALU.subtract).then_inc(eolo_done, 1)

            def add_y(e, q):
                for k in range(2):
                    n = 2 * (GP * e + q) + k
                    dve.wait_ge(y_made, n + 1)
                    dst = y_acc[:, k, q * PTOK:(q + 1) * PTOK]
                    if e == 0:
                        dve.tensor_copy(dst, bank[6 + k][0:DH, 0:PTOK]).then_inc(y_done, 1)
                    else:
                        dve.wait_ge(y_done, n + 1 - 2 * GP)
                        dve.tensor_tensor(dst, bank[6 + k][0:DH, 0:PTOK], dst, ALU.add).then_inc(y_done, 1)

            def slot_rows(e, q):
                n = GP * e + q
                dve.wait_ge(bc_made, n + 1)
                if e >= 2:
                    dve.wait_ge(y_made, 2 * GP * (e - 2) + 2 * q + 2)
                dve.tensor_scalar(comb[:, e % 2, q, :], bank[4 + q % 2][0:PS, 0:PTOK], slot_of_row[:], None, ALU.is_equal).then_inc(comb_done, 1)

            for e in range(NE):
                for m in range(FM):
                    dve.wait_ge(hidhi_done, FM * e + m + 1)
                    dve.scalar_tensor_tensor(hid_lo[:, m, :], bank[m % 2][:, 0:SLOTS], 0.0, hid_hi[:, m, :].bitcast(F32), ALU.max, ALU.subtract).then_inc(hidlo_done, 1)
                    if e and m == 1:
                        eo_low(e - 1)
                    if e and m in (3, 5):
                        add_y(e - 1, (m - 3) // 2)
                if e == 0:
                    dve.wait_ge(gate_made, GP)
                    dve.tensor_copy(gate_slot[:], bank[6][0:PS, 0:2 * NE * GP].rearrange("p (n c) -> p n c", c=2)[:, :, 0]).then_inc(gate_done, 1)
                for q in range(GP):
                    if e and q in (1, 3):
                        add_y(e - 1, 2 + q // 2)
                    slot_rows(e, q)
            eo_low(NE - 1)
            for q in range(GP):
                add_y(NE - 1, q)
            for i in range(NT):
                dve.wait_ge(yt_made, i + 1)
                dve.tensor_tensor(a[:, i, :], bank[i % 2][:, 0:D], h[:, i, :], ALU.add).then_inc(fin_done, 1)


_NAMES = ["x", "L0_tok_ln1_g", "L0_tok_ln1_b", "L0_tok_Wl", "L0_tok_bl", "L0_tok_ln2_g", "L0_tok_ln2_b",
          "L0_attn_W_qkv", "L0_attn_b_qkv", "L0_attn_W_out", "L0_attn_b_out", "L0_ffn_w_router", "L0_ffn_wi", "L0_ffn_wo"]


def kernel(**inputs):
    import numpy as np
    import concourse.bacc as bacc
    from concourse.bass_utils import run_bass_kernel_spmd

    nc = bacc.Bacc("TRN2", target_bir_lowering=False, num_devices=1)
    arrays, args = {}, []
    for name in _NAMES:
        arrays[name] = np.ascontiguousarray(inputs[name])
        args.append(nc.dram_tensor(name, arrays[name].shape, F32, kind="ExternalInput").ap())
    out = nc.dram_tensor("out", (N, D), F32, kind="ExternalOutput").ap()
    build(nc, *args, out)
    r = run_bass_kernel_spmd(nc, [arrays], core_ids=[0])
    return r.results[0]["out"].reshape(B, T, D)
```

```python
from contextlib import ExitStack

import concourse.bass as bass
from concourse import mybir

ALU = mybir.AluOpType
ACT = mybir.ActivationFunctionType
AX = mybir.AxisListType
F32 = mybir.dt.float32
F32R = mybir.dt.float32r
BF16 = mybir.dt.bfloat16

P = 128
B, C_IN, IMG = 32, 3, 96
PATCH = 16
SIDE = IMG // PATCH
T = SIDE * SIDE
N = B * T
NT = N // P
D_PATCH = PATCH * PATCH * C_IN
KJ = D_PATCH // P
D = 192
DH = D // 2
DT = D - P
HEADS, HD = 12, 16
H6 = DH // HD
HG = HEADS // H6
KP = 4
H3 = 3
G3 = HEADS // H3
PAIRS = B // 2
QROWS = 64 + T
NE = 8
GROUPS = 8
S = N // GROUPS
CAP = max(int(2 * 1.25 * S / NE), 4)
SLOTS = GROUPS * CAP
FF = 768
FM = FF // P
GP = GROUPS // 2
PS = 2 * CAP
PTOK = 2 * S
SHIFT = P - (2 * P - S)
ROWS = B // 2 * SIDE
QI = 8
NQ = B // QI
CHUNK = QI * T
QP = QI // 2
EPS = 1e-5
NEG = -1e30
LAST_EARLY = PAIRS + 1
STATS_BETWEEN = 1
WARM_FIRST, WARM_DRAIN, WARM_ROUTE, WARM_LAST = 44, (2, 2, 2), (5, 1, 6), (4, 4)
TAILS_BY_ACT = (1, 4)
LG = 256
LATE = NQ // 4 * 3 * QP - 1
assert all((LATE + i - 4 + 1) * 2 * T >= (i + 1) * P for i in range(NT))
assert LATE + NT == PAIRS + 4
assert SHIFT == S - P and NT == GROUPS + 1 and ROWS == DH
TABLES = 16 + NT
R_LSH, R_PICK1, R_PICK2, R_SLOT = 2, 5, 11, 17


def build(nc, x, ln1_g, ln1_b, Wl, bl, ln2_g, ln2_b, W_qkv, b_qkv, W_out, b_out, w_router, wi, wo, out):
    v_dram = nc.dram_tensor("v_scratch", (N, D), F32, kind="Internal").ap()
    with ExitStack() as ctx:
        def sb(name, shape, dt=F32, where=ctx):
            return where.enter_context(nc.sbuf_tensor(name, shape, dt))

        def sem(name):
            return ctx.enter_context(nc.semaphore(name))

        bank = [ctx.enter_context(nc.psum_tensor(f"bank{i}", [P, 512], F32)) for i in range(8)]
        bank_bf = {i: bank[i][:, :].bitcast(BF16) for i in (6, 7)}

        identity = sb("identity", [P, P])
        identity_bf = sb("identity_bf", [P, P], BF16)
        fold = sb("fold", [P, DT])
        sum_halves = sb("sum_halves", [2 * NE, NE])
        minus_half = sb("minus_half", [P, NT])
        h = sb("h", [P, NT, D])
        a = sb("a", [P, NT, D])
        aT = sb("aT", [DH, 2, N])
        act_warm = sb("act_warm", [P, 1])
        stats = sb("stats", [P, NT, 6])
        moments = sb("moments", [P, NT, 2])
        rstd = sb("rstd", [P, NT])
        wr_sb = sb("wr_sb", [DH, 2, NE])
        wout_sb = sb("wout_sb", [DH, 2, D])
        bout_bc = sb("bout_bc", [P, D])
        y_acc = sb("y_acc", [P, 2, N])
        oT = y_acc
        same = sb("same", [P, NT, P], BF16)
        before = sb("before", [P, NT, P], BF16)
        prev_tile = sb("prev_tile", [P, NT, P], BF16)
        next_tile = sb("next_tile", [P, NT, P], BF16)
        expert_no = sb("expert_no", [P, NE])
        slot_no = sb("slot_no", [P, 2, CAP])
        parity = sb("parity", [P, NT])
        slot_of_row = sb("slot_of_row", [PS, 1])
        second_row = sb("second_row", [PS, 1])
        pick = sb("pick", [NE, NE, PS], BF16)

        with ExitStack() as r1:
            xin = sb("xin", [ROWS, 2, C_IN * PATCH, SIDE, PATCH], where=r1)
            pT = sb("pT", [P, KJ, N], where=r1)
        wi_raw = sb("wi_raw", [P, 2, 2, FF])
        wo_raw = sb("wo_raw", [P, 2, FM, D])
        wi_hi = sb("wi_hi", [P, 2, 2, FF], F32R)
        wi_lo = sb("wi_lo", [P, 2, 2, FF], F32R)
        wo_hi = sb("wo_hi", [P, 2, FM, 2 * P], F32R)
        wo_lo = sb("wo_lo", [P, 2, FM, P], F32R)

        with ExitStack() as r2:
            wqkv_sb = sb("wqkv_sb", [DH, 2, 3 * D], where=r2)
            bqk_sb = sb("bqk_sb", [DH, 2, HG], where=r2)
            bv_bc = sb("bv_bc", [P, D], where=r2)
            v_sb = sb("v_sb", [P, 3, D], where=r2)
            qT = sb("qT", [DH, 2, HG, CHUNK], where=r2)
            k_tmp = sb("k_tmp", [DH, 3, CHUNK], where=r2)
            with ExitStack() as r5:
                ones = sb("ones", [P, NT, P], BF16, where=r5)
                row_ge = sb("row_ge", [P, NT, P], BF16, where=r5)
                col_ge = sb("col_ge", [P, NT, P], BF16, where=r5)
            k_diag = sb("k_diag", [DH, 2, HG, H6, CHUNK], where=r2)
            v_diag = sb("v_diag", [H3 * T, 2 * QI, G3, H3, HD + 1], where=r2)
            own_head = sb("own_head", [H3 * T, H3], where=r2)
            causal = sb("causal", [QROWS, T], where=r2)
            causal2 = sb("causal2", [QROWS, T], where=r2)
            head_rows = sb("head_rows", [DH, H6], where=r2)
            with ExitStack() as r4:
                xn = sb("xn", [ROWS, SIDE, D_PATCH], where=r4)
                wl_sb = sb("wl_sb", [P, 2, C_IN, D], where=r4)
                g1_sb = sb("g1_sb", [P, 2, C_IN], where=r4)
                b1_sb = sb("b1_sb", [P, 2, C_IN], where=r4)
                bl_bc = sb("bl_bc", [P, D], where=r4)
                g2_bc = sb("g2_bc", [P, D], where=r4)
                b2_bc = sb("b2_bc", [P, D], where=r4)
                pstats = sb("pstats", [ROWS, 2, SIDE, C_IN, 6], where=r4)
                pmom = sb("pmom", [ROWS, 2, SIDE, 2], where=r4)
                prstd = sb("prstd", [ROWS, 2, SIDE], where=r4)
                pshift = sb("pshift", [ROWS, 2, SIDE], where=r4)
            v_rep = sb("v_rep", [H3 * T, QI, D], where=r2)
            sm = sb("sm", [QROWS, 2, HEADS, T], where=r2)
            smax = sb("smax", [QROWS, 2, HEADS], where=r2)
            probs = sb("probs", [QROWS, 2, HEADS, T], where=r2)
            probsT = sb("probsT", [H3 * T, 2, G3, QROWS], where=r2)
            rsum = sb("rsum", [QROWS, 2, HEADS], where=r2)
            o_sb = sb("o_sb", [QROWS, 2, HEADS, HD], where=r2)
        lg2 = sb("lg2", [P, NT, NE])
        top = sb("top", [P, 2, NT])
        eq = sb("eq", [P, NT, NE])
        first = sb("first", [P, 2, NT])
        pick1 = sb("pick1", [P, NT, NE], BF16)
        pick2 = sb("pick2", [P, NT, NE], BF16)
        lsh = sb("lsh", [P, NT, NE])
        ex = sb("ex", [P, NT, NE])
        esum = sb("esum", [P, NT])
        erec = sb("erec", [P, NT])
        gate = sb("gate", [P, NT, NE])
        gate_split = sb("gate_split", [P, NT, 2 * NE], F32R)
        gate_rows = sb("gate_rows", [2 * NE, NE, SLOTS])
        gate_line = sb("gate_line", [2 * NE, SLOTS])
        gate_slot = sb("gate_slot", [PS, GP, NE])
        s1 = sb("s1", [P, NT, NE])
        s2 = sb("s2", [P, NT, NE])
        slot = sb("slot", [P, NT, NE])
        slot_bf = sb("slot_bf", [P, NT, NE], BF16)
        slotT = sb("slotT", [NE, N], BF16)
        ein_hi = sb("ein_hi", [P, NE, SLOTS], F32R)
        ein_lo = sb("ein_lo", [P, NE, SLOTS], F32R)
        ein_tail = sb("ein_tail", [P, NE, SLOTS], F32R)
        with ExitStack() as r3:
            a_split = sb("a_split", [P, NT, 3 * P], F32R, where=r3)
            d01 = sb("d01", [P, 4, NE, CAP], F32R, where=r3)
        hid_hi = sb("hid_hi", [P, FM, SLOTS], F32R)
        hid_lo = sb("hid_lo", [P, FM, SLOTS], F32R)
        comb = sb("comb", [PS, 2, GP, PTOK], F32R)
        eoT = sb("eoT", [P, 2, SLOTS])
        eo_split = sb("eo_split", [PS, GP, 3 * P], F32R)

        x_in = [[sem(f"x_in{t}_{c}") for c in range(C_IN)] for t in range(2)]
        wl_in, aff_in, bias_in, wq_in, wo_in, bqk_in = sem("wl_in"), sem("aff_in"), sem("bias_in"), sem("wq_in"), sem("wo_in"), sem("bqk_in")
        wi_in = [sem(f"wi_in{i}") for i in range(2)]
        consts, vones, tables, scratch = sem("consts"), sem("vones"), sem("tables"), sem("scratch")
        bank_set = sem("bank_set")
        pstat_done, pmom_done, prstd_done, pshift_done, pnorm_act, pnorm_dve = (sem(s) for s in ("pstat_done", "pmom_done", "prstd_done", "pshift_done", "pnorm_act", "pnorm_dve"))
        pt_made, pt_act, pt_dve = sem("pt_made"), sem("pt_act"), sem("pt_dve")
        emb_made, emb_out = sem("emb_made"), sem("emb_out")
        st_done, mo_done, var_done, rstd_done = sem("st_done"), sem("mo_done"), sem("var_done"), sem("rstd_done")
        centred, norm_done, gain_done = sem("centred"), sem("norm_done"), sem("gain_done")
        aT_made, aT_done = sem("aT_made"), sem("aT_done")
        v_made, v_out, v_stored, v_loaded, v_ready = sem("v_made"), sem("v_out"), [sem(f"v_stored{i}") for i in range(3)], [sem(f"v_loaded{i}") for i in range(2)], sem("v_ready")
        masks = sem("masks")
        qk_made, k_ready_act, q_out, k_out, k_ready = sem("qk_made"), sem("k_ready_act"), sem("q_out"), sem("k_out"), sem("k_ready")
        sc_made, sm_masked, sm_max, sm_shift, p_done = sem("sc_made"), sem("sm_masked"), sem("sm_max"), sem("sm_shift"), sem("p_done")
        pT_made, pT_done, o_made, rs_done, o_done, oT_made, oT_done = (sem(s) for s in ("pT_made", "pT_done", "o_made", "rs_done", "o_done", "oT_made", "oT_done"))
        wout_made, res1 = sem("wout_made"), sem("res1")
        lg_made, route, ex_done, prio_made, slotT_made, slotT_done, ahi_done, alo_done = (sem(s) for s in ("lg_made", "route", "ex_done", "prio_made", "slotT_made", "slotT_done", "ahi_done", "alo_done"))
        slotbf_done, gates, own_gates, line_done = (sem(s) for s in ("slotbf_done", "gates", "own_gates", "line_done"))
        d01_done, disp_made, ein_act, ein_dve, gate_made, gate_done = (sem(s) for s in ("d01_done", "disp_made", "ein_act", "ein_dve", "gate_made", "gate_done"))
        whi_done, wlo_done = sem("whi_done"), sem("wlo_done")
        up_made, hidhi_done, hidlo_done, down_made, eoT_done = (sem(s) for s in ("up_made", "hidhi_done", "hidlo_done", "down_made", "eoT_done"))
        eo_made, eohi_done, eolo_done, bc_made, comb_done, y_made, y_done = (sem(s) for s in ("eo_made", "eohi_done", "eolo_done", "bc_made", "comb_done", "y_made", "y_done"))
        yt_made, yt_out, fin_done, fin_shared, out_sent = (sem(s) for s in ("yt_made", "yt_out", "fin_done", "fin_shared", "out_sent"))

        def y_bank(e, q, k):
            return bank[(6, 0, 2, 6)[q] + k if e == NE - 1 else 6 + k]

        def transposed_early(step):
            return [step - LATE - 2] if LATE + 2 <= step <= LAST_EARLY else []

        def transposed_late(step):
            return [step - LATE - 1] if step >= LAST_EARLY else []

        last_masked = {PAIRS % 2: PAIRS - 1, 1 - PAIRS % 2: PAIRS}

        def norm_bank(i):
            return bank[{NT - 2: 2, NT - 1: 3}.get(i, 7)]

        def projected(i):
            return bank[0 if i == NT - 1 else 6][:, 0:D]

        def by_act(g):
            return 3 * (g + 1) + len([t for t in TAILS_BY_ACT if t <= g])

        def dispatch_matrix(n):
            g = n // 2
            return (d01[:, n % 4, :, :], slot[:, g + n % 2, :, None].to_broadcast([P, NE, CAP]),
                    slot_no[:, g % 2, None, :].to_broadcast([P, NE, CAP]))

        LAST_BANKS = (4, 5, 0, 1)
        SHARED = (1, 3)
        own_tiles = [i for i in range(NT) if i not in SHARED]

        def wait_last_bank(pe, i):
            if i in SHARED:
                pe.wait_ge(yt_out, SHARED.index(i) + 1)
            else:
                pe.wait_ge(fin_done, own_tiles.index(i) + 1)
        BATCHES = [range(0, 4), range(4, NT)]

        ctx.enter_context(nc.allow_non_contiguous_dma("row-sized runs"))
        block = ctx.enter_context(nc.Block())

        def patch_unit(u):
            t, w, j = u // (2 * KJ), u // KJ % 2, u % KJ
            src = bank[u % 4][:, 0:3 * ROWS].rearrange("p (w r) -> p w r", w=3)
            dst = pT[:, j, t * ROWS * SIDE:(t + 1) * ROWS * SIDE].rearrange("p (r w) -> p w r", w=SIDE)[:, 3 * w:3 * w + 3, :]
            gain, bias = (v[:, j % 2, j // 2:j // 2 + 1] for v in (g1_sb, b1_sb))
            return src, dst, gain, bias

        UNITS = range(4 * KJ)
        dve_units = [u for u in UNITS if u % 2 or u == 0]
        act_units = [u for u in UNITS if u not in dve_units]

        def wait_unit_out(pe, u):
            if u in dve_units:
                pe.wait_ge(pt_dve, dve_units.index(u) + 1)
            else:
                pe.wait_ge(pt_act, act_units.index(u) + 1)

        @block.sync
        def _(sp):
            xv = x.rearrange("(t b) c (h q) w -> t c b h (q w)", t=2, q=PATCH)
            for t in range(2):
                for c in range(C_IN):
                    sp.dma_start(xin[:, t, c * PATCH:(c + 1) * PATCH, :, :], xv[t, c]).then_inc(x_in[t][c], 16)
                if t == 0:
                    sp.dma_start(wl_sb[:], Wl.rearrange("(f n c) e -> n f c e", f=2, c=C_IN)).then_inc(wl_in, 16)
            for dst, src in ((bl_bc, bl), (g2_bc, ln2_g), (b2_bc, ln2_b), (bv_bc, b_qkv[2 * D:3 * D])):
                sp.dma_start(dst[:], src.rearrange("(o n) -> o n", o=1).to_broadcast([P, D])).then_inc(bias_in, 16)
            for i in range(2):
                sp.dma_start(bqk_sb[:, i, :], b_qkv[i * D:(i + 1) * D].rearrange("(g p) -> p g", g=HG)).then_inc(bqk_in, 16)
            sp.dma_start(wqkv_sb[:], W_qkv.rearrange("(k p) n -> p k n", k=2)).then_inc(wq_in, 16)
            sp.dma_start(wout_sb[:], W_out.rearrange("(k p) n -> p k n", k=2)).then_inc(wo_in, 16)
            sp.dma_start(wr_sb[:], w_router.rearrange("(k p) n -> p k n", k=2)).then_inc(wo_in, 16)
            sp.dma_start(bout_bc[:], b_out.rearrange("(o n) -> o n", o=1).to_broadcast([P, D])).then_inc(wo_in, 16)

            def store_values(tiles):
                for i in tiles:
                    sp.wait_ge(v_out, i + 1)
                    sp.dma_start(v_dram[i * P:(i + 1) * P, :], v_sb[:, i % 3, :]).then_inc(v_stored[i % 3], 16)

            def load_values(q):
                for i in range(-(-q * CHUNK // P), -(-(q + 1) * CHUNK // P)):
                    sp.wait_ge(v_stored[i % 3], 16 * (i // 3 + 1))
                if q >= 1:
                    sp.wait_ge(v_ready, q)
                vq = v_dram[q * CHUNK:(q + 1) * CHUNK, :].rearrange("(b k) d -> k b d", k=T)
                for r in range(H3):
                    sp.dma_start(v_rep[r * T:(r + 1) * T, :, :], vq).then_inc(v_loaded[q % 2], 16)

            store_values(range(3))
            load_values(0)
            store_values(range(3, NT))
            for q in range(1, NQ):
                load_values(q)
            sp.wait_ge(tables, TABLES)
            for e in range(NE):
                if e >= 2:
                    sp.wait_ge(wlo_done, 2 * (e - 1))
                sp.dma_start(wi_raw[:, e % 2, 0, :], wi[e, 0:P, :]).then_inc(wi_in[e % 2], 16)
                for r in range(2):
                    sp.dma_start(wi_raw[r * DT:(r + 1) * DT, e % 2, 1, :], wi[e, P:D, :]).then_inc(wi_in[e % 2], 16)
                sp.dma_start(wo_raw[:, e % 2, :, :], wo[e].rearrange("(m p) d -> p m d", m=FM)).then_inc(wi_in[e % 2], 16)
            out_tiles = out.rearrange("(t p) d -> p t d", p=P)
            for i in range(0, NT, 2):
                n = min(2, NT - i)
                sp.wait_ge(fin_done, len([j for j in own_tiles if j < i + n]))
                if i + 1 in SHARED:
                    sp.wait_ge(fin_shared, SHARED.index(i + 1) + 1)
                sp.dma_start(out_tiles[:, i:i + n, :], a[:, i:i + n, :]).then_inc(out_sent, 16)
            sp.wait_ge(out_sent, 16 * -(-NT // 2))

        @block.gpsimd
        def _(gp):
            gp.memset(identity[:], 0.0).then_inc(consts, 1)
            gp.memset(identity_bf[:], 0.0).then_inc(consts, 1)
            gp.memset(minus_half[:], -0.5).then_inc(consts, 1)
            gp.memset(causal[:], 0.0).then_inc(consts, 1)
            gp.memset(causal2[:], 0.0).then_inc(consts, 1)
            gp.memset(head_rows[:], 1.0).then_inc(consts, 1)
            gp.memset(own_head[:], 1.0).then_inc(consts, 1)
            gp.memset(pick[:], 1.0).then_inc(consts, 1)
            gp.wait_ge(consts, 8)
            for m in (identity, identity_bf):
                gp.affine_select(out=m[:], in_=m[:], compare_op=ALU.not_equal, fill=1.0, base=0,
                                 pattern=[[-1, P]], channel_multiplier=1).then_inc(consts, 1)
            gp.wait_ge(consts, 10)
            gp.tensor_tensor(fold[:], identity[:, 0:DT], identity[:, DT:P], ALU.add).then_inc(consts, 1)
            gp.tensor_tensor(sum_halves[:], identity[0:2 * NE, 0:NE], identity[0:2 * NE, NE:2 * NE], ALU.add).then_inc(consts, 1)

            def patch_rstd(t):
                for w in range(2):
                    part = slice(w * SIDE // 2, (w + 1) * SIDE // 2)
                    gp.wait_ge(pmom_done, SIDE * t + (w + 1) * SIDE // 2)
                    gp.tensor_scalar(prstd[:, t, part], pmom[:, t, part, 1], EPS, None, ALU.add).then_inc(prstd_done, 1)
                    if w == 1:
                        gp.tensor_scalar(pshift[:, t, part], pmom[:, t, part, 0], -1.0, None, ALU.mult).then_inc(pshift_done, 1)
                    gp.wait_ge(prstd_done, 2 * (2 * t + w) + 1)
                    gp.tensor_tensor(prstd[:, t, part], prstd[:, t, part], minus_half[0:ROWS, 0:SIDE // 2], ALU.pow).then_inc(prstd_done, 1)
                    if w == 1:
                        gp.wait_ge(prstd_done, 2 * (2 * t + w) + 2)
                        gp.wait_ge(pshift_done, 2 * t + 1)
                        gp.tensor_tensor(pshift[:, t, part], pshift[:, t, part], prstd[:, t, part], ALU.mult).then_inc(pshift_done, 1)
            patch_rstd(0)
            gp.affine_select(out=causal[:], in_=causal[:], compare_op=ALU.is_ge, fill=NEG, base=0,
                             pattern=[[-1, T]], channel_multiplier=1).then_inc(masks, 1)
            gp.affine_select(out=causal2[:], in_=causal2[:], compare_op=ALU.is_ge, fill=NEG, base=-64,
                             pattern=[[-1, T]], channel_multiplier=1).then_inc(masks, 1)
            gp.affine_select(out=own_head[:], in_=own_head[:], compare_op=ALU.is_ge, fill=0.0, base=0,
                             pattern=[[-T, H3]], channel_multiplier=1).then_inc(masks, 1)
            gp.affine_select(out=head_rows[:], in_=head_rows[:], compare_op=ALU.is_ge, fill=0.0, base=0,
                             pattern=[[-HD, H6]], channel_multiplier=1).then_inc(masks, 1)
            gp.wait_ge(masks, 4)
            gp.affine_select(out=causal2[:], in_=causal2[:], compare_op=ALU.is_ge, fill=0.0, base=-64,
                             pattern=[[0, T]], channel_multiplier=1).then_inc(masks, 1)
            gp.affine_select(out=own_head[:], in_=own_head[:], compare_op=ALU.is_ge, fill=0.0, base=T - 1,
                             pattern=[[T, H3]], channel_multiplier=-1).then_inc(masks, 1)
            gp.affine_select(out=head_rows[:], in_=head_rows[:], compare_op=ALU.is_ge, fill=0.0, base=HD - 1,
                             pattern=[[HD, H6]], channel_multiplier=-1).then_inc(masks, 1)
            gp.wait_ge(masks, 7)
            gp.tensor_tensor(causal[:], causal[:], causal2[:], ALU.add).then_inc(masks, 1)
            gp.memset(ones[:], 1.0).then_inc(scratch, 1)
            gp.wait_ge(scratch, 1)
            gp.affine_select(out=row_ge[:], in_=ones[:], compare_op=ALU.is_ge, fill=0.0, base=0,
                             pattern=[[-SHIFT, NT], [0, P]], channel_multiplier=1).then_inc(tables, 1)
            gp.affine_select(out=col_ge[:], in_=ones[:], compare_op=ALU.is_ge, fill=0.0, base=0,
                             pattern=[[-SHIFT, NT], [1, P]], channel_multiplier=0).then_inc(tables, 1)
            gp.affine_select(out=prev_tile[:], in_=ones[:], compare_op=ALU.is_ge, fill=0.0, base=SHIFT,
                             pattern=[[-SHIFT, NT], [0, P]], channel_multiplier=1).then_inc(tables, 1)
            gp.affine_select(out=next_tile[:], in_=ones[:], compare_op=ALU.is_gt, fill=0.0, base=SHIFT,
                             pattern=[[SHIFT, NT], [0, P]], channel_multiplier=-1).then_inc(tables, 1)
            gp.affine_select(out=pick[:], in_=pick[:], compare_op=ALU.is_equal, fill=0.0, base=0,
                             pattern=[[-1, NE], [0, PS]], channel_multiplier=1).then_inc(tables, 1)
            gp.iota(expert_no[:], pattern=[[1, NE]], base=-NE, channel_multiplier=0, allow_small_or_imprecise_dtypes=True).then_inc(tables, 1)
            gp.iota(slot_no[:], pattern=[[64, 2], [1, CAP]], base=1, channel_multiplier=0, allow_small_or_imprecise_dtypes=True).then_inc(tables, 1)
            gp.iota(slot_of_row[:], pattern=[[0, 1]], base=1, channel_multiplier=1, allow_small_or_imprecise_dtypes=True).then_inc(tables, 1)
            gp.memset(second_row[:], 64.0 - CAP).then_inc(tables, 1)
            patch_rstd(1)
            gp.wait_ge(tables, 9)
            gp.tensor_tensor(ones[:], row_ge[:], col_ge[:], ALU.subtract).then_inc(tables, 1)
            gp.affine_select(out=prev_tile[:], in_=prev_tile[:], compare_op=ALU.is_gt, fill=0.0, base=0,
                             pattern=[[SHIFT, NT], [-1, P]], channel_multiplier=0).then_inc(tables, 1)
            gp.affine_select(out=next_tile[:], in_=next_tile[:], compare_op=ALU.is_ge, fill=0.0, base=0,
                             pattern=[[-SHIFT, NT], [1, P]], channel_multiplier=0).then_inc(tables, 1)
            gp.tensor_copy(parity[:], row_ge[:, :, 0]).then_inc(tables, 1)
            gp.affine_select(out=second_row[:], in_=second_row[:], compare_op=ALU.is_ge, fill=0.0, base=-CAP,
                             pattern=[[0, 1]], channel_multiplier=1).then_inc(tables, 1)
            gp.wait_ge(tables, 14)
            gp.tensor_tensor(col_ge[:], ones[:], ones[:], ALU.mult).then_inc(scratch, 1)
            gp.wait_ge(scratch, 2)
            gp.tensor_scalar(same[:], col_ge[:], -1.0, 1.0, ALU.mult, ALU.add).then_inc(scratch, 1)
            gp.wait_ge(scratch, 3)

            def embedded_rstd(n):
                tiles = BATCHES[n // 2]
                lo, hi = tiles[0], tiles[-1] + 1
                gp.wait_ge(mo_done, [4, 8, 13, 18][n])
                gp.tensor_scalar(rstd[:, lo:hi], moments[:, lo:hi, 1], EPS, None, ALU.add).then_inc(var_done, 1)
                gp.wait_ge(var_done, n + 1)
                gp.tensor_tensor(rstd[:, lo:hi], rstd[:, lo:hi], minus_half[:, lo:hi], ALU.pow).then_inc(rstd_done, 1)

            embedded_rstd(0)
            gp.affine_select(out=before[:], in_=same[:], compare_op=ALU.is_gt, fill=0.0, base=0,
                             pattern=[[0, NT], [1, P]], channel_multiplier=-1).then_inc(tables, 1)
            gp.tensor_tensor(slot_of_row[:], slot_of_row[:], second_row[:], ALU.add).then_inc(tables, 1)
            for t in range(NT):
                scale, off = (64.0, 0.0) if t % 2 else (-64.0, 64.0)
                gp.tensor_scalar(parity[:, t:t + 1], parity[:, t:t + 1], scale, off, ALU.mult, ALU.add).then_inc(tables, 1)

            for n in range(1, 4):
                embedded_rstd(n)
                if n == 1:
                    for b in range(2 * QI):
                        gp.tensor_copy(v_diag[:, b, :, :, HD], own_head[:, None, :].to_broadcast([H3 * T, G3, H3])).then_inc(vones, 1)
            def late_rstd(i):
                gp.wait_ge(mo_done, 2 * NT + i + 1)
                gp.tensor_scalar(rstd[:, i:i + 1], moments[:, i, 1:2], EPS, None, ALU.add).then_inc(var_done, 1)
                gp.wait_ge(var_done, 4 + i + 1)
                gp.tensor_tensor(rstd[:, i:i + 1], rstd[:, i:i + 1], minus_half[:, i:i + 1], ALU.pow).then_inc(rstd_done, 1)

            def add_output_bias(n):
                lo, hi = BATCHES[n][0], BATCHES[n][-1] + 1
                gp.wait_ge(wo_in, 48)
                gp.wait_ge(norm_done, (8, 18)[n])
                gp.tensor_tensor(h[:, lo:hi, :], h[:, lo:hi, :], bout_bc[:, None, :].to_broadcast([P, hi - lo, D]), ALU.add).then_inc(gain_done, 1)

            for q in range(NQ):
                if q >= 2:
                    gp.wait_ge(sc_made, QP * (q - 1))
                for g in range(HG):
                    n = q * HG + g
                    gp.wait_ge(k_out, n + 1)
                    gp.tensor_tensor(k_diag[:, q % 2, g, 0:KP, :], k_tmp[:, n % 3, None, :].to_broadcast([DH, KP, CHUNK]),
                                     head_rows[:, 0:KP, None].to_broadcast([DH, KP, CHUNK]), ALU.mult).then_inc(k_ready, 1)
                if q >= 2:
                    gp.wait_ge(o_made, QP * (q - 1))
                gp.wait_ge(v_loaded[q % 2], 16 * H3 * (q // 2 + 1))
                for b in range(QI):
                    if q == NQ - 1 and b == QI // 2:
                        late_rstd(0)
                    ins = gp.tensor_tensor(v_diag[:, q % 2 * QI + b, :, :, 0:HD],
                                           v_rep[:, b, :].rearrange("p (g h d) -> p g h d", g=G3, h=H3),
                                           own_head[:, None, :, None].to_broadcast([H3 * T, G3, H3, HD]), ALU.mult)
                ins.then_inc(v_ready, 1)
                if q in (1, 2):
                    add_output_bias(q - 1)

            def split_up(e):
                s = e % 2
                gp.wait_ge(whi_done, 2 * e + 1)
                gp.tensor_tensor(wi_lo[:, s, :, :], wi_raw[:, s, :, :], wi_hi[:, s, :, :].bitcast(F32), ALU.subtract).then_inc(wlo_done, 1)

            def split_down(e):
                s = e % 2
                gp.wait_ge(whi_done, 2 * e + 2)
                gp.tensor_tensor(wo_lo[:, s, :, :], wo_raw[:, s, :, 0:P], wo_hi[:, s, :, 0:P].bitcast(F32), ALU.subtract)
                gp.tensor_tensor(wo_hi[:, s, :, D:2 * P], wo_raw[:, s, :, P:D], wo_hi[:, s, :, P:D].bitcast(F32), ALU.subtract).then_inc(wlo_done, 1)

            for i in range(1, NT):
                late_rstd(i)
                if i == 1:
                    split_up(0)
                if i == 2:
                    split_down(0)
            for r in range(3):
                gp.wait_ge(ahi_done, r + 1)
                part = slice(3 * r, 3 * r + 3)
                gp.tensor_tensor(a_split[:, part, D:2 * P], a[:, part, P:D], a_split[:, part, P:D].bitcast(F32), ALU.subtract)
                gp.tensor_tensor(a_split[:, part, 2 * P:3 * P], a[:, part, 0:P], a_split[:, part, 0:P].bitcast(F32), ALU.subtract).then_inc(alo_done, 1)
            gp.wait_ge(route, R_SLOT)
            gp.tensor_copy(slot_bf[:], slot[:]).then_inc(slotbf_done, 1)
            split_up(1)
            gp.wait_ge(ein_act, by_act(GROUPS - 1))
            gp.tensor_tensor(gate_rows[:], gate_rows[:], sum_halves[:, :, None].to_broadcast([2 * NE, NE, SLOTS]), ALU.mult).then_inc(own_gates, 1)
            for e in range(1, NE):
                split_down(e)
                if e + 1 < NE:
                    split_up(e + 1)
            for n, i in enumerate(SHARED):
                gp.wait_ge(yt_out, n + 1)
                gp.tensor_tensor(a[:, i, :], a[:, i, :], h[:, i, :], ALU.add).then_inc(fin_shared, 1)

        @block.scalar
        def _(act):
            act.dma_start(g1_sb[:], ln1_g.rearrange("(f n c) -> n f c", f=2, c=C_IN)).then_inc(aff_in, 16)
            act.dma_start(b1_sb[:], ln1_b.rearrange("(f n c) -> n f c", f=2, c=C_IN)).then_inc(aff_in, 16)
            def patch_norm_act(t):
                act.wait_ge(pshift_done, 2 * t + 2)
                if t:
                    act.wait_ge(pt_made, 2 * KJ * t)
                for w in range(SIDE // 2, SIDE):
                    act.activation(xn[:, w, :].rearrange("p (r e) -> p r e", e=PATCH), xin[:, t, :, w, :], ACT.Identity,
                                   bias=pshift[:, t, w:w + 1], scale=prstd[:, t, w:w + 1]).then_inc(pnorm_act, 1)

            def patches_out(t):
                for u in [u for u in act_units if u // (2 * KJ) == t]:
                    src, dst, gain, bias = patch_unit(u)
                    act.wait_ge(pt_made, u + 1)
                    act.activation(dst, src, ACT.Identity, bias=bias, scale=gain).then_inc(pt_act, 1)

            act.wait_ge(consts, 8)
            act.activation(act_warm[:], minus_half[:, 0:1], ACT.Identity)
            act.wait_ge(aff_in, 32)
            patch_norm_act(0)
            patches_out(0)
            patch_norm_act(1)
            patches_out(1)
            def transposed_out(i):
                act.wait_ge(aT_made, i + 1)
                act.activation(aT[:, :, i * P:(i + 1) * P], bank[6 + i % 2][0:DH, 0:2 * P].rearrange("p (k n) -> p k n", k=2),
                               ACT.Copy).then_inc(aT_done, 1)
            for i in BATCHES[0]:
                transposed_out(i)
            act.wait_ge(bqk_in, 32)
            act.wait_ge(scratch, 3)
            act.wait_ge(tables, TABLES)

            def key_out(n):
                act.wait_ge(qk_made, 2 * n + 2)
                if n >= 3:
                    act.wait_ge(k_ready, n - 2)
                act.activation(k_tmp[:, n % 3, :], bank[7][0:DH, 0:CHUNK], ACT.Identity,
                               bias=bqk_sb[:, 1, n % HG:n % HG + 1]).then_inc(k_out, 1)
                q = n // HG
                if n == 0:
                    act.wait_ge(masks, 8)
                if q >= 2:
                    act.wait_ge(sc_made, QP * (q - 1))
                act.wait_ge(k_out, n + 1)
                for hh in range(KP, H6):
                    ins = act.activation(k_diag[:, q % 2, n % HG, hh, :], k_tmp[:, n % 3, :], ACT.Copy, scale=head_rows[:, hh:hh + 1])
                ins.then_inc(k_ready_act, 1)

            def round_up_weights(e):
                s = e % 2
                act.wait_ge(wi_in[s], 16 * 4 * (e // 2 + 1))
                if e >= 2:
                    act.wait_ge(up_made, FM * (e - 1))
                act.activation(wi_hi[:, s, :, :], wi_raw[:, s, :, :], ACT.Copy).then_inc(whi_done, 1)

            def round_down_weights(e):
                s = e % 2
                if e >= 2:
                    act.wait_ge(down_made, e - 1)
                act.activation(wo_hi[:, s, :, 0:D], wo_raw[:, s, :, :], ACT.Copy).then_inc(whi_done, 1)

            def late_transposed(i):
                act.wait_ge(aT_made, NT + i + 1)
                act.activation(aT[:, :, i * P:(i + 1) * P], norm_bank(i)[0:DH, 0:2 * P].rearrange("p (k n) -> p k n", k=2), ACT.Copy).then_inc(aT_done, 1)

            def output_out(p):
                act.wait_ge(oT_made, p + 1)
                src = bank[5][0:DH, 0:256].rearrange("p (k b q) -> p k b q", k=2, b=2)[:, :, :, 0:T]
                act.activation(oT[0:DH, :, p * 2 * T:(p + 1) * 2 * T].rearrange("p k (b q) -> p k b q", b=2), src,
                               ACT.Copy).then_inc(oT_done, 1)

            for n in range(HG):
                key_out(n)
            for i in BATCHES[1]:
                transposed_out(i)
            for step in range(PAIRS + 2):
                p = step - 1
                if 0 <= p < PAIRS:
                    act.wait_ge(sm_shift, p + 1)
                    if p >= 2:
                        act.wait_ge(pT_made, p - 1)
                    act.activation(probs[:, p % 2, :, :], sm[:, p % 2, :, :], ACT.Exp, scale=HD ** -0.5).then_inc(p_done, 1)
                p = step - 2
                if 0 <= p < PAIRS:
                    act.wait_ge(pT_made, p + 1)
                    if p >= 2:
                        act.wait_ge(o_made, p - 1)
                    act.activation(probsT[:, p % 2, :, :], bank[2 + p % 2][0:H3 * T, 0:G3 * QROWS].rearrange("p (g q) -> p g q", g=G3),
                                   ACT.Copy).then_inc(pT_done, 1)
                if step >= 4:
                    output_out(step - 4)
                if step % QP < HG and step // QP + 1 < NQ:
                    key_out((step // QP + 1) * HG + step % QP)
                for i in [*transposed_early(step), *transposed_late(step)]:
                    late_transposed(i)
                if step == LATE + 1:
                    round_up_weights(0)
                if step == LATE + 2:
                    round_down_weights(0)
            output_out(PAIRS - 2)
            output_out(PAIRS - 1)
            for i in range(NT - 3, NT):
                late_transposed(i)
            for r in range(3):
                act.wait_ge(norm_done, 2 * NT + 3 * r + 3)
                act.activation(a_split[:, 3 * r:3 * r + 3, 0:D], a[:, 3 * r:3 * r + 3, :], ACT.Copy).then_inc(ahi_done, 1)
            act.wait_ge(route, R_LSH)
            act.activation(ex[:], lsh[:], ACT.Exp).then_inc(ex_done, 1)
            round_up_weights(1)
            for g in range(GROUPS):
                for k, dst in ((0, ein_hi), (1, ein_lo), (2, ein_tail), (3, gate_rows)):
                    if k == 2 and g not in TAILS_BY_ACT:
                        continue
                    act.wait_ge(disp_made, 4 * g + k + 1)
                    rows = 2 * NE if k == 3 else P
                    act.activation(dst[:, :, g * CAP:(g + 1) * CAP], bank[4 * (g % 2) + k][0:rows, 0:NE * CAP].rearrange("p (e c) -> p e c", e=NE),
                                   ACT.Copy).then_inc(ein_act, 1)

            def eo_high(e):
                for r in range(2):
                    act.wait_ge(eo_made, 2 * e + r + 1)
                    if e >= 1:
                        act.wait_ge(y_made, 2 * GP * e)
                    if e == 0 and r == 0:
                        act.wait_ge(gate_done, 1)
                    for q in (2 * r, 2 * r + 1):
                        act.activation(eo_split[:, q, 0:D], bank[4 + r][0:PS, q % 2 * D:(q % 2 + 1) * D], ACT.Copy,
                                       scale=gate_slot[:, q, e:e + 1]).then_inc(eohi_done, 1)

            for e in range(NE):
                for m in range(FM):
                    act.wait_ge(up_made, FM * e + m + 1)
                    if e >= 1:
                        act.wait_ge(down_made, e)
                    act.activation(hid_hi[:, m, :], bank[m % 4][:, 0:SLOTS], ACT.Relu).then_inc(hidhi_done, 1)
                    if m == 1 and e >= 1:
                        eo_high(e - 1)
                if e + 1 < NE:
                    round_down_weights(e + 1)
                if e + 2 < NE:
                    round_up_weights(e + 2)
                act.wait_ge(down_made, e + 1)
                if e >= 1:
                    act.wait_ge(eo_made, 2 * e)
                for k in range(2):
                    act.activation(eoT[:, k, :], bank[2 + k][:, 0:SLOTS], ACT.Copy).then_inc(eoT_done, 1)
            eo_high(NE - 1)
            for i in SHARED:
                act.wait_ge(yt_made, i + 1)
                act.activation(a[:, i, :], bank[LAST_BANKS[i % 4]][:, 0:D], ACT.Copy).then_inc(yt_out, 1)

        @block.tensor
        def _(pe):
            pe.wait_ge(consts, 12)
            pe.wait_ge(bank_set, 3)

            def keep_clock(b, times, operand=prev_tile[:, 0:4, :], n=512):
                for _ in range(times):
                    pe.matmul(bank[b][:, 0:n], identity_bf[:], operand, start=True, stop=True)

            pe.wait_ge(x_in[0][C_IN - 1], 16)
            keep_clock(5, WARM_FIRST, identity_bf[:], P)

            def embed(i):
                for j in range(KJ):
                    mm = pe.matmul(bank[(4 + i) % 8][:, 0:D], pT[:, j, i * P:(i + 1) * P], wl_sb[:, j % 2, j // 2, :],
                                   start=(j == 0), stop=(j == KJ - 1))
                mm.then_inc(emb_made, 1)

            for t in range(2):
                for v in range(2 * KJ):
                    u = 2 * KJ * t + v
                    j, w = v % KJ, v // KJ
                    if j == 0:
                        pe.wait_ge((pnorm_dve, pnorm_act)[w], SIDE // 2 * (t + 1))
                    if u >= 4:
                        wait_unit_out(pe, u - 4)
                    for k in range(3):
                        src = xn[:, 3 * w + k, j * P:(j + 1) * P]
                        mm = pe.transpose(bank[u % 4][:, k * ROWS:(k + 1) * ROWS], src, identity[0:ROWS, 0:ROWS])
                    mm.then_inc(pt_made, 1)
                for u in (2 * KJ * (t + 1) - 2, 2 * KJ * (t + 1) - 1):
                    wait_unit_out(pe, u)
                pe.wait_ge(wl_in, 16)
                for i in BATCHES[t]:
                    if i >= 8:
                        pe.wait_ge(emb_out, i - 7)
                    embed(i)

            def transpose_norm(i):
                pe.wait_ge(norm_done, [*range(4 + 1, 8 + 1), *range(13 + 1, 18 + 1)][i])
                if i >= 2:
                    pe.wait_ge(aT_done, i - 1)
                if i == 4:
                    pe.wait_ge(q_out, HG)
                    pe.wait_ge(k_out, HG)
                for k in range(2):
                    mm = pe.transpose(bank[6 + i % 2][0:DH, k * P:(k + 1) * P], a[:, i, k * DH:(k + 1) * DH], identity[:])
                mm.then_inc(aT_made, 1)

            def values(i):
                pe.wait_ge(aT_done, i + 1)
                if i == 0:
                    pe.wait_ge(wq_in, 16)
                if i >= 2:
                    pe.wait_ge(v_out, i - 1)
                for k in range(2):
                    mm = pe.matmul(bank[4 + i % 2][:, 0:D], aT[:, k, i * P:(i + 1) * P], wqkv_sb[:, k, 2 * D:3 * D], start=(k == 0), stop=(k == 1))
                mm.then_inc(v_made, 1)

            def project(n):
                q, g = n // HG, n % HG
                for i in range(2):
                    if n == 0:
                        pe.wait_ge(aT_done, len(BATCHES[0]))
                    else:
                        pe.wait_ge(k_out if i else q_out, n)
                    if n == HG:
                        pe.wait_ge(aT_done, NT)
                    for k in range(2):
                        mm = pe.matmul(bank[6 + i][0:DH, 0:CHUNK], wqkv_sb[:, k, i * D + g * DH:i * D + (g + 1) * DH],
                                       aT[:, k, q * CHUNK:(q + 1) * CHUNK], start=(k == 0), stop=(k == 1))
                    mm.then_inc(qk_made, 1)

            for i in BATCHES[0]:
                transpose_norm(i)
            pe.wait_ge(emb_out, NT)
            for i in BATCHES[0]:
                values(i)
            def late_project(i):
                if i == 0:
                    pe.wait_ge(wo_in, 48)
                    pe.wait_ge(q_out, HG * NQ)
                    pe.wait_ge(k_out, HG * NQ)
                pe.wait_ge(oT_done, min(PAIRS, -(-(i + 1) * P // (2 * T))))
                if i == NT - 1:
                    pe.wait_ge(sm_masked, last_masked[0])
                elif i:
                    pe.wait_ge(res1, i)
                for k in range(2):
                    mm = pe.matmul(projected(i), oT[0:DH, k, i * P:(i + 1) * P], wout_sb[:, k, :], start=(k == 0), stop=(k == 1))
                mm.then_inc(wout_made, 1)

            def late_transpose(i):
                pe.wait_ge(norm_done, 2 * NT + i + 1)
                if i >= NT - 2:
                    pe.wait_ge(pT_done, PAIRS)
                elif i:
                    pe.wait_ge(aT_done, NT + i)
                for k in range(2):
                    mm = pe.transpose(norm_bank(i)[0:DH, k * P:(k + 1) * P], a[:, i, k * DH:(k + 1) * DH], identity[:])
                mm.then_inc(aT_made, 1)

            def logits(i):
                pe.wait_ge(aT_done, NT + i + 1)
                for k in range(2):
                    mm = pe.matmul(bank[7][:, LG + i * NE:LG + (i + 1) * NE], aT[:, k, i * P:(i + 1) * P], wr_sb[:, k, :], start=(k == 0), stop=(k == 1))
                mm.then_inc(lg_made, 1)

            def weigh_values(p):
                pe.wait_ge(pT_done, p + 1)
                if p % QP == 0:
                    pe.wait_ge(v_ready, p // QP + 1)
                if p == 0:
                    pe.wait_ge(v_out, NT)
                    pe.wait_ge(vones, 2 * QI)
                if p >= 1:
                    pe.wait_ge(o_done, p)
                for b in range(2):
                    for g in range(G3):
                        w = H3 * (HD + 1)
                        mm = pe.matmul(bank[4][64 * b:64 * b + T, g * w:(g + 1) * w], probsT[:, p % 2, g, 64 * b:64 * b + T],
                                       v_diag[:, (2 * p + b) % (2 * QI), g, :, :], start=True, stop=True)
                mm.then_inc(o_made, 1)

            def transpose_output(p):
                pe.wait_ge(o_done, p + 1)
                if p >= 1:
                    pe.wait_ge(oT_done, p)
                for k in range(2):
                    mm = pe.transpose(bank[5][0:DH, k * P:k * P + QROWS], o_sb[:, p % 2, 6 * k:6 * k + 6, :], identity[0:QROWS, 0:QROWS])
                mm.then_inc(oT_made, 1)

            for n in range(HG):
                project(n)
            for i in BATCHES[1]:
                transpose_norm(i)
            for i in BATCHES[1]:
                values(i)
            for step in range(PAIRS + 2):
                p = step
                if p < PAIRS:
                    if p % QP == 0:
                        pe.wait_ge(q_out, HG * (p // QP + 1))
                        pe.wait_ge(k_ready, HG * (p // QP + 1))
                        pe.wait_ge(k_ready_act, HG * (p // QP + 1))
                    if p >= 2:
                        pe.wait_ge(sm_masked, p - 1)
                    for b in range(2):
                        tok = (2 * p + b) % QI * T
                        s = p // QP % 2
                        for g in range(HG):
                            mm = pe.matmul(bank[p % 2][64 * b:64 * b + T, g * H6 * T:(g + 1) * H6 * T], qT[:, s, g, tok:tok + T],
                                           k_diag[:, s, g, :, tok:tok + T], start=True, stop=True)
                    mm.then_inc(sc_made, 1)
                if step % QP < HG and step // QP + 1 < NQ:
                    project((step // QP + 1) * HG + step % QP)
                for i in transposed_early(step):
                    late_transpose(i)
                p = step - 2
                if 0 <= p < PAIRS:
                    pe.wait_ge(p_done, p + 1)
                    if p >= 2:
                        pe.wait_ge(pT_done, p - 1)
                    for g in range(G3):
                        mm = pe.transpose(bank[2 + p % 2][0:H3 * T, g * QROWS:(g + 1) * QROWS], probs[:, p % 2, H3 * g:H3 * g + H3, :],
                                          identity[0:QROWS, 0:QROWS])
                    mm.then_inc(pT_made, 1)
                if step >= 3:
                    weigh_values(step - 3)
                if step >= 4:
                    transpose_output(step - 4)
                if step >= LATE:
                    late_project(step - LATE)
                if step >= LATE + 2:
                    logits(step - LATE - 2)
                for i in transposed_late(step):
                    late_transpose(i)
            pe.wait_ge(tables, TABLES)
            keep_clock(1, WARM_DRAIN[0])
            weigh_values(PAIRS - 1)
            transpose_output(PAIRS - 2)
            keep_clock(1, WARM_DRAIN[1])
            late_project(NT - 2)
            transpose_output(PAIRS - 1)
            keep_clock(1, WARM_DRAIN[2])
            late_project(NT - 1)
            logits(NT - 4)
            late_transpose(NT - 3)
            late_transpose(NT - 2)
            logits(NT - 3)
            late_transpose(NT - 1)
            logits(NT - 2)
            logits(NT - 1)
            pe.wait_ge(res1, NT)
            keep_clock(4, WARM_ROUTE[0])
            pe.wait_ge(route, R_PICK1)

            def count_tokens(bk, c0, t, terms):
                terms = [(m, pk, t + d) for m, pk, d in terms if 0 <= t + d < NT]
                for n, (m, pk, ts) in enumerate(terms):
                    mm = pe.matmul(bank[bk][:, c0 + t * NE:c0 + (t + 1) * NE], m[:, t, :], pk[:, ts, :], start=(n == 0), stop=(n == len(terms) - 1))
                return mm

            for t in range(NT):
                count_tokens(6, 0, t, [(before, pick1, 0), (prev_tile, pick1, -1)])
            for t in range(NT):
                mm = count_tokens(6, 128, t, [(same, pick1, 0), (prev_tile, pick1, -1), (next_tile, pick1, 1)])
            mm.then_inc(prio_made, 1)
            keep_clock(4, WARM_ROUTE[1])
            pe.wait_ge(route, R_PICK2)
            pe.wait_ge(oT_done, PAIRS)
            for t in range(NT):
                mm = count_tokens(5, 0, t, [(before, pick2, 0), (prev_tile, pick2, -1)])
            mm.then_inc(prio_made, 1)
            keep_clock(4, WARM_ROUTE[2])
            for g in range(GROUPS):
                pe.wait_ge(d01_done, 2 * g + 2)
                if g == 0:
                    pe.wait_ge(alo_done, 3)
                    pe.wait_ge(ahi_done, 3)
                if g >= 2:
                    pe.wait_ge(ein_act, by_act(g - 2))
                    pe.wait_ge(ein_dve, 4 * (g - 1) - by_act(g - 2))
                for k, (w, c0, m) in enumerate(((a_split, 0, P), (a_split, 2 * P, P), (a_split, P, P), (gate_split, 0, 2 * NE))):
                    if g == 0 and k == 3:
                        pe.wait_ge(gates, 5)
                    for t in (g, g + 1):
                        mm = pe.matmul(bank[4 * (g % 2) + k][0:m, 0:NE * CAP], w[:, t, c0:c0 + m], d01[:, (2 * g + t - g) % 4, :, :],
                                       start=(t == g), stop=(t == g + 1))
                    mm.then_inc(disp_made, 1)

            def transpose_slots():
                pe.wait_ge(slotbf_done, 1)
                pe.wait_ge(ein_act, by_act(GROUPS - 1))
                for t in range(NT):
                    dst = bank_bf[7 - t // 8]
                    mm = pe.transpose(dst[0:NE, (t % 8) * P:(t % 8 + 1) * P], slot_bf[:, t, :], identity_bf[:])
                mm.then_inc(slotT_made, 1)

            def gates_to_slots():
                pe.wait_ge(line_done, GP)
                for q in range(GP):
                    mm = pe.matmul(bank[6][0:PS, NE * q:NE * (q + 1)], gate_line[:, q * PS:(q + 1) * PS], sum_halves[:], start=True, stop=True)
                mm.then_inc(gate_made, 1)

            def transpose_out(e):
                pe.wait_ge(eoT_done, 2 * e + 2)
                for r in range(2):
                    pe.wait_ge(comb_done, GP * (e + 1))
                    for gg in range(2):
                        rows = slice((2 * r + gg) * PS, (2 * r + gg + 1) * PS)
                        pe.transpose(bank[4 + r][0:PS, gg * D:gg * D + P], eoT[:, 0, rows], identity[:])
                        mm = pe.matmul(bank[4 + r][0:PS, gg * D + P:(gg + 1) * D], eoT[:, 1, rows], fold[:], start=True, stop=True)
                    mm.then_inc(eo_made, 1)

            def slots_bc(e, q):
                n = GP * e + q
                if e == 0 and q == 0:
                    pe.wait_ge(slotT_done, 2)
                if q >= 2:
                    pe.wait_ge(comb_done, n - 1)
                elif e >= 1:
                    pe.wait_ge(eolo_done, GP * e)
                    pe.wait_ge(eohi_done, GP * e)
                pe.matmul(bank[4 + q % 2][0:PS, 0:PTOK], pick[:, e, :], slotT[:, q * PTOK:(q + 1) * PTOK], start=True, stop=True).then_inc(bc_made, 1)

            def combine(e, q):
                pe.wait_ge(eohi_done, GP * e + q + 1)
                pe.wait_ge(eolo_done, GP * e + q + 1)
                pe.wait_ge(comb_done, GP * e + q + 1)
                for k in range(2):
                    n = 2 * (GP * e + q) + k
                    if e == NE - 1:
                        if q == 0:
                            pe.wait_ge(y_done, n - 1)
                        elif q == 1:
                            pe.wait_ge(hidlo_done, FM * NE)
                        elif q == 2:
                            pe.wait_ge(eoT_done, 2 * NE)
                        else:
                            pe.wait_ge(y_done, 2 * GP * e + k + 1)
                    elif n >= 2:
                        pe.wait_ge(y_done, n - 1)
                    elif k == 0:
                        pe.wait_ge(gate_done, 1)
                    parts = ((P, 2 * P),) if k else ((0, P), (2 * P, 3 * P))
                    for j, (c0, c1) in enumerate(parts):
                        mm = pe.matmul(y_bank(e, q, k)[:, 0:PTOK], eo_split[:, q, c0:c1], comb[:, e % 2, q, :], start=(j == 0), stop=(j == len(parts) - 1))
                    mm.then_inc(y_made, 1)

            def tail_columns(s, m):
                return pe.matmul(bank[3][:, 0:SLOTS], wo_hi[:, s, m, P:2 * P], hid_hi[:, m, :], start=(m == 0), stop=(m == FM - 1))

            pe.wait_ge(ein_act, by_act(GROUPS - 1) - 1)
            pe.wait_ge(ein_dve, 4 * GROUPS - by_act(GROUPS - 1))
            for e in range(NE):
                s = e % 2
                pe.wait_ge(wlo_done, 2 * e + 2)
                for m in range(FM):
                    n = FM * e + m
                    if e and m < 2:
                        pe.wait_ge(hidlo_done, n - 1)
                    elif e and m < 4:
                        pe.wait_ge(eoT_done, 2 * (e - 1) + m - 1)
                    elif m >= 4:
                        pe.wait_ge(hidlo_done, n - 3)
                    for i, (w, k, r) in enumerate(((wi_hi, 0, ein_hi), (wi_lo, 0, ein_hi), (wi_hi, 0, ein_lo), (wi_hi, 1, ein_tail), (wi_lo, 1, ein_tail))):
                        mm = pe.matmul(bank[m % 4][:, 0:SLOTS], w[:, s, k, m * P:(m + 1) * P], r[:, e, :], start=(i == 0), stop=(i == 4))
                    mm.then_inc(up_made, 1)
                    if e == 0 and m == 1:
                        transpose_slots()
                    if e == 1 and m == 1:
                        gates_to_slots()
                    if e and m == 1:
                        transpose_out(e - 1)
                    if e and m == 4:
                        combine(e - 1, 0)
                pe.wait_ge(hidlo_done, FM * e + 4)
                for m in range(FM):
                    pe.wait_ge(hidhi_done, FM * e + m + 1)
                    pe.wait_ge(hidlo_done, FM * e + m + 1)
                    if m == 0:
                        tail_columns(s, m)
                    for i, (w, r) in enumerate(((wo_hi, hid_hi), (wo_lo, hid_hi), (wo_hi, hid_lo))):
                        pe.matmul(bank[2][:, 0:SLOTS], w[:, s, m, 0:P], r[:, m, :], start=(m == 0 and i == 0), stop=(m == FM - 1 and i == 2))
                    mm = pe.matmul(bank[3][0:DT, 0:SLOTS], wo_hi[:, s, m, P:D], hid_lo[:, m, :], start=False, stop=False)
                    if m:
                        mm = tail_columns(s, m)
                    if e and m % 2:
                        combine(e - 1, 1 + m // 2)
                    if m < GP:
                        slots_bc(e, m)
                mm.then_inc(down_made, 1)
            keep_clock(1, WARM_LAST[0])
            transpose_out(NE - 1)
            keep_clock(1, WARM_LAST[1])

            def back_to_tokens(i):
                pe.wait_ge(y_done, 2 * GP * (NE - 1) + 2 * -(-(i + 1) * P // PTOK))
                if i >= 4:
                    wait_last_bank(pe, i - 4)
                elif i < 2:
                    pe.wait_ge(eolo_done, GP * NE)
                b = LAST_BANKS[i % 4]
                pe.transpose(bank[b][:, 0:P], y_acc[:, 0, i * P:(i + 1) * P], identity[:])
                mm = pe.matmul(bank[b][:, P:D], y_acc[:, 1, i * P:(i + 1) * P], fold[:], start=True, stop=True)
                mm.then_inc(yt_made, 1)

            for q in range(3):
                combine(NE - 1, q)
            for i in range(2):
                back_to_tokens(i)
            combine(NE - 1, 3)
            for i in range(2, NT):
                back_to_tokens(i)

        @block.vector
        def _(dve):
            def normalize(i):
                dve.tensor_scalar(a[:, i, :], h[:, i, :], moments[:, i, 0:1], rstd[:, i:i + 1], ALU.subtract, ALU.mult).then_inc(norm_done, 1)

            def statistics(tiles, n0):
                for n, i in enumerate(tiles):
                    dve.bn_stats(stats[:, i, :], h[:, i, :]).then_inc(st_done, 1)
                for n, i in enumerate(tiles):
                    dve.wait_ge(st_done, n0 + n + 1)
                    dve.bn_aggr(moments[:, i, :], stats[:, i, :]).then_inc(mo_done, 1)

            def channel_stats(t, c, ws):
                for w in ws:
                    if w == ws[0]:
                        dve.wait_ge(x_in[t][c], 16)
                    dve.bn_stats(pstats[:, t, w, c, :], xin[:, t, c * PATCH:(c + 1) * PATCH, w, :]).then_inc(pstat_done, 1)

            def patch_moments(t, ws):
                for w in ws:
                    dve.wait_ge(pstat_done, SIDE * (C_IN * t + 2) + w + 1)
                    dve.bn_aggr(pmom[:, t, w, :], pstats[:, t, w, :, :]).then_inc(pmom_done, 1)

            def patch_norm(t):
                dve.wait_ge(prstd_done, 4 * t + 2)
                if t:
                    dve.wait_ge(pt_made, KJ * (2 * t - 1))
                dve.wait_ge(pmom_done, SIDE * t + SIDE // 2)
                for w in range(SIDE // 2):
                    dve.tensor_scalar(xn[:, w, :].rearrange("p (r e) -> p r e", e=PATCH), xin[:, t, :, w, :], pmom[:, t, w, 0:1], prstd[:, t, w:w + 1], ALU.subtract, ALU.mult).then_inc(pnorm_dve, 1)

            def add_bias(i):
                dve.wait_ge(emb_made, i + 1)
                dve.tensor_tensor(h[:, i, :], bank[(4 + i) % 8][:, 0:D], bl_bc[:], ALU.add).then_inc(emb_out, 1)

            def embedded(t, between):
                tiles = BATCHES[t]
                done, w = 2 * tiles[0], len(tiles)
                dve.wait_ge(emb_out, tiles[-1] + 1)
                statistics(tiles, done)
                dve.wait_ge(mo_done, done + w)
                for n, i in enumerate(tiles):
                    dve.scalar_tensor_tensor(h[:, i, :], h[:, i, :], moments[:, i, 0:1], g2_bc[:], ALU.subtract, ALU.mult).then_inc(centred, 1)
                    between(0, n)
                dve.wait_ge(rstd_done, 2 * t + 1)
                for n, i in enumerate(tiles):
                    dve.wait_ge(centred, i + 1)
                    dve.scalar_tensor_tensor(h[:, i, :], h[:, i, :], rstd[:, i:i + 1], b2_bc[:], ALU.mult, ALU.add).then_inc(norm_done, 1)
                    between(1, n)
                dve.wait_ge(norm_done, done + w)
                statistics(tiles, done + w)
                for n in range(w):
                    between(2, n)
                dve.wait_ge(rstd_done, 2 * t + 2)
                for n, i in enumerate(tiles):
                    normalize(i)
                    between(3, n)

            def value_out(i):
                dve.wait_ge(v_made, i + 1)
                if i >= 3:
                    dve.wait_ge(v_stored[i % 3], 16 * (i // 3))
                dve.tensor_tensor(v_sb[:, i % 3, :], bank[4 + i % 2][:, 0:D], bv_bc[:], ALU.add).then_inc(v_out, 1)

            def query_out(n):
                q, g = n // HG, n % HG
                if n == 0:
                    dve.wait_ge(bqk_in, 32)
                dve.wait_ge(qk_made, 2 * n + 1)
                if q >= 2:
                    dve.wait_ge(sc_made, QP * (q - 1))
                dve.tensor_scalar(qT[:, q % 2, g, :], bank[6][0:DH, 0:CHUNK], bqk_sb[:, 0, g:g + 1], None, ALU.add).then_inc(q_out, 1)

            def patch_out(u):
                src, dst, gain, bias = patch_unit(u)
                dve.wait_ge(pt_made, u + 1)
                dve.tensor_scalar(dst, src, gain, bias, ALU.mult, ALU.add).then_inc(pt_dve, 1)

            for i in (0, 1, 4):
                dve.memset(bank[i][:], 1.0).then_inc(bank_set, 1)
            left, right = range(0, SIDE // 2), range(SIDE // 2, SIDE)
            for c in range(C_IN):
                for ws in (left, right):
                    channel_stats(0, c, ws)
                    if c == C_IN - 1:
                        patch_moments(0, ws)
            patch_norm(0)
            dve.wait_ge(aff_in, 32)
            todo = [(c, w) for c in range(C_IN) for w in range(SIDE)]
            for u in [u for u in dve_units if u < 2 * KJ]:
                patch_out(u)
                for c, w in [todo.pop(0) for _ in range(STATS_BETWEEN)]:
                    channel_stats(1, c, [w])
            for c, w in todo:
                channel_stats(1, c, [w])
                if c == C_IN - 1:
                    patch_moments(1, [w])
            patch_norm(1)
            for u in [u for u in dve_units if u >= 2 * KJ]:
                patch_out(u)
            dve.wait_ge(bias_in, 64)
            for i in BATCHES[0]:
                add_bias(i)
            embedded(0, lambda stage, n: add_bias(4 + n) if stage == 2 else None)
            add_bias(NT - 1)

            def first_values_and_queries(stage, n):
                todo = {(0, 2): (value_out, 0), (0, 4): (value_out, 1), (1, 2): (value_out, 2), (1, 4): (value_out, 3),
                        (2, 0): (query_out, 0), (3, 1): (query_out, 1)}
                if (stage, n) in todo:
                    f, k = todo[stage, n]
                    f(k)

            embedded(1, first_values_and_queries)
            for i in BATCHES[1]:
                value_out(i)
            def late_residual(i):
                dve.wait_ge(wout_made, i + 1)
                dve.wait_ge(gain_done, 1 if i in BATCHES[0] else 2)
                dve.tensor_tensor(h[:, i, :], projected(i), h[:, i, :], ALU.add).then_inc(res1, 1)
                dve.wait_ge(res1, i + 1)
                statistics([i], 2 * NT + i)

            def late_normalize(i):
                dve.wait_ge(rstd_done, 4 + i + 1)
                normalize(i)

            def divide(p):
                s = p % 2
                o = bank[4][0:QROWS, 0:HEADS * (HD + 1)].rearrange("p (h d) -> p h d", h=HEADS)
                dve.wait_ge(o_made, p + 1)
                dve.reciprocal(rsum[:, s, :], o[:, :, HD]).then_inc(rs_done, 1)
                dve.wait_ge(rs_done, p + 1)
                if p >= 2:
                    dve.wait_ge(oT_made, p - 1)
                dve.tensor_tensor(o_sb[:, s, :, :], o[:, :, 0:HD], rsum[:, s, :, None].to_broadcast([QROWS, HEADS, HD]), ALU.mult).then_inc(o_done, 1)

            dve.wait_ge(masks, 8)
            for step in range(PAIRS + 2):
                p = step
                if p < PAIRS:
                    s = p % 2
                    dve.wait_ge(sc_made, p + 1)
                    if p >= 2:
                        dve.wait_ge(p_done, p - 1)
                    dve.tensor_tensor(sm[:, s, :, :], bank[s][0:QROWS, 0:HEADS * T].rearrange("p (h k) -> p h k", h=HEADS),
                                      causal[:, None, :].to_broadcast([QROWS, HEADS, T]), ALU.add).then_inc(sm_masked, 1)
                    dve.wait_ge(sm_masked, p + 1)
                    dve.tensor_reduce(smax[:, s, :], sm[:, s, :, :], AX.X, ALU.max).then_inc(sm_max, 1)
                    dve.wait_ge(sm_max, p + 1)
                    dve.tensor_tensor(sm[:, s, :, :], sm[:, s, :, :], smax[:, s, :, None].to_broadcast([QROWS, HEADS, T]), ALU.subtract).then_inc(sm_shift, 1)
                if step % QP < HG and step // QP + 1 < NQ:
                    query_out((step // QP + 1) * HG + step % QP)
                if step >= 3:
                    divide(step - 3)
                if step >= LATE + 1:
                    late_normalize(step - LATE - 1)
                if step >= LATE:
                    late_residual(step - LATE)
            divide(PAIRS - 1)
            late_normalize(NT - 3)
            late_residual(NT - 2)
            late_residual(NT - 1)
            late_normalize(NT - 2)
            late_normalize(NT - 1)
            count = [0]

            def link(ins):
                count[0] += 1
                ins.then_inc(route, 1)
                dve.wait_ge(route, count[0])

            def bc(ap):
                return ap[:, :, None].to_broadcast([P, NT, NE])

            exp_bc = expert_no[:, None, :].to_broadcast([P, NT, NE])
            dve.wait_ge(lg_made, NT)
            dve.wait_ge(tables, TABLES)
            logit = bank[7][:, LG:LG + NT * NE].rearrange("p (t e) -> p t e", t=NT)
            link(dve.tensor_reduce(top[:, 0, :], logit, AX.X, ALU.max))
            link(dve.tensor_tensor(lsh[:], logit, bc(top[:, 0, :]), ALU.subtract))
            assert count[0] == R_LSH
            link(dve.scalar_tensor_tensor(eq[:], lsh[:], 0.0, exp_bc, ALU.is_equal, ALU.mult))
            link(dve.tensor_reduce(first[:, 0, :], eq[:], AX.X, ALU.min))
            link(dve.tensor_tensor(pick1[:], exp_bc, bc(first[:, 0, :]), ALU.is_equal))
            assert count[0] == R_PICK1
            link(dve.scalar_tensor_tensor(lg2[:], pick1[:], -3e38, lsh[:], ALU.mult, ALU.add))
            link(dve.tensor_reduce(top[:, 1, :], lg2[:], AX.X, ALU.max))
            link(dve.tensor_tensor(lg2[:], lg2[:], bc(top[:, 1, :]), ALU.subtract))
            link(dve.scalar_tensor_tensor(eq[:], lg2[:], 0.0, exp_bc, ALU.is_equal, ALU.mult))
            link(dve.tensor_reduce(first[:, 1, :], eq[:], AX.X, ALU.min))
            link(dve.tensor_tensor(pick2[:], exp_bc, bc(first[:, 1, :]), ALU.is_equal))
            assert count[0] == R_PICK2
            def counted(bk, c0):
                return bank[bk][:, c0:c0 + NT * NE].rearrange("p (t e) -> p t e", t=NT)

            dve.wait_ge(prio_made, 1)
            link(dve.scalar_tensor_tensor(s1[:], counted(6, 0), 1.0, pick1[:], ALU.add, ALU.mult))
            link(dve.tensor_copy(s2[:], counted(6, 128)))
            dve.wait_ge(prio_made, 2)
            link(dve.scalar_tensor_tensor(s2[:], counted(5, 0), 1.0, s2[:], ALU.add, ALU.add))
            link(dve.tensor_tensor(s2[:], s2[:], pick2[:], ALU.mult))
            link(dve.tensor_tensor(s1[:], s1[:], s2[:], ALU.add))
            link(dve.scalar_tensor_tensor(slot[:], s1[:], CAP + 5.0, bc(parity[:]), ALU.min, ALU.add))
            assert count[0] == R_SLOT

            def ein_last(g):
                dve.wait_ge(disp_made, 4 * g + 3)
                dve.tensor_copy(ein_tail[:, :, g * CAP:(g + 1) * CAP],
                                bank[4 * (g % 2) + 2][:, 0:NE * CAP].rearrange("p (e c) -> p e c", e=NE)).then_inc(ein_dve, 1)

            def gate_step(n):
                if n == 0:
                    dve.wait_ge(ex_done, 1)
                    dve.tensor_reduce(esum[:], ex[:], AX.X, ALU.add).then_inc(gates, 1)
                if n == 1:
                    dve.wait_ge(gates, 1)
                    dve.reciprocal(erec[:], esum[:]).then_inc(gates, 1)
                    dve.wait_ge(gates, 2)
                    dve.tensor_tensor(gate[:], ex[:], bc(erec[:]), ALU.mult).then_inc(gates, 1)
                if n == 2:
                    dve.wait_ge(gates, 3)
                    dve.tensor_copy(gate_split[:, :, 0:NE], gate[:]).then_inc(gates, 1)
                if n == 3:
                    dve.wait_ge(gates, 4)
                    dve.tensor_tensor(gate_split[:, :, NE:2 * NE], gate[:], gate_split[:, :, 0:NE].bitcast(F32), ALU.subtract).then_inc(gates, 1)

            for n in range(2 * GROUPS):
                g = n // 2
                if n >= 4:
                    dve.wait_ge(disp_made, 4 * (g - 1))
                dve.tensor_tensor(*dispatch_matrix(n), ALU.is_equal).then_inc(d01_done, 1)
                gate_step(n)
                if n >= 3 and n % 2 and g - 1 not in TAILS_BY_ACT:
                    ein_last(g - 1)
            ein_last(GROUPS - 1)

            def eo_low(e):
                for r in range(2):
                    dve.wait_ge(eohi_done, GP * e + 2 * r + 2)
                    for q in (2 * r, 2 * r + 1):
                        for src, dst in (((P, D), (D, 2 * P)), ((0, P), (2 * P, 3 * P))):
                            ins = dve.scalar_tensor_tensor(eo_split[:, q, dst[0]:dst[1]], bank[4 + r][0:PS, q % 2 * D + src[0]:q % 2 * D + src[1]],
                                                           gate_slot[:, q, e:e + 1], eo_split[:, q, src[0]:src[1]].bitcast(F32),
                                                           ALU.mult, ALU.subtract)
                        ins.then_inc(eolo_done, 1)

            def add_y(e, q):
                for k in range(2):
                    n = 2 * (GP * e + q) + k
                    dve.wait_ge(y_made, n + 1)
                    dst = y_acc[:, k, q * PTOK:(q + 1) * PTOK]
                    if e == 0:
                        dve.tensor_copy(dst, bank[6 + k][:, 0:PTOK]).then_inc(y_done, 1)
                    else:
                        dve.wait_ge(y_done, n + 1 - 2 * GP)
                        dve.tensor_tensor(dst, y_bank(e, q, k)[:, 0:PTOK], dst, ALU.add).then_inc(y_done, 1)

            def slot_rows(e, q):
                n = GP * e + q
                dve.wait_ge(bc_made, n + 1)
                if e >= 2:
                    dve.wait_ge(y_made, 2 * GP * (e - 2) + 2 * q + 2)
                dve.tensor_scalar(comb[:, e % 2, q, :], bank[4 + q % 2][0:PS, 0:PTOK], slot_of_row[:], None, ALU.is_equal).then_inc(comb_done, 1)

            def own_gates_of(q):
                dve.wait_ge(own_gates, 1)
                dve.tensor_reduce(gate_line[:, q * PS:(q + 1) * PS], gate_rows[:, :, q * PS:(q + 1) * PS].rearrange("p e s -> p s e"),
                                  AX.X, ALU.add).then_inc(line_done, 1)

            for e in range(NE):
                for m in range(FM):
                    dve.wait_ge(hidhi_done, FM * e + m + 1)
                    dve.scalar_tensor_tensor(hid_lo[:, m, :], bank[m % 4][:, 0:SLOTS], 0.0, hid_hi[:, m, :].bitcast(F32), ALU.max, ALU.subtract).then_inc(hidlo_done, 1)
                    if e == 0 and m == 1:
                        dve.wait_ge(slotT_made, 1)
                        dve.tensor_copy(slotT[:, 0:8 * P], bank_bf[7][0:NE, :]).then_inc(slotT_done, 1)
                        dve.tensor_copy(slotT[:, 8 * P:], bank_bf[6][0:NE, 0:P]).then_inc(slotT_done, 1)
                    if e == 1 and m == 1:
                        dve.wait_ge(gate_made, 1)
                        dve.tensor_copy(gate_slot[:], bank[6][0:PS, 0:NE * GP].rearrange("p (q e) -> p q e", e=NE)).then_inc(gate_done, 1)
                    if e and m == 1:
                        eo_low(e - 1)
                    if e and m == 4:
                        add_y(e - 1, 0)
                for q in range(GP):
                    if e and q % 2:
                        add_y(e - 1, 1 + q // 2)
                    slot_rows(e, q)
                    if e == 0:
                        for r in {0: (0,), 2: (1,), 3: (2, 3)}.get(q, ()):
                            own_gates_of(r)
                if e:
                    add_y(e - 1, GP - 1)
            eo_low(NE - 1)

            def finish(i):
                dve.wait_ge(yt_made, i + 1)
                dve.tensor_tensor(a[:, i, :], bank[LAST_BANKS[i % 4]][:, 0:D], h[:, i, :], ALU.add).then_inc(fin_done, 1)

            add_y(NE - 1, 0)
            add_y(NE - 1, 1)
            finish(0)
            add_y(NE - 1, 2)
            finish(2)
            add_y(NE - 1, 3)
            for i in own_tiles[2:]:
                finish(i)


_NAMES = ["x", "L0_tok_ln1_g", "L0_tok_ln1_b", "L0_tok_Wl", "L0_tok_bl", "L0_tok_ln2_g", "L0_tok_ln2_b",
          "L0_attn_W_qkv", "L0_attn_b_qkv", "L0_attn_W_out", "L0_attn_b_out", "L0_ffn_w_router", "L0_ffn_wi", "L0_ffn_wo"]


def kernel(**inputs):
    import numpy as np
    import concourse.bacc as bacc
    from concourse.bass_utils import run_bass_kernel_spmd

    nc = bacc.Bacc("TRN2", target_bir_lowering=False, num_devices=1)
    arrays, args = {}, []
    for name in _NAMES:
        arrays[name] = np.ascontiguousarray(inputs[name])
        args.append(nc.dram_tensor(name, arrays[name].shape, F32, kind="ExternalInput").ap())
    out = nc.dram_tensor("out", (N, D), F32, kind="ExternalOutput").ap()
    build(nc, *args, out)
    r = run_bass_kernel_spmd(nc, [arrays], core_ids=[0])
    return r.results[0]["out"].reshape(B, T, D)
```
